# Optimizing a Trainium2 kernel written in Bass

```python
import numpy as np
import jax
import jax.numpy as jnp

def _softmax(x, axis=-1):
    return jax.nn.softmax(x, axis=axis)

def _gelu(x):
    return jax.nn.gelu(x, approximate=True)

def _silu(x):
    return jax.nn.silu(x)

def _sigmoid(x):
    return jax.nn.sigmoid(x)

def _layernorm(x, axis=-1, eps=1e-05):
    m = jnp.mean(x, axis=axis, keepdims=True)
    v = jnp.var(x, axis=axis, keepdims=True)
    return (x - m) / jnp.sqrt(v + eps)

def _scatter_add(tgt, idx, src, axis=0):
    return tgt.at[idx].add(src)

def _segment_sum(src, seg, n):
    return jax.ops.segment_sum(src, seg, n)
kernel_name = 'mk_flamingo_gated_d1_seqx_r2_6e1307'

def setup_inputs(seed: int=0):
    np.random.seed(seed)
    _w = jnp.asarray

    def _rec_inputs():
        import jax
        import jax.numpy as jnp
        _rk = jax.random.key(seed)
        x = -7.109e-05 + 0.9999 * jax.random.normal(jax.random.fold_in(_rk, 1), (4, 1024, 2048), jnp.float32)
        _lenS = 1024 - jax.random.randint(jax.random.fold_in(_rk, 7), (4,), 0, max(1, 1024 // 4) + 1, jnp.int32)
        _lenS2 = 64 - jax.random.randint(jax.random.fold_in(_rk, 8), (4,), 0, max(1, 64 // 4) + 1, jnp.int32)
        _ctx_4096P = jax.random.normal(jax.random.fold_in(_rk, 11), (4, 16, 2048), jnp.float32)
        _ctx_4096c = jax.random.dirichlet(jax.random.fold_in(_rk, 511), 0.3 * jnp.ones((16,), jnp.float32), (4, 64))
        _ctx_4096t = jnp.einsum('bsk,bkd->bsd', _ctx_4096c, _ctx_4096P)
        _ctx_4096t = _ctx_4096t * jax.lax.rsqrt(jnp.mean(jnp.square(_ctx_4096t)) + 1e-12) * 0.953939
        ctx_4096 = -2.6191e-05 + 0.999952 * (_ctx_4096t + 0.3 * jax.random.normal(jax.random.fold_in(_rk, 611), (4, 64, 2048), jnp.float32))
        _g = jax.random.normal(jax.random.fold_in(_rk, 9001), (2, 1), jnp.float32)
        _g = jnp.sign(_g) * jnp.maximum(jnp.abs(_g), 1.0) + (_g == 0) * 1.0
        g_xattn = _g[0]
        g_ffn = _g[1]
        return (x, ctx_4096, g_xattn, g_ffn)
    x, ctx_4096, g_xattn, g_ffn = _rec_inputs()

    def _L0_xattn_setup():
        import jax, jax.numpy as jnp
        import numpy as np
        TEXT_DIM = 2048
        FEATURE_DIM = 2048

        def _xavier_uniform(key, shape):
            fan_in, fan_out = (shape[1], shape[0])
            limit = float(np.sqrt(6.0 / (fan_in + fan_out)))
            return jax.random.uniform(key, shape, jnp.float32, -limit, limit)
        key = jax.random.key(seed)
        k1, k2, k3, k4 = jax.random.split(key, 4)
        text = jax.random.normal(k1, (8, 1024, TEXT_DIM), jnp.float32)
        features = jax.random.normal(k2, (8, 288, FEATURE_DIM), jnp.float32)
        Wq = _xavier_uniform(k3, (FEATURE_DIM, TEXT_DIM))
        bq = jnp.zeros((FEATURE_DIM,), jnp.float32)
        Wk = _xavier_uniform(k4, (FEATURE_DIM, FEATURE_DIM))
        bk = jnp.zeros((FEATURE_DIM,), jnp.float32)
        return {'text': text, 'features': features, 'Wq': Wq, 'bq': bq, 'Wk': Wk, 'bk': bk}
    _L0_xattn_all = _L0_xattn_setup()
    _L0_xattn_in = {k: v for k, v in _L0_xattn_all.items() if k in ('Wq', 'bq', 'Wk', 'bk')}
    del _L0_xattn_all

    def _L0_ffn_setup():
        import jax, jax.numpy as jnp
        import numpy as np
        HID, BOT, RDIM, NSLOT, K, VB = (2048, 64, 48, 512, 8, 128)
        TAU_LOW, TAU_HIGH, EARLY_EXIT = (0.5, 2.0, 0.05)

        def _uncertainty(h, Wu1, bu1, Wu2, bu2):
            var = jnp.var(h, axis=-1)
            log_var = jnp.log1p(var)
            norm_var = log_var / (jnp.mean(log_var) + 1e-06)
            learned = (jax.nn.gelu(h @ Wu1.T + bu1) @ Wu2.T + bu2)[..., 0]
            return jnp.clip(norm_var * 0.5 + jax.nn.sigmoid(learned) * 2.5, 0.0, 5.0)
        key = jax.random.key(seed)
        ks = jax.random.split(key, 12)
        B, S = (2, 1024)
        return {'hidden_states': jax.random.normal(ks[0], (B, S, HID), dtype=jnp.float32), 'Wq': jax.random.normal(ks[1], (BOT, HID), dtype=jnp.float32) / np.sqrt(HID), 'Wr': jax.random.normal(ks[2], (RDIM, BOT), dtype=jnp.float32) / np.sqrt(BOT), 'aux_keys': jax.random.normal(ks[3], (NSLOT, BOT), dtype=jnp.float32) * 0.01, 'aux_values': jax.random.normal(ks[4], (NSLOT, HID), dtype=jnp.float32) * 0.02, 'Wvd': jax.random.normal(ks[5], (VB, HID), dtype=jnp.float32) * 0.1 / np.sqrt(HID), 'Wvu': jax.random.normal(ks[6], (HID, VB), dtype=jnp.float32) * 0.1 / np.sqrt(VB), 'Wu1': jax.random.normal(ks[7], (HID // 4, HID), dtype=jnp.float32) / np.sqrt(HID), 'bu1': jnp.zeros((HID // 4,), dtype=jnp.float32), 'Wu2': jax.random.normal(ks[8], (1, HID // 4), dtype=jnp.float32) * 0.01, 'bu2': jnp.zeros((1,), dtype=jnp.float32), 'gate_w1': jnp.float32(0.5), 'gate_bias': jnp.float32(-1.0), 'log_rel': jnp.zeros((NSLOT,), dtype=jnp.float32)}
    _L0_ffn_all = _L0_ffn_setup()
    _L0_ffn_in = {k: v for k, v in _L0_ffn_all.items() if k in ('Wq', 'Wr', 'aux_keys', 'aux_values', 'Wvd', 'Wvu', 'Wu1', 'bu1', 'Wu2', 'bu2', 'gate_w1', 'gate_bias', 'log_rel')}
    del _L0_ffn_all
    return {'x': x, 'ctx_4096': ctx_4096, 'g_xattn': g_xattn, 'g_ffn': g_ffn, 'L0_xattn_Wq': _L0_xattn_in['Wq'], 'L0_xattn_bq': _L0_xattn_in['bq'], 'L0_xattn_Wk': _L0_xattn_in['Wk'], 'L0_xattn_bk': _L0_xattn_in['bk'], 'L0_ffn_Wq': _L0_ffn_in['Wq'], 'L0_ffn_Wr': _L0_ffn_in['Wr'], 'L0_ffn_aux_keys': _L0_ffn_in['aux_keys'], 'L0_ffn_aux_values': _L0_ffn_in['aux_values'], 'L0_ffn_Wvd': _L0_ffn_in['Wvd'], 'L0_ffn_Wvu': _L0_ffn_in['Wvu'], 'L0_ffn_Wu1': _L0_ffn_in['Wu1'], 'L0_ffn_bu1': _L0_ffn_in['bu1'], 'L0_ffn_Wu2': _L0_ffn_in['Wu2'], 'L0_ffn_bu2': _L0_ffn_in['bu2'], 'L0_ffn_gate_w1': _L0_ffn_in['gate_w1'], 'L0_ffn_gate_bias': _L0_ffn_in['gate_bias'], 'L0_ffn_log_rel': _L0_ffn_in['log_rel']}

def reference(x, ctx_4096, g_xattn, g_ffn, L0_xattn_Wq, L0_xattn_bq, L0_xattn_Wk, L0_xattn_bk, L0_ffn_Wq, L0_ffn_Wr, L0_ffn_aux_keys, L0_ffn_aux_values, L0_ffn_Wvd, L0_ffn_Wvu, L0_ffn_Wu1, L0_ffn_bu1, L0_ffn_Wu2, L0_ffn_bu2, L0_ffn_gate_w1, L0_ffn_gate_bias, L0_ffn_log_rel):
    import jax
    import jax.numpy as jnp

    def _L0_xattn_ref(text, features, Wq, bq, Wk, bk):
        import jax, jax.numpy as jnp
        import numpy as np
        TEXT_DIM = 2048
        FEATURE_DIM = 2048

        def _xavier_uniform(key, shape):
            fan_in, fan_out = (shape[1], shape[0])
            limit = float(np.sqrt(6.0 / (fan_in + fan_out)))
            return jax.random.uniform(key, shape, jnp.float32, -limit, limit)
        Q = jnp.einsum('btx,dx->btd', text, Wq) + bq
        K = jnp.einsum('bpx,dx->bpd', features, Wk) + bk
        scale = 1.0 / jnp.sqrt(jnp.asarray(K.shape[-1], K.dtype))
        scores = jnp.einsum('btd,bpd->btp', Q, K) * scale
        attn = jax.nn.softmax(scores, axis=-1)
        attended = jnp.einsum('btp,bpd->btd', attn, features)
        return attended

    def _L0_ffn_ref(hidden_states, Wq, Wr, aux_keys, aux_values, Wvd, Wvu, Wu1, bu1, Wu2, bu2, gate_w1, gate_bias, log_rel):
        import jax, jax.numpy as jnp
        import numpy as np
        HID, BOT, RDIM, NSLOT, K, VB = (2048, 64, 48, 512, 8, 128)
        TAU_LOW, TAU_HIGH, EARLY_EXIT = (0.5, 2.0, 0.05)

        def _uncertainty(h, Wu1, bu1, Wu2, bu2):
            var = jnp.var(h, axis=-1)
            log_var = jnp.log1p(var)
            norm_var = log_var / (jnp.mean(log_var) + 1e-06)
            learned = (jax.nn.gelu(h @ Wu1.T + bu1) @ Wu2.T + bu2)[..., 0]
            return jnp.clip(norm_var * 0.5 + jax.nn.sigmoid(learned) * 2.5, 0.0, 5.0)
        query = hidden_states @ Wq.T
        rq = query @ Wr.T
        rk = aux_keys @ Wr.T
        router_scores = jnp.einsum('bsr,nr->bsn', rq, rk) / np.sqrt(RDIM) + log_rel
        top_scores, top_idx = jax.lax.top_k(router_scores, K)
        sel_keys = aux_keys[top_idx]
        attn = jnp.einsum('bsd,bskd->bsk', query, sel_keys) / np.sqrt(BOT) + log_rel[top_idx]
        w = jax.nn.softmax(attn, axis=-1)
        sel_vals = aux_values[top_idx]
        aux_out = jnp.einsum('bsk,bskh->bsh', w, sel_vals)
        aux_out = aux_out @ Wvd.T @ Wvu.T
        u = _uncertainty(hidden_states, Wu1, bu1, Wu2, bu2)
        u_norm = jnp.clip((u - TAU_LOW) / (TAU_HIGH - TAU_LOW), 0.0, 1.0)
        gate = jax.nn.sigmoid(gate_w1 * u_norm + gate_bias)
        gate = jnp.where(gate < EARLY_EXIT, 0.0, gate)
        return hidden_states + gate[..., None] * aux_out
    x = x + jnp.tanh(g_xattn[0]) * _L0_xattn_ref(_layernorm(x, axis=-1), ctx_4096, L0_xattn_Wq, L0_xattn_bq, L0_xattn_Wk, L0_xattn_bk)
    x = x + jnp.tanh(g_ffn[0]) * _L0_ffn_ref(_layernorm(x, axis=-1), L0_ffn_Wq, L0_ffn_Wr, L0_ffn_aux_keys, L0_ffn_aux_values, L0_ffn_Wvd, L0_ffn_Wvu, L0_ffn_Wu1, L0_ffn_bu1, L0_ffn_Wu2, L0_ffn_bu2, L0_ffn_gate_w1, L0_ffn_gate_bias, L0_ffn_log_rel)
    return x

_drawn_inputs = setup_inputs


def setup_inputs(seed=0):
    import zlib

    import numpy as np

    out = dict(_drawn_inputs(seed))
    spreads = {'L0_xattn_bq': (0.0, 0.313),
     'L0_xattn_bk': (0.0, 0.8),
     'L0_ffn_bu1': (0.0, 0.8),
     'L0_ffn_log_rel': (0.0, 0.8)}
    factors = {'L0_ffn_Wq': 8.0,
     'L0_ffn_Wr': 8.0,
     'L0_ffn_aux_keys': 8.0,
     'L0_ffn_aux_values': 8.0,
     'L0_ffn_Wvd': 8.0,
     'L0_ffn_Wvu': 8.0,
     'L0_ffn_Wu1': 8.0,
     'L0_ffn_Wu2': 8.0}
    for name, (base, spread) in spreads.items():
        noise = np.random.default_rng([zlib.crc32(name.encode()), seed]).standard_normal(out[name].shape)
        drawn = base * np.exp(spread * noise) if base else spread * noise
        out[name] = jnp.asarray(drawn.astype(out[name].dtype))
    for name, factor in factors.items():
        out[name] = (out[name] * factor).astype(out[name].dtype)
    return out
```

```python
from contextlib import ExitStack

import concourse.bass as bass
from concourse import mybir

P = 128
D = 2048
KC = D // P
BATCH, SEQ, NCTX = 4, 1024, 64
TILES = BATCH * SEQ // P
PAIRS = TILES // 2
CR = BATCH * NCTX
HU = 512
BOT, RDIM, NSLOT, VB, TOPK = 64, 48, 512, 128, 8
QN = 512
GROUPS = KC // 4
BW = 3 * NCTX
CWN = NCTX + BOT + HU
EPS = 1e-5
TAU_LOW, TAU_HIGH, EARLY_EXIT = 0.5, 2.0, 0.05
ATT_SCALE = 1.0 / float(D) ** 0.5
OUT_OF_RANGE = -1.0e30
PICKED = 1.0e30

ALU = mybir.AluOpType
ACT = mybir.ActivationFunctionType
AX = mybir.AxisListType
F32 = mybir.dt.float32
F32R = mybir.dt.float32r


def f32(ap):
    return ap.bitcast(F32)


def split_product(pe, out, left, right, start, stop, skip=False):
    (lh, ll), (rh, rl) = left, right
    pe.matmul(out, lh, rh, start=start, stop=False, skip_group_check=skip)
    pe.matmul(out, lh, rl, start=False, stop=False, skip_group_check=skip)
    return pe.matmul(out, ll, rh, start=False, stop=stop, skip_group_check=skip)


def at(t, i):
    return t[:, bass.ds(i, 1), :].rearrange("p o n -> p (o n)")


class Memory:

    def __init__(self, nc, ctx, tag):
        self.nc, self.ctx, self.tag = nc, ctx, tag

    def sb(self, name, shape, dt=F32):
        return self.ctx.enter_context(self.nc.sbuf_tensor(f"{self.tag}_{name}", shape, dt))

    def ps(self, name, shape=(P, QN), dt=F32):
        return self.ctx.enter_context(self.nc.psum_tensor(f"{self.tag}_{name}", list(shape), dt))

    def sem(self, name):
        return self.ctx.enter_context(self.nc.semaphore(f"{self.tag}_{name}"))


def transpose_group(pe, bank, src, g, ident, rows=P):
    for k in range(4):
        c = 4 * g + k
        ins = pe.transpose(bank[:, k * rows:(k + 1) * rows], src[0:rows, c * P:(c + 1) * P],
                           ident[0:rows, 0:rows])
    return ins


def context_block(nc, m0, io, scr, keep):
    with ExitStack() as ctx:
        m = Memory(nc, ctx, "cx")
        ctxT = keep["ctxT"]
        rows, cT = keep["rows"], keep["T"]
        nat = [(m.sb(f"nat_hi{r}", [P, D], F32R), m.sb(f"nat_lo{r}", [P, D], F32R)) for r in range(2)]
        raw32 = m.sb("bias_rows", [2 * KC, P])
        stats = [m.sb(f"stats{r}", [P, 4, 6]) for r in range(2)]
        mv = [m.sb(f"mv{r}", [P, 2]) for r in range(2)]
        nmean = [m.sb(f"nmean{r}", [P, 1]) for r in range(2)]
        diag = [m.sb(f"diag{r}", [P, P]) for r in range(2)]
        bank = [m.ps(f"bank{i}") for i in range(2)]
        ps_mu, ps_bias = m.ps("mu"), m.ps("bias")
        rows_in = [m.sem(f"rows_in{r}") for r in range(2)]
        small_in = m.sem("small_in")
        ident_zero, ident_done = m.sem("ident_zero"), m.sem("ident_done")
        turned, hi_done, lo_done = m.sem("turned"), m.sem("hi_done"), m.sem("lo_done")
        nat_hi_done, nat_lo_done = m.sem("nat_hi_done"), m.sem("nat_lo_done")
        mean_done, centred = m.sem("mean_done"), m.sem("centred")
        diag_done, mu_ready, bias_turned = m.sem("diag_done"), m.sem("mu_ready"), m.sem("bias_turned")
        gates_ready, stored = m.sem("gates_ready"), m.sem("stored")
        ident, ones = keep["ident"], keep["ones"]
        block = ctx.enter_context(nc.Block())

        @block.sync
        def _(sp):
            for r in range(2):
                sp.dma_start(rows[r][:], io["ctx"][r * P:(r + 1) * P, :]).then_inc(rows_in[r], 16)
            sp.dma_start(raw32[0:KC, :], io["bk"].rearrange("(c p) -> c p", p=P)).then_inc(small_in, 16)
            sp.dma_start(raw32[KC:2 * KC, :], io["bq"].rearrange("(c p) -> c p", p=P)).then_inc(small_in, 16)
            for dst, src in (("tgx", "g_xattn"), ("tgf", "g_ffn"), ("w1", "gate_w1"), ("gb", "gate_bias"),
                             ("bu2", "bu2")):
                sp.dma_start(keep[dst][:], io[src].broadcast_to([P, 1])).then_inc(small_in, 16)
            for r in range(2):
                sp.wait_ge(nat_hi_done, r + 1)
                sp.wait_ge(nat_lo_done, r + 1)
                for part in range(2):
                    sp.dma_start(scr["ctx"][part, r * P:(r + 1) * P, :], f32(nat[r][part][:])).then_inc(stored, 16)
            for r in range(2):
                sp.wait_ge(lo_done, 4 * GROUPS - (1 - r) * GROUPS)
                for part in range(2):
                    for k in range(2):
                        sp.dma_start(scr["x"][2 * r + k, part, :, :, NCTX:2 * NCTX],
                                     f32(cT[r][part][:, :, k * NCTX:(k + 1) * NCTX])).then_inc(stored, 16)
            sp.wait_ge(stored, 16 * 12)

        @block.gpsimd
        def _(pool):
            pool.memset(ident[:], 0.0).then_inc(ident_zero, 1)
            pool.memset(ones[:], 1.0).then_inc(ident_done, 1)
            pool.wait_ge(ident_zero, 1)
            pool.affine_select(out=ident[:], in_=ident[:], compare_op=ALU.not_equal, fill=1.0, base=0,
                               pattern=[[-1, P]], channel_multiplier=1).then_inc(ident_done, 1)

        @block.tensor
        def _(pe):
            pe.wait_ge(ident_done, 2)
            for n in range(4 * GROUPS):
                r = (n // GROUPS) % 2
                if n < 2 * GROUPS:
                    pe.wait_ge(rows_in[r], 16)
                else:
                    pe.wait_ge(centred, r + 1)
                if n >= 2:
                    pe.wait_ge(lo_done, n - 1)
                transpose_group(pe, bank[n % 2], rows[r], n % GROUPS, ident).then_inc(turned, 1)
            pe.wait_ge(diag_done, 2)
            for r in range(2):
                ins = pe.matmul(ps_mu[:, r * P:(r + 1) * P], ones[:], diag[r][:], start=True, stop=True)
            ins.then_inc(mu_ready, 1)
            pe.wait_ge(small_in, 16 * 7)
            pe.transpose(ps_bias[:, 0:2 * KC], raw32[:], ident[0:2 * KC, 0:2 * KC]).then_inc(bias_turned, 1)

        def out_of(n, part):
            r, g = (n // GROUPS) % 2, n % GROUPS
            if n < 2 * GROUPS:
                return ctxT[part][:, 4 * g:4 * g + 4, r * P:(r + 1) * P]
            return cT[r][part][:, 4 * g:4 * g + 4, :]

        @block.scalar
        def _(act):
            act.wait_ge(small_in, 16 * 7)
            act.activation(keep["tgx"][:], keep["tgx"][:], ACT.Tanh).then_inc(gates_ready, 1)
            act.activation(keep["tgf"][:], keep["tgf"][:], ACT.Tanh).then_inc(gates_ready, 1)
            for n in range(4 * GROUPS):
                r = (n // GROUPS) % 2
                if n in (2 * GROUPS, 3 * GROUPS):
                    act.wait_ge(turned, (r + 1) * GROUPS)
                    act.wait_ge(nat_lo_done, r + 1)
                    act.wait_ge(mean_done, r + 1)
                    act.activation(rows[r][:], rows[r][:], ACT.Identity, bias=nmean[r][:, 0:1]).then_inc(centred, 1)
                act.wait_ge(turned, n + 1)
                act.activation(out_of(n, 0), bank[n % 2][:].rearrange("p (k n) -> p k n", k=4),
                               ACT.Copy).then_inc(hi_done, 1)
                if n in (GROUPS - 1, 2 * GROUPS - 1):
                    act.activation(nat[r][0][:], rows[r][:], ACT.Copy).then_inc(nat_hi_done, 1)

        @block.vector
        def _(dve):
            for r in range(2):
                dve.wait_ge(rows_in[r], 16)
                for k in range(4):
                    dve.bn_stats(stats[r][:, k, :], rows[r][:, k * QN:(k + 1) * QN])
                dve.drain()
                dve.bn_aggr(mv[r][:], stats[r][:])
                dve.drain()
                dve.tensor_scalar(nmean[r][:], mv[r][:, 0:1], -1.0, None, ALU.mult).then_inc(mean_done, 1)
            dve.wait_ge(ident_done, 2)
            for r in range(2):
                dve.tensor_scalar(diag[r][:], ident[:], mv[r][:, 0:1], None, ALU.mult).then_inc(diag_done, 1)
            for n in range(4 * GROUPS):
                r = (n // GROUPS) % 2
                dve.wait_ge(hi_done, n + 1)
                dve.tensor_tensor(out_of(n, 1), bank[n % 2][:].rearrange("p (k n) -> p k n", k=4),
                                  f32(out_of(n, 0)), ALU.subtract).then_inc(lo_done, 1)
                if n in (GROUPS - 1, 2 * GROUPS - 1):
                    dve.wait_ge(nat_hi_done, r + 1)
                    dve.tensor_tensor(nat[r][1][:], rows[r][:], f32(nat[r][0][:]),
                                      ALU.subtract).then_inc(nat_lo_done, 1)
            dve.wait_ge(mu_ready, 1)
            dve.wait_ge(gates_ready, 2)
            for b in range(BATCH):
                for k in range(4):
                    dve.tensor_scalar(keep["mu_rows"][:, 4 * b + k, :], ps_mu[:, b * NCTX:(b + 1) * NCTX],
                                      keep["tgx"][:, 0:1], None, ALU.mult)
            dve.wait_ge(bias_turned, 1)
            dve.tensor_copy(keep["bias_cols"][:], ps_bias[:, 0:2 * KC])


def keys_block(nc, io, keep):
    with ExitStack() as ctx:
        m = Memory(nc, ctx, "ky")
        rows, T, ctxT, KT = keep["rows"], keep["T"], keep["ctxT"], keep["KT"]
        ident, ones, bias = keep["ident"], keep["ones"], keep["bias_cols"]
        kf = [m.sb(f"key_f32_{u}", [P, CR]) for u in range(2)]
        dot = m.sb("bq_dot", [P, CR])
        bank = [m.ps(f"bank{i}") for i in range(2)]
        kp = [m.ps(f"keys{u}") for u in range(2)]
        ps_row = m.ps("bq_row")
        rows_in = [m.sem(f"rows_in{u}") for u in range(2)]
        turned, hi_done, lo_done = m.sem("turned"), m.sem("hi_done"), m.sem("lo_done")
        product, biased, key_hi, key_lo = m.sem("product"), m.sem("biased"), m.sem("key_hi"), m.sem("key_lo")
        dot_zero, dot_done, row_done = m.sem("dot_zero"), m.sem("dot_done"), m.sem("row_done")
        block = ctx.enter_context(nc.Block())
        wk = io["Wk"].rearrange("(t p) d -> t p d", p=P)

        def load(sp, n, u):
            sp.dma_start(rows[u][:], wk[bass.ds(n, 1)].rearrange("o p d -> p (o d)")).then_inc(rows_in[u], 16)

        @block.sync
        def _(sp):
            for u in range(2):
                load(sp, u, u)
            with sp.Fori(1, KC // 2) as j:
                for u in range(2):
                    sp.wait_ge(turned, GROUPS * (2 * j + u - 1))
                    load(sp, 2 * j + u, u)

        @block.tensor
        def _(pe):
            for g in range(GROUPS):
                if g == 0:
                    pe.wait_ge(rows_in[0], 16)
                if g >= 2:
                    pe.wait_ge(lo_done, g - 1)
                transpose_group(pe, bank[g % 2], rows[0], g, ident).then_inc(turned, 1)

            def body(j, first=False, last=False):
                for u in range(2):
                    n = 2 * j + u
                    if not first:
                        pe.wait_ge(biased, n - 1)
                    for g in range(GROUPS):
                        pe.wait_ge(lo_done, GROUPS * n + g + 1)
                        for c in range(4 * g, 4 * g + 4):
                            ins = split_product(pe, kp[u][:, 0:CR], (T[u][0][:, c, :], T[u][1][:, c, :]),
                                                (ctxT[0][:, c, :], ctxT[1][:, c, :]), c == 0, c == KC - 1)
                        if g == GROUPS - 1:
                            ins.then_inc(product, 1)
                        if last and u == 1:
                            continue
                        if g == 0:
                            pe.wait_ge(rows_in[1 - u], 16 * (j + 1 + u))
                        pe.wait_ge(lo_done, GROUPS * (n + 1) + g - 1)
                        transpose_group(pe, bank[g % 2], rows[1 - u], g, ident).then_inc(turned, 1)

            body(0, first=True)
            with pe.Fori(1, KC // 2 - 1) as j:
                body(j)
            body(KC // 2 - 1, last=True)
            pe.wait_ge(dot_done, KC)
            pe.matmul(ps_row[:, 0:CR], ones[:], dot[:], start=True, stop=True).then_inc(row_done, 1)

        @block.scalar
        def _(act):
            def parts_hi(n, u):
                for g in range(GROUPS):
                    act.wait_ge(turned, GROUPS * n + g + 1)
                    act.activation(T[u][0][:, 4 * g:4 * g + 4, :],
                                   bank[g % 2][:].rearrange("p (k n) -> p k n", k=4),
                                   ACT.Copy).then_inc(hi_done, 1)

            def key_parts(n, u):
                act.wait_ge(biased, n + 1)
                act.activation(KT[0][:, bass.ds(n, 1), :].rearrange("p o n -> p (o n)"), kf[u][:],
                               ACT.Copy).then_inc(key_hi, 1)

            def body(j, last=False):
                for u in range(2):
                    if not (last and u == 1):
                        parts_hi(2 * j + u + 1, 1 - u)
                    key_parts(2 * j + u, u)

            parts_hi(0, 0)
            with act.Fori(0, KC // 2 - 1) as j:
                body(j)
            body(KC // 2 - 1, last=True)

        @block.vector
        def _(dve):
            def parts_lo(n, u):
                for g in range(GROUPS):
                    dve.wait_ge(hi_done, GROUPS * n + g + 1)
                    dve.tensor_tensor(T[u][1][:, 4 * g:4 * g + 4, :],
                                      bank[g % 2][:].rearrange("p (k n) -> p k n", k=4),
                                      f32(T[u][0][:, 4 * g:4 * g + 4, :]), ALU.subtract).then_inc(lo_done, 1)

            def key_parts(n, u):
                dve.wait_ge(product, n + 1)
                dve.tensor_scalar(kf[u][:], kp[u][:, 0:CR], bias[:, bass.ds(n, 1)], None,
                                  ALU.add).then_inc(biased, 1)
                dve.drain()
                dve.scalar_tensor_tensor(dot[:], kf[u][:], bias[:, bass.ds(KC + n, 1)], dot[:],
                                         ALU.mult, ALU.add).then_inc(dot_done, 1)
                dve.wait_ge(key_hi, n + 1)
                hi = f32(KT[0][:, bass.ds(n, 1), :]).rearrange("p o n -> p (o n)")
                dve.tensor_tensor(KT[1][:, bass.ds(n, 1), :].rearrange("p o n -> p (o n)"), kf[u][:], hi,
                                  ALU.subtract).then_inc(key_lo, 1)

            def body(j, last=False):
                for u in range(2):
                    if not (last and u == 1):
                        parts_lo(2 * j + u + 1, 1 - u)
                    key_parts(2 * j + u, u)

            dve.memset(dot[:], 0.0)
            parts_lo(0, 0)
            with dve.Fori(0, KC // 2 - 1) as j:
                body(j)
            body(KC // 2 - 1, last=True)
            dve.wait_ge(row_done, 1)
            for b in range(BATCH):
                for k in range(4):
                    dve.tensor_scalar(keep["bq_rows"][:, 4 * b + k, :], ps_row[:, b * NCTX:(b + 1) * NCTX],
                                      ATT_SCALE, None, ALU.mult)


def score_weights_block(nc, io, scr, keep):
    with ExitStack() as ctx:
        m = Memory(nc, ctx, "sw")
        rows, T, KT = keep["rows"], keep["T"], keep["KT"]
        mp = [m.ps(f"mt{u}") for u in range(2)]
        out = [(m.sb(f"mt_hi{u}", [P, CR], F32R), m.sb(f"mt_lo{u}", [P, CR], F32R)) for u in range(2)]
        rows_in = [m.sem(f"rows_in{u}") for u in range(2)]
        hi_done, lo_done, product = m.sem("hi_done"), m.sem("lo_done"), m.sem("product")
        out_hi, out_lo = m.sem("out_hi"), m.sem("out_lo")
        stored = [m.sem(f"stored{u}") for u in range(2)]
        block = ctx.enter_context(nc.Block())
        wq = io["Wq"].rearrange("(c p) (t x) -> t p c x", p=P, x=P)

        def load(sp, n, u):
            sp.dma_start(rows[u][:].rearrange("p (c x) -> p c x", x=P),
                         wq[bass.ds(n, 1)].rearrange("o p c x -> p (o c) x")).then_inc(rows_in[u], 16)

        @block.sync
        def _(sp):
            for u in range(2):
                load(sp, u, u)
            with sp.Fori(1, KC // 2) as j:
                for u in range(2):
                    sp.wait_ge(lo_done, 2 * j + u - 1)
                    load(sp, 2 * j + u, u)

        @block.scalar
        def _(act):
            def weights_hi(n, u, first=False):
                act.wait_ge(rows_in[u], 8 * (n - u) + 16)
                if not first:
                    act.wait_ge(product, n - 1)
                act.activation(T[u][0][:].rearrange("p c x -> p (c x)"), rows[u][:], ACT.Copy).then_inc(hi_done, 1)

            def result(n, u, j, first):
                act.wait_ge(product, n + 1)
                if not first:
                    act.wait_ge(stored[u], 32 * j)
                act.activation(out[u][0][:], mp[u][:, 0:CR], ACT.Copy).then_inc(out_hi, 1)
                act.wait_ge(out_lo, n + 1)
                for part in range(2):
                    act.dma_start(scr["x"][:, part, :, bass.ds(n, 1), 0:NCTX].rearrange("b p o n -> p (o b) n"),
                                  f32(out[u][part][:]).rearrange("p (b n) -> p b n", n=NCTX)
                                  ).then_inc(stored[u], 16)

            def body(j, first=False, last=False):
                for u in range(2):
                    if not (last and u == 1):
                        weights_hi(2 * j + u + 1, 1 - u, first and u == 0)
                    result(2 * j + u, u, j, first)

            weights_hi(0, 0, True)
            body(0, first=True)
            with act.Fori(1, KC // 2 - 1) as j:
                body(j)
            body(KC // 2 - 1, last=True)
            for u in range(2):
                act.wait_ge(stored[u], 32 * (KC // 2))

        @block.vector
        def _(dve):
            def weights_lo(n, u):
                dve.wait_ge(hi_done, n + 1)
                dve.tensor_tensor(T[u][1][:].rearrange("p c x -> p (c x)"), rows[u][:],
                                  f32(T[u][0][:]).rearrange("p c x -> p (c x)"), ALU.subtract).then_inc(lo_done, 1)

            def body(j, last=False):
                for u in range(2):
                    n = 2 * j + u
                    if not (last and u == 1):
                        weights_lo(n + 1, 1 - u)
                    dve.wait_ge(out_hi, n + 1)
                    dve.tensor_tensor(out[u][1][:], mp[u][:, 0:CR], f32(out[u][0][:]),
                                      ALU.subtract).then_inc(out_lo, 1)

            weights_lo(0, 0)
            with dve.Fori(0, KC // 2 - 1) as j:
                body(j)
            body(KC // 2 - 1, last=True)

        @block.tensor
        def _(pe):
            def body(j, first):
                for u in range(2):
                    n = 2 * j + u
                    pe.wait_ge(lo_done, n + 1)
                    if not first:
                        pe.wait_ge(out_lo, n - 1)
                    for c in range(KC):
                        ins = split_product(pe, mp[u][:, 0:CR], (T[u][0][:, c, :], T[u][1][:, c, :]),
                                            (KT[0][:, c, :], KT[1][:, c, :]), c == 0, c == KC - 1)
                    ins.then_inc(product, 1)

            body(0, True)
            with pe.Fori(1, KC // 2) as j:
                body(j, False)


def ffn_block(nc, io, scr, keep):
    with ExitStack() as ctx:
        m = Memory(nc, ctx, "fw")
        ident, ones = keep["ident"], keep["ones"]
        bw, wu = keep["bw"], keep["wu"]
        rows = [m.sb(f"rows{u}", [P, D]) for u in range(2)]
        part = (m.sb("part_hi", [P, KC, P], F32R), m.sb("part_lo", [P, KC, P], F32R))
        wvd = (m.sb("wvd_hi", [P, KC, P], F32R), m.sb("wvd_lo", [P, KC, P], F32R))
        wr, ak = m.sb("wr", [RDIM, BOT]), m.sb("aux_keys", [P, 4, BOT])
        wrT, akT = m.sb("wr_turned", [BOT, RDIM]), m.sb("aux_keys_turned", [P, NSLOT])
        rkT, gate2 = m.sb("router_keys", [RDIM, NSLOT]), m.sb("router_weights", [P, NSLOT])
        wr2, logr = m.sb("wr_twice", [RDIM, 2 * BOT]), m.sb("log_rel", [P, 2 * NSLOT])
        akT8 = m.sb("aux_keys_scaled", [P, NSLOT])
        bank = [m.ps(f"bank{i}") for i in range(2)]
        ps_av, ps_small, ps_rk, ps_g = m.ps("av"), m.ps("small"), m.ps("rk"), m.ps("g")
        rows_in = [m.sem(f"rows_in{u}") for u in range(2)]
        small_in, wvu_out = m.sem("small_in"), m.sem("wvu_out")
        turned, hi_done, lo_done = m.sem("turned"), m.sem("hi_done"), m.sem("lo_done")
        product, av_done = m.sem("product"), m.sem("av_done")
        keys_turned, keys_out, wr_turned, wr_out = (m.sem("keys_turned"), m.sem("keys_out"),
                                                    m.sem("wr_turned"), m.sem("wr_out"))
        wr2_done, ak2_done = m.sem("wr2_done"), m.sem("ak2_done")
        rk_ready, rk_out, g_ready = m.sem("rk_ready"), m.sem("rk_out"), m.sem("g_ready")
        slot_f32, slot_hi, log_hi = m.sem("slot_f32"), m.sem("slot_hi"), m.sem("log_hi")
        rs1, rs2, q2s = keep["rs1"], keep["rs2"], keep["q2s"]
        block = ctx.enter_context(nc.Block())

        wu1 = io["Wu1"].rearrange("(t p) d -> t p d", p=P)
        av = io["aux_values"].rearrange("(t p) d -> t p d", p=P)
        jobs = [(io["fWq"], BOT, [bw[i][:, :, 2 * NCTX:BW] for i in range(2)])]
        jobs += [(wu1[t], P, [wu[i][:, :, t * P:(t + 1) * P] for i in range(2)]) for t in range(4)]
        jobs += [(io["Wvd"], P, [wvd[i][:] for i in range(2)])]
        jobs += [(av[t], P, [part[i][:] for i in range(2)]) for t in range(4)]
        jobs += [(None, P, [part[i][:] for i in range(2)])]
        FIRST_AV, WVU = 6, 10

        @block.sync
        def _(sp):
            for n, (src, r, _) in enumerate(jobs):
                if n >= 2:
                    sp.wait_ge(turned, GROUPS * (n - 1))
                if src is None:
                    sp.dma_start(rows[n % 2][:].rearrange("p (c v) -> p c v", v=VB),
                                 io["Wvu"].rearrange("(c p) v -> p c v", p=P)).then_inc(rows_in[n % 2], 16)
                else:
                    sp.dma_start(rows[n % 2][0:r, :], src).then_inc(rows_in[n % 2], 16)
                if n == 1:
                    sp.dma_start(wr[:], io["Wr"]).then_inc(small_in, 16)
                    sp.dma_start(ak[:], io["aux_keys"].rearrange("(t p) b -> p t b", p=P)).then_inc(small_in, 16)
                    sp.dma_start(logr[BOT:BOT + 2, 0:NSLOT],
                                 io["log_rel"].rearrange("(a n) -> a n", a=1).broadcast_to([2, NSLOT])
                                 ).then_inc(small_in, 16)
                    sp.dma_start(logr[BOT:BOT + 2, NSLOT:2 * NSLOT],
                                 io["log_rel"].rearrange("(a n) -> a n", a=1).broadcast_to([2, NSLOT])
                                 ).then_inc(small_in, 16)
                    for dst, src in (("bu1", "bu1"), ("wu2", "wu2")):
                        sp.dma_start(keep[dst][:], io[src].rearrange("(a n) -> a n", a=1).broadcast_to([P, HU])
                                     ).then_inc(small_in, 16)
            for i in range(2):
                sp.wait_ge(lo_done, GROUPS * (WVU + 1))
                sp.dma_start(scr["wvu"][i], f32(part[i][:]).rearrange("p c v -> p (c v)")).then_inc(wvu_out, 16)
            sp.wait_ge(wvu_out, 32)

        @block.tensor
        def _(pe):
            for n, (_, r, _) in enumerate(jobs):
                pe.wait_ge(rows_in[n % 2], 16 * (n // 2 + 1))
                for g in range(GROUPS):
                    if GROUPS * n + g >= 2:
                        pe.wait_ge(lo_done, GROUPS * n + g - 1)
                    transpose_group(pe, bank[g % 2], rows[n % 2], g, ident, r).then_inc(turned, 1)
                if n == 1:
                    pe.wait_ge(small_in, 16 * 6)
                    for t in range(4):
                        ins = pe.transpose(ps_small[0:BOT, t * P:(t + 1) * P], ak[:, t, :], ident[:])
                    ins.then_inc(keys_turned, 1)
                    pe.transpose(ps_g[0:BOT, 0:RDIM], wr[:], ident[0:RDIM, 0:RDIM]).then_inc(wr_turned, 1)
                    pe.wait_ge(keys_out, 1)
                    pe.wait_ge(wr_out, 1)
                    pe.matmul(ps_rk[0:RDIM, :], wrT[:], akT[0:BOT, :], start=True, stop=True).then_inc(rk_ready, 1)
                    pe.wait_ge(rk_out, 1)
                    pe.wait_ge(wr2_done, 1)
                    pe.matmul(ps_g[:], wr2[:], rkT[:], start=True, stop=True).then_inc(g_ready, 1)
                    pe.wait_ge(ak2_done, 1)
                    for t in range(4):
                        ins = pe.transpose(ps_small[:, t * P:(t + 1) * P], keep["ak2"][:, t, :], ident[:])
                    ins.then_inc(keys_turned, 1)
                if FIRST_AV <= n < WVU:
                    pe.wait_ge(lo_done, GROUPS * (n + 1))
                    if n > FIRST_AV:
                        pe.wait_ge(av_done, n - FIRST_AV)
                    for c in range(KC):
                        ins = split_product(pe, ps_av[:, 0:VB], (part[0][:, c, :], part[1][:, c, :]),
                                            (wvd[0][:, c, :], wvd[1][:, c, :]), c == 0, c == KC - 1)
                    ins.then_inc(product, 1)

        @block.scalar
        def _(act):
            for n, (_, r, dst) in enumerate(jobs):
                if n > FIRST_AV:
                    act.wait_ge(product, n - FIRST_AV)
                for g in range(GROUPS):
                    act.wait_ge(turned, GROUPS * n + g + 1)
                    act.activation(dst[0][:, 4 * g:4 * g + 4, :],
                                   bank[g % 2][:, 0:4 * r].rearrange("p (k n) -> p k n", k=4),
                                   ACT.Copy).then_inc(hi_done, 1)
                if n == 1:
                    act.wait_ge(small_in, 16 * 6)
                    act.activation(wr2[:, 0:BOT], wr[:], ACT.Copy)
                    act.activation(wr2[:, BOT:2 * BOT], wr[:], ACT.Copy).then_inc(wr2_done, 1)
                    act.activation(keep["ak2"][:, :, 0:BOT], ak[:], ACT.Copy, scale=0.125)
                    act.activation(keep["ak2"][:, :, BOT:2 * BOT], ak[:], ACT.Copy, scale=0.125).then_inc(ak2_done, 1)
                    act.wait_ge(slot_f32, 2)
                    act.activation(rs1[:, 0:NSLOT], gate2[:], ACT.Copy)
                    act.activation(rs1[:, NSLOT:2 * NSLOT], akT8[:], ACT.Copy)
                    act.activation(rs2[BOT:BOT + 2, :], logr[BOT:BOT + 2, :], ACT.Copy).then_inc(slot_hi, 1)

        @block.vector
        def _(dve):
            dve.memset(q2s[BOT:BOT + 2, :].bitcast(F32), 1.0)
            for n, (_, r, dst) in enumerate(jobs):
                for g in range(GROUPS):
                    dve.wait_ge(hi_done, GROUPS * n + g + 1)
                    dve.tensor_tensor(dst[1][:, 4 * g:4 * g + 4, :],
                                      bank[g % 2][:, 0:4 * r].rearrange("p (k n) -> p k n", k=4),
                                      f32(dst[0][:, 4 * g:4 * g + 4, :]), ALU.subtract).then_inc(lo_done, 1)
                if n == 1:
                    dve.wait_ge(small_in, 16 * 6)
                    dve.tensor_scalar(keep["wu2"][:], keep["wu2"][:], 0.5, None, ALU.mult)
                    dve.wait_ge(keys_turned, 1)
                    dve.tensor_copy(akT[0:BOT, :], ps_small[0:BOT, :]).then_inc(keys_out, 1)
                    dve.wait_ge(wr_turned, 1)
                    dve.tensor_copy(wrT[:], ps_g[0:BOT, 0:RDIM]).then_inc(wr_out, 1)
                    dve.wait_ge(rk_ready, 1)
                    dve.tensor_copy(rkT[:], ps_rk[0:RDIM, :]).then_inc(rk_out, 1)
                    dve.wait_ge(g_ready, 1)
                    dve.tensor_scalar(gate2[:], ps_g[:], 1.0 / float(RDIM) ** 0.5, None, ALU.mult).then_inc(slot_f32, 1)
                    dve.wait_ge(keys_turned, 2)
                    dve.tensor_copy(akT8[:], ps_small[:]).then_inc(slot_f32, 1)
                    dve.wait_ge(slot_hi, 1)
                    dve.tensor_tensor(rs2[0:BOT, 0:NSLOT], gate2[0:BOT, :], f32(rs1[0:BOT, 0:NSLOT]), ALU.subtract)
                    dve.tensor_tensor(rs2[0:BOT, NSLOT:2 * NSLOT], akT8[0:BOT, :],
                                      f32(rs1[0:BOT, NSLOT:2 * NSLOT]), ALU.subtract)
                    dve.tensor_tensor(rs2[BOT:BOT + 1, :], logr[BOT:BOT + 1, :], f32(rs2[BOT:BOT + 1, :]),
                                      ALU.subtract).then_inc(log_hi, 1)
                if FIRST_AV <= n < WVU:
                    s = n - FIRST_AV
                    dve.wait_ge(product, s + 1)
                    dve.tensor_copy(keep["av"][:, s, :], ps_av[:, 0:VB]).then_inc(av_done, 1)


def context_weights_block(nc, io, scr, keep):
    with ExitStack() as ctx:
        m = Memory(nc, ctx, "cw")
        bw, wu, tgx = keep["bw"], keep["wu"], keep["tgx"]
        cT = [m.sb(f"ctx_turned{i}", [P, KC, CR], F32R) for i in range(2)]
        cw = [m.sb(f"cw{r}", [P, CWN]) for r in range(2)]
        hr = [m.sb(f"cw_hi{r}", [P, CWN], F32R) for r in range(2)]
        lo = [m.sb(f"cw_lo{r}", [P, CWN]) for r in range(2)]
        bank_u = [m.ps(f"hidden{r}") for r in range(2)]
        bank_q = [m.ps(f"query{r}") for r in range(2)]
        ctx_in, product, scaled, high, low, stored = (m.sem("ctx_in"), m.sem("product"), m.sem("scaled"),
                                                      m.sem("high"), m.sem("low"), m.sem("stored"))
        block = ctx.enter_context(nc.Block())

        @block.sync
        def _(sp):
            for part in range(2):
                for b in range(BATCH):
                    sp.dma_start(f32(cT[part][:, :, b * NCTX:(b + 1) * NCTX]),
                                 scr["x"][b, part, :, :, NCTX:2 * NCTX]).then_inc(ctx_in, 16)
            for r in range(2):
                sp.wait_ge(low, r + 1)
                for part, src in ((0, f32(hr[r][:])), (1, lo[r][:])):
                    sp.dma_start(scr["cw"][part, r * P:(r + 1) * P, :], src).then_inc(stored, 16)
            sp.wait_ge(stored, 64)

        @block.tensor
        def _(pe):
            pe.wait_ge(ctx_in, 16 * 2 * BATCH)
            for r in range(2):
                for c in range(KC):
                    left = tuple(cT[i][:, c, r * P:(r + 1) * P] for i in range(2))
                    split_product(pe, bank_u[r][:], left, (wu[0][:, c, :], wu[1][:, c, :]), c == 0, c == KC - 1)
                    split_product(pe, bank_q[r][:, 0:P], left,
                                  tuple(cT[i][:, c, r * P:(r + 1) * P] for i in range(2)), c == 0, c == KC - 1, True)
                    ins = split_product(pe, bank_q[r][:, P:P + BOT], left,
                                        (bw[0][:, c, 2 * NCTX:BW], bw[1][:, c, 2 * NCTX:BW]), False, c == KC - 1, True)
                ins.then_inc(product, 1)

        @block.vector
        def _(dve):
            for r in range(2):
                dve.wait_ge(product, r + 1)
                dve.tensor_scalar(cw[r][:, NCTX + BOT:CWN], bank_u[r][:], tgx[:, 0:1], None, ALU.mult)
                dve.tensor_scalar(cw[r][:, NCTX:NCTX + BOT], bank_q[r][:, P:P + BOT], tgx[:, 0:1], None, ALU.mult)
                for k in range(2):
                    own = slice(k * NCTX, (k + 1) * NCTX)
                    ins = dve.tensor_scalar(cw[r][own, 0:NCTX], bank_q[r][own, own], tgx[own, 0:1], 0.5,
                                            ALU.mult, ALU.mult)
                ins.then_inc(scaled, 1)
                dve.wait_ge(high, r + 1)
                dve.tensor_tensor(lo[r][:], cw[r][:], f32(hr[r][:]), ALU.subtract).then_inc(low, 1)

        @block.scalar
        def _(act):
            for r in range(2):
                act.wait_ge(scaled, r + 1)
                act.activation(hr[r][:], cw[r][:], ACT.Copy).then_inc(high, 1)


def token_block(nc, io, scr, keep):
    with ExitStack() as ctx:
        m = Memory(nc, ctx, "tk")
        ident = keep["ident"]
        bw, wu, rs1, rs2, av = keep["bw"], keep["wu"], keep["rs1"], keep["rs2"], keep["av"]
        x = [m.sb(f"x{u}", [P, D]) for u in range(2)]
        xT = [(m.sb(f"x_turned_hi{u}", [P, KC, P], F32R), m.sb(f"x_turned_lo{u}", [P, KC, P], F32R))
              for u in range(2)]
        cw1, cw2 = m.sb("cw_stack", [P, CWN], F32R), m.sb("cw_low", [NCTX, CWN], F32R)
        stats = m.sb("stats", [P, 4, 6])
        mv = [m.sb(f"mean_var{u}", [P, 2]) for u in range(2)]
        nmean = [m.sb(f"nmean{u}", [P, 1]) for u in range(2)]
        rstd1 = [m.sb(f"rstd1_{u}", [P, 1]) for u in range(2)]
        nscale = m.sb("neg_score_scale", [P, 1])
        neg_s, neg_max = m.sb("neg_scores", [P, NCTX]), m.sb("neg_max", [P, 1])
        esum, einv = m.sb("exp_sum", [P, 1]), m.sb("exp_inv", [P, 1])
        e1 = m.sb("exp_scores", [P, NCTX])
        att2 = [m.sb(f"att_twice{u}", [P, 2 * NCTX]) for u in range(2)]
        attS = m.sb("att_stack", [P, P], F32R)
        junk, junk2, shift = m.sb("junk", [P, NCTX]), m.sb("junk2", [P, NCTX]), m.sb("mean_shift", [P, 1])
        mvk = [m.sb(f"mean_var_kept{u}", [P, 2]) for u in range(2)]
        st2 = [m.sb(f"stats2_{u}", [P, 4]) for u in range(2)]
        ve = m.sb("var_eps", [P, 1])
        ve1 = m.sb("var_eps1", [P, 1])
        q2, qS = m.sb("query_twice", [P, 2 * BOT]), m.sb("query_stack", [P, P], F32R)
        q2s = keep["q2s"]
        hid, act1, hw = m.sb("hidden", [P, HU]), m.sb("gelu", [P, HU]), m.sb("hidden_wu2", [P, HU])
        top8, picked = m.sb("top8", [P, TOPK]), m.sb("picked", [P, NSLOT])
        ws, wmax, wneg = m.sb("slot_weights", [P, NSLOT]), m.sb("slot_max", [P, 1]), m.sb("slot_neg", [P, 1])
        wsum, winv = m.sb("slot_sum", [P, 1]), m.sb("slot_inv", [P, 1])
        wT = m.sb("weights_turned", [P, NSLOT])
        bank = [m.ps(f"bank{i}") for i in range(2)]
        psA, psB = m.ps("hidden_sum"), [m.ps(f"b_sum{u}") for u in range(2)]
        psR, psS, psM = m.ps("router"), m.ps("slots"), m.ps("small")
        att_turned_ps, q_turned_ps, z_ps = psM[:, 0:P], psM[:, P:2 * P], psM[:, 2 * P:2 * P + VB]

        S = {n: m.sem(n) for n in (
            "b_in", "cw_in", "turned", "x_hi", "x_lo", "b_sum", "a_sum", "c_sum", "centred",
            "mean_var", "rstd1", "neg_scores", "exp", "att", "att_turned", "att_hi", "att_lo",
            "var1", "rstd2", "query", "q_turned", "q_hi", "q_lo", "hidden", "routed", "slots",
            "slot_exp", "w_turned", "w_out", "z_sum", "z_out", "square", "inner", "tanh", "hw", "learned",
            "kept_att", "kept_stats", "poly")}
        x_in = [m.sem(f"x_in{u}") for u in range(2)]
        block = ctx.enter_context(nc.Block())
        xin = io["x"].rearrange("(t p) d -> t p d", p=P)
        G = GROUPS

        def load_x(sp, t, u):
            sp.dma_start(x[u][:], xin[bass.ds(t, 1)].rearrange("o p d -> p (o d)")).then_inc(x_in[u], 16)

        def load_batch_b(sp, b):
            for part in range(2):
                sp.dma_start(f32(bw[part][:, :, 0:2 * NCTX]),
                             scr["x"][bass.ds(b, 1), part].rearrange("o p c n -> p (o c) n")).then_inc(S["b_in"], 16)

        def load_batch_cw(sp, b):
            for half in range(2):
                sp.dma_start(f32(cw1[half * NCTX:(half + 1) * NCTX, :]),
                             scr["cw"][0, bass.ds(b * NCTX, NCTX), :]).then_inc(S["cw_in"], 16)
            sp.dma_start(f32(cw2[:]), scr["cw"][1, bass.ds(b * NCTX, NCTX), :]).then_inc(S["cw_in"], 16)

        @block.sync
        def _(sp):
            for t in range(2):
                load_x(sp, t, t)
            load_batch_b(sp, 0)
            load_batch_cw(sp, 0)
            for t in range(2, 8):
                sp.wait_ge(S["turned"], G * (t - 1))
                load_x(sp, t, t % 2)
            with sp.Fori(1, BATCH) as b:
                for k in range(8):
                    sp.wait_ge(S["turned"], G * (8 * b + k - 1))
                    load_x(sp, 8 * b + k, k % 2)
                    if k == 1:
                        sp.wait_ge(S["b_sum"], 8 * b)
                        load_batch_b(sp, b)
                        sp.wait_ge(S["c_sum"], 8 * b)
                        load_batch_cw(sp, b)

        @block.tensor
        def _(pe):
            def turn_x(t, u, g, first=False):
                if not (first and g < 2):
                    pe.wait_ge(S["x_lo"], G * t + g - 1)
                transpose_group(pe, bank[g % 2], x[u], g, ident).then_inc(S["turned"], 1)

            def a_part(t, u, g, first):
                if g == 0 and not first:
                    pe.wait_ge(S["hidden"], t)
                for c in range(4 * g, 4 * g + 4):
                    split_product(pe, psA[:], (xT[u][0][:, c, :], xT[u][1][:, c, :]),
                                  (wu[0][:, c, :], wu[1][:, c, :]), c == 0, c == KC - 1, True)

            def late_query(t, first=False):
                pe.wait_ge(S["query"], t + 1)
                if not first:
                    pe.wait_ge(S["z_out"], t)
                pe.transpose(q_turned_ps, q2[:], ident[:]).then_inc(S["q_turned"], 1)

            def late_route(t, first):
                pe.wait_ge(S["q_lo"], t + 1)
                pe.wait_ge(S["q_hi"], t + 1)
                if not first:
                    pe.wait_ge(S["w_out"], t)
                    pe.wait_ge(S["slots"], t)
                for bank_, n in ((psR, 0), (psS, NSLOT)):
                    pe.matmul(bank_[:], qS[:], rs1[:, n:n + NSLOT], start=True, stop=False)
                    ins = pe.matmul(bank_[:], q2s[0:BOT + 2, :], rs2[:, n:n + NSLOT], start=False, stop=True)
                ins.then_inc(S["routed"], 1)

            def late_turn_w(t):
                pe.wait_ge(S["slot_exp"], t + 1)
                for k in range(4):
                    ins = pe.transpose(psR[:, k * P:(k + 1) * P], ws[:, k * P:(k + 1) * P], ident[:])
                ins.then_inc(S["w_turned"], 1)

            def late_z(t, more=True):
                pe.wait_ge(S["w_out"], t + 1)
                pe.wait_ge(S["att_lo"], t + 2 if more else t + 1)
                for k in range(4):
                    ins = pe.matmul(z_ps, wT[:, k * P:(k + 1) * P], av[:, k, :], start=(k == 0), stop=(k == 3))
                ins.then_inc(S["z_sum"], 1)

            def tile(t, u, late=True, late_first=False, first=False, last=False, second=False, j=None):
                pe.wait_ge(S["b_in"], 32 * b_of(j))
                pe.wait_ge(S["x_lo"], G * (t + 1))
                if not (first or second):
                    pe.wait_ge(S["query"], t - 1)
                for c in range(KC):
                    ins = split_product(pe, psB[u][:, 0:BW], (xT[u][0][:, c, :], xT[u][1][:, c, :]),
                                        (bw[0][:, c, :], bw[1][:, c, :]), c == 0, c == KC - 1, True)
                ins.then_inc(S["b_sum"], 1)
                if late:
                    late_query(t - 1, late_first)
                a_part(t, u, 0, first)
                if not last:
                    pe.wait_ge(S["centred"], t + 2)
                    turn_x(t + 1, 1 - u, 0)
                if late:
                    late_route(t - 1, late_first)
                a_part(t, u, 1, first)
                if not last:
                    turn_x(t + 1, 1 - u, 1)
                pe.wait_ge(S["att"], t + 1)
                pe.transpose(att_turned_ps, att2[u][:], ident[:]).then_inc(S["att_turned"], 1)
                a_part(t, u, 2, first)
                if not last:
                    turn_x(t + 1, 1 - u, 2)
                if late:
                    late_turn_w(t - 1)
                a_part(t, u, 3, first)
                if not last:
                    turn_x(t + 1, 1 - u, 3)
                if late:
                    late_z(t - 1)
                pe.wait_ge(S["cw_in"], 48 * b_of(j))
                pe.wait_ge(S["att_hi"], t + 1)
                pe.wait_ge(S["att_lo"], t + 1)
                for out, n0, n1 in ((psB[u][:, NCTX:BW], 0, NCTX + BOT), (psA[:], NCTX + BOT, CWN)):
                    pe.matmul(out, attS[:], cw1[:, n0:n1], start=False, stop=False, skip_group_check=True)
                    ins = pe.matmul(out, attS[0:NCTX, :], cw2[:, n0:n1], start=False, stop=True,
                                    skip_group_check=True)
                ins.then_inc(S["c_sum"], 1)

            def b_of(j):
                return j // 4 + 1

            pe.wait_ge(S["centred"], 1)
            for g in range(G):
                turn_x(0, 0, g, first=True)
            tile(0, 0, late=False, first=True, j=0)
            tile(1, 1, late_first=True, second=True, j=0)
            with pe.Fori(1, PAIRS - 1) as j:
                for u in range(2):
                    tile(2 * j + u, u, j=j)
            tile(TILES - 2, 0, j=PAIRS - 1)
            tile(TILES - 1, 1, j=PAIRS - 1, last=True)
            late_query(TILES - 1)
            late_route(TILES - 1, False)
            late_turn_w(TILES - 1)
            late_z(TILES - 1, more=False)

        @block.scalar
        def _(act):
            def centre(t, u, j):
                act.wait_ge(S["mean_var"], t + 1)
                act.activation(x[u][:], x[u][:], ACT.Identity, bias=nmean[u][:, 0:1]).then_inc(S["centred"], 1)

            def x_hi(t, u, g):
                act.wait_ge(S["turned"], G * t + g + 1)
                act.activation(xT[u][0][:, 4 * g:4 * g + 4, :], bank[g % 2][:].rearrange("p (k n) -> p k n", k=4),
                               ACT.Copy).then_inc(S["x_hi"], 1)

            def soft(t, u):
                act.wait_ge(S["neg_scores"], t + 1)
                act.activation(e1[:], neg_s[:], ACT.Exp, bias=neg_max[:, 0:1], scale=-1.0,
                               accum_out=esum[:]).then_inc(S["exp"], 1)

            def late_square(t):
                act.wait_ge(S["hidden"], t + 1)
                act.activation(act1[:], hid[:], ACT.Square).then_inc(S["square"], 1)

            def late_q_hi(t, first):
                act.wait_ge(S["q_turned"], t + 1)
                if not first:
                    act.wait_ge(S["routed"], t)
                act.activation(qS[:], q_turned_ps, ACT.Copy)
                act.activation(q2s[0:BOT, :], q_turned_ps[0:BOT, :], ACT.Copy).then_inc(S["q_hi"], 1)

            def att_hi(t):
                act.wait_ge(S["att_turned"], t + 1)
                act.activation(attS[:], att_turned_ps, ACT.Copy).then_inc(S["att_hi"], 1)

            def late_exp(t):
                act.wait_ge(S["slots"], t + 1)
                act.activation(ws[:], ws[:], ACT.Exp, bias=wneg[:, 0:1], accum_out=wsum[:]).then_inc(S["slot_exp"], 1)

            def late_w_out(t, first):
                act.wait_ge(S["w_turned"], t + 1)
                if not first:
                    act.wait_ge(S["z_sum"], t)
                act.activation(wT[:], psR[:], ACT.Copy).then_inc(S["w_out"], 1)

            def late_tanh(t):
                act.wait_ge(S["inner"], t + 1)
                act.activation(act1[:], act1[:], ACT.Tanh, scale=0.7978845608028654).then_inc(S["tanh"], 1)

            def tile(t, u, late=True, late_first=False, last=False, ahead=True, j=None):
                if late:
                    late_square(t - 1)
                soft(t, u)
                if late:
                    late_q_hi(t - 1, late_first)
                if not last:
                    x_hi(t + 1, 1 - u, 0)
                if late:
                    late_tanh(t - 1)
                if not last:
                    x_hi(t + 1, 1 - u, 1)
                att_hi(t)
                if late:
                    late_exp(t - 1)
                if not last:
                    x_hi(t + 1, 1 - u, 2)
                if late:
                    late_w_out(t - 1, late_first)
                if not last:
                    x_hi(t + 1, 1 - u, 3)
                if ahead:
                    centre(t + 2, u, j)

            for t in range(2):
                centre(t, t, 0)
            for g in range(G):
                x_hi(0, 0, g)
            tile(0, 0, late=False, j=0)
            tile(1, 1, late_first=True, j=0)
            with act.Fori(1, PAIRS - 1) as j:
                for u in range(2):
                    tile(2 * j + u, u, j=j)
            tile(TILES - 2, 0, ahead=False)
            tile(TILES - 1, 1, last=True, ahead=False)
            t = TILES - 1
            late_square(t)
            late_q_hi(t, False)
            late_tanh(t)
            late_exp(t)
            late_w_out(t, False)

        @block.gpsimd
        def _(pool):
            def power(out, in_, tmp):
                pool.tensor_tensor(tmp, in_, keep["eps"][:], ALU.add)
                pool.drain()
                return pool.tensor_tensor(out, tmp, keep["minus_half"][:], ALU.pow)

            def first_rstd(t, u):
                pool.drain()
                pool.wait_ge(S["mean_var"], t + 1)
                power(rstd1[u][:], mv[u][:, 1:2], ve1[:]).then_inc(S["rstd1"], 1)

            def late(t, u):
                pool.drain()
                pool.wait_ge(S["var1"], t + 1)
                power(st2[u][:, 2:3], st2[u][:, 1:2], ve[:]).then_inc(S["rstd2"], 1)
                pool.wait_ge(S["hidden"], t + 1)
                if not (isinstance(t, int) and t == 0):
                    pool.wait_ge(S["learned"], t)
                pool.tensor_tensor(hw[:], hid[:], keep["wu2"][:], ALU.mult).then_inc(S["hw"], 1)
                pool.wait_ge(S["poly"], t + 1)
                pool.tensor_tensor(act1[:], act1[:], hid[:], ALU.mult).then_inc(S["inner"], 1)
                pool.wait_ge(S["learned"], t + 1)
                pool.tensor_copy(keep["stats"][:, bass.ds(t, 1), :].rearrange("p o n -> p (o n)"),
                                 st2[u][:]).then_inc(S["kept_stats"], 1)

            def keep_att(t, u):
                pool.wait_ge(S["att"], t + 1)
                pool.tensor_copy(keep["att"][:, bass.ds(t, 1), :].rearrange("p o n -> p (o n)"),
                                 att2[u][:, 0:NCTX]).then_inc(S["kept_att"], 1)

            pool.memset(keep["minus_half"][:], -0.5)
            pool.memset(keep["eps"][:], EPS).then_inc(S["kept_stats"], 1)
            pool.drain()
            for t in range(2):
                first_rstd(t, t)
            keep_att(0, 0)
            first_rstd(2, 0)
            late(0, 0)
            keep_att(1, 1)
            first_rstd(3, 1)
            with pool.Fori(1, PAIRS - 1) as j:
                for u in range(2):
                    t = 2 * j + u
                    late(t - 1, 1 - u)
                    keep_att(t, u)
                    first_rstd(t + 2, u)
            for t in (TILES - 2, TILES - 1):
                late(t - 1, 1 - t % 2)
                keep_att(t, t % 2)
            late(TILES - 1, 1)

        @block.vector
        def _(dve):
            def moments(t, u, j):
                dve.wait_ge(x_in[u], 16 * j + 16)
                for k in range(4):
                    dve.bn_stats(stats[:, k, :], x[u][:, k * QN:(k + 1) * QN])
                dve.drain()
                dve.bn_aggr(mv[u][:], stats[:])
                dve.drain()
                dve.tensor_scalar(nmean[u][:], mv[u][:, 0:1], -1.0, None, ALU.mult).then_inc(S["mean_var"], 1)

            def x_lo(t, u, g):
                dve.wait_ge(S["x_hi"], G * t + g + 1)
                dve.tensor_tensor(xT[u][1][:, 4 * g:4 * g + 4, :], bank[g % 2][:].rearrange("p (k n) -> p k n", k=4),
                                  f32(xT[u][0][:, 4 * g:4 * g + 4, :]), ALU.subtract).then_inc(S["x_lo"], 1)

            def soft_scores(t, u, row):
                dve.wait_ge(S["rstd1"], t + 1)
                dve.tensor_scalar(nscale[:], rstd1[u][:], -ATT_SCALE, None, ALU.mult)
                dve.tensor_copy(mvk[u][:], mv[u][:])
                dve.drain()
                dve.wait_ge(S["b_sum"], t + 1)
                dve.scalar_tensor_tensor(neg_s[:], psB[u][:, 0:NCTX], nscale[:, 0:1], at(keep["bq_rows"], row),
                                         ALU.mult, ALU.subtract)
                dve.drain()
                dve.tensor_reduce(neg_max[:], neg_s[:], AX.X, ALU.min).then_inc(S["neg_scores"], 1)

            def soft_att(t, u, first):
                dve.wait_ge(S["exp"], t + 1)
                dve.reciprocal(einv[:], esum[:])
                dve.drain()
                if not first:
                    dve.wait_ge(S["kept_att"], t - 1)
                dve.tensor_scalar(att2[u][:, 0:NCTX], e1[:], einv[:, 0:1], None, ALU.mult)
                dve.tensor_scalar(att2[u][:, NCTX:2 * NCTX], e1[:], einv[:, 0:1], None,
                                  ALU.mult).then_inc(S["att"], 1)

            def att_lo(t):
                dve.wait_ge(S["att_hi"], t + 1)
                dve.tensor_tensor(attS[NCTX:P, :], att_turned_ps[NCTX:P, :], f32(attS[NCTX:P, :]),
                                  ALU.subtract).then_inc(S["att_lo"], 1)

            def late_stats(t, u, row, first):
                dve.wait_ge(S["c_sum"], t + 1)
                if not first:
                    dve.wait_ge(S["kept_stats"], t)
                dve.tensor_tensor_reduce(junk[:], psB[u][:, NCTX:2 * NCTX], att2[u][:, 0:NCTX],
                                         keep["cov_scale"][:, 0:1], mvk[u][:, 1:2],
                                         ALU.mult, ALU.add, st2[u][:, 1:2]).then_inc(S["var1"], 1)
                dve.scalar_tensor_tensor(junk2[:], att2[u][:, 0:NCTX], 1.0, at(keep["mu_rows"], row),
                                         ALU.mult, ALU.mult, accum_out=shift[:])
                dve.drain()
                dve.tensor_tensor(st2[u][:, 0:1], shift[:], mvk[u][:, 0:1], ALU.add)

            def late_scale(t, u):
                dve.wait_ge(S["rstd2"], t + 1)
                dve.tensor_scalar(q2[:, 0:BOT], psB[u][:, 2 * NCTX:BW], st2[u][:, 2:3], None, ALU.mult)
                dve.tensor_scalar(q2[:, BOT:2 * BOT], psB[u][:, 2 * NCTX:BW], st2[u][:, 2:3], None,
                                  ALU.mult).then_inc(S["query"], 1)
                dve.scalar_tensor_tensor(hid[:], psA[:], st2[u][:, 2:3], keep["bu1"][:], ALU.mult,
                                         ALU.add).then_inc(S["hidden"], 1)

            def late_q_lo(t):
                dve.wait_ge(S["q_hi"], t + 1)
                dve.tensor_tensor(qS[BOT:P, :], q_turned_ps[BOT:P, :], f32(qS[BOT:P, :]),
                                  ALU.subtract).then_inc(S["q_lo"], 1)

            def late_poly(t):
                dve.wait_ge(S["square"], t + 1)
                dve.tensor_scalar(act1[:], act1[:], 0.044715, 1.0, ALU.mult, ALU.add).then_inc(S["poly"], 1)

            def late_slots(t):
                dve.wait_ge(S["routed"], t + 1)
                dve.memset(wmax[:], OUT_OF_RANGE)
                dve.max(top8[:], psR[:])
                dve.drain()
                dve.match_replace(picked[:], top8[:], psR[:], PICKED)
                dve.drain()
                dve.tensor_scalar(picked[:], picked[:], PICKED, OUT_OF_RANGE, ALU.is_lt, ALU.mult)
                dve.drain()
                dve.tensor_tensor_reduce(ws[:], psS[:], picked[:], 1.0, -3.0e38, ALU.add, ALU.max, wmax[:])
                dve.drain()
                dve.tensor_scalar(wneg[:], wmax[:], -1.0, None, ALU.mult).then_inc(S["slots"], 1)

            def late_learned(t, u):
                dve.wait_ge(S["tanh"], t + 1)
                dve.wait_ge(S["hw"], t + 1)
                dve.scalar_tensor_tensor(act1[:], act1[:], 1.0, hw[:], ALU.add, ALU.mult,
                                         accum_out=st2[u][:, 3:4]).then_inc(S["learned"], 1)

            def late_z(t):
                dve.wait_ge(S["slot_exp"], t + 1)
                dve.reciprocal(winv[:], wsum[:])
                dve.drain()
                dve.wait_ge(S["z_sum"], t + 1)
                dve.tensor_scalar(keep["z"][:, bass.ds(t, 1), :].rearrange("p o n -> p (o n)"), z_ps,
                                  winv[:, 0:1], None, ALU.mult).then_inc(S["z_out"], 1)

            def tile(t, u, row, late=True, last=False, ahead=True, first=False, second=False, j=None):
                if late:
                    prev = row if u else row - 1
                    late_stats(t - 1, 1 - u, prev, second)
                    late_scale(t - 1, 1 - u)
                soft_scores(t, u, row)
                if late:
                    late_q_lo(t - 1)
                    late_poly(t - 1)
                soft_att(t, u, first or second)
                if not last:
                    x_lo(t + 1, 1 - u, 0)
                if late:
                    late_slots(t - 1)
                if not last:
                    x_lo(t + 1, 1 - u, 1)
                att_lo(t)
                if not last:
                    x_lo(t + 1, 1 - u, 2)
                if late:
                    late_learned(t - 1, 1 - u)
                if not last:
                    x_lo(t + 1, 1 - u, 3)
                if late:
                    late_z(t - 1)
                if ahead:
                    moments(t + 2, u, j + 1)

            dve.tensor_scalar(keep["cov_scale"][:], keep["tgx"][:], 2.0 / D, None, ALU.mult)
            for t in range(2):
                moments(t, t, 0)
            for g in range(G):
                x_lo(0, 0, g)
            tile(0, 0, 0, late=False, first=True, j=0)
            tile(1, 1, 0, second=True, j=0)
            with dve.Fori(1, PAIRS - 1) as j:
                for u in range(2):
                    tile(2 * j + u, u, j, j=j)
            tile(TILES - 2, 0, PAIRS - 1, ahead=False)
            tile(TILES - 1, 1, PAIRS - 1, ahead=False, last=True)
            t, u, row = TILES - 1, 1, PAIRS - 1
            late_stats(t, u, row, False)
            late_scale(t, u)
            late_q_lo(t)
            late_poly(t)
            late_slots(t)
            late_learned(t, u)
            late_z(t)


def gate_block(nc, keep):
    with ExitStack() as ctx:
        m = Memory(nc, ctx, "gt")
        st, tgx, tgf = keep["stats"], keep["tgx"], keep["tgf"]
        mean, var, rstd, learned = (st[:, :, k] for k in range(4))
        t = {n: m.sb(n, [P, TILES]) for n in ("ve", "ratio", "one_plus", "flat", "dist", "log", "th", "u", "gate")}
        total, rowsum, half_bu2, half_gb = (m.sb("mean_log", [P, 1]), m.sb("row_sum", [P, 1]),
                                            m.sb("half_bu2", [P, 1]), m.sb("half_bias", [P, 1]))
        ps = m.ps("total")
        ready, logged, summed, unit, squashed, gated = (m.sem("ready"), m.sem("logged"), m.sem("summed"),
                                                        m.sem("unit"), m.sem("squashed"), m.sem("gated"))
        all_summed = m.sem("all_summed")
        block = ctx.enter_context(nc.Block())

        @block.vector
        def _(dve):
            def op(f, *args, **kw):
                ins = f(*args, **kw)
                dve.drain()
                return ins

            op(dve.tensor_scalar, half_bu2[:], keep["bu2"][:], 0.5, None, ALU.mult)
            op(dve.tensor_scalar, half_gb[:], keep["gb"][:], 0.5, None, ALU.mult)
            op(dve.tensor_scalar, t["ve"][:], var, EPS, None, ALU.add)
            op(dve.reciprocal, t["ve"][:], t["ve"][:])
            op(dve.tensor_tensor, t["ratio"][:], t["ve"][:], var, ALU.mult)
            dve.tensor_scalar(t["one_plus"][:], t["ratio"][:], 1.0, None, ALU.add).then_inc(ready, 1)
            dve.drain()
            op(dve.tensor_scalar, t["dist"][:], t["one_plus"][:], 1.0, None, ALU.subtract)
            op(dve.tensor_scalar, t["flat"][:], t["dist"][:], 0.0, None, ALU.is_equal)
            op(dve.tensor_tensor, t["dist"][:], t["dist"][:], t["flat"][:], ALU.add)
            op(dve.reciprocal, t["dist"][:], t["dist"][:])
            op(dve.tensor_tensor, t["ratio"][:], t["ratio"][:], t["dist"][:], ALU.mult)
            dve.wait_ge(logged, 1)
            op(dve.tensor_tensor, t["log"][:], t["log"][:], t["flat"][:], ALU.add)
            op(dve.tensor_tensor, t["log"][:], t["log"][:], t["ratio"][:], ALU.mult)
            dve.tensor_reduce(rowsum[:], t["log"][:], AX.X, ALU.add).then_inc(summed, 1)
            dve.wait_ge(all_summed, 1)
            op(dve.tensor_scalar, total[:], ps[:, 0:1], 1.0 / (TILES * P), 1.0e-6, ALU.mult, ALU.add)
            op(dve.reciprocal, total[:], total[:])
            op(dve.tensor_scalar, t["log"][:], t["log"][:], total[:, 0:1], 0.5, ALU.mult, ALU.mult)
            dve.wait_ge(unit, 1)
            op(dve.tensor_scalar, t["u"][:], t["th"][:], 1.25, 1.25, ALU.mult, ALU.add)
            op(dve.tensor_tensor, t["u"][:], t["u"][:], t["log"][:], ALU.add)
            op(dve.tensor_scalar, t["u"][:], t["u"][:], 0.0, 5.0, ALU.max, ALU.min)
            op(dve.tensor_scalar, t["u"][:], t["u"][:], -TAU_LOW, 1.0 / (TAU_HIGH - TAU_LOW), ALU.add, ALU.mult)
            op(dve.tensor_scalar, t["u"][:], t["u"][:], 0.0, 1.0, ALU.max, ALU.min)
            dve.tensor_scalar(t["u"][:], t["u"][:], keep["w1"][:, 0:1], keep["gb"][:, 0:1], ALU.mult,
                              ALU.add).then_inc(squashed, 1)
            dve.wait_ge(gated, 1)
            op(dve.tensor_scalar, t["gate"][:], t["gate"][:], 0.5, 0.5, ALU.mult, ALU.add)
            op(dve.tensor_scalar, t["u"][:], t["gate"][:], EARLY_EXIT, None, ALU.is_ge)
            op(dve.tensor_tensor, t["gate"][:], t["gate"][:], t["u"][:], ALU.mult)
            op(dve.tensor_scalar, keep["f_z"][:], t["gate"][:], tgf[:, 0:1], None, ALU.mult)
            op(dve.tensor_scalar, t["u"][:], rstd, tgf[:, 0:1], None, ALU.mult)
            op(dve.tensor_scalar, keep["f_x"][:], t["u"][:], 1.0, None, ALU.add)
            op(dve.tensor_tensor, t["u"][:], t["u"][:], mean, ALU.mult)
            op(dve.tensor_scalar, keep["f_0"][:], t["u"][:], -1.0, None, ALU.mult)
            op(dve.tensor_scalar, keep["f_att"][:], keep["f_x"][:], tgx[:, 0:1], None, ALU.mult)

        @block.scalar
        def _(act):
            act.wait_ge(ready, 1)
            act.activation(t["log"][:], t["one_plus"][:], ACT.Ln).then_inc(logged, 1)
            act.activation(t["th"][:], learned, ACT.Tanh, bias=half_bu2[:, 0:1], scale=0.5).then_inc(unit, 1)
            act.wait_ge(squashed, 1)
            act.activation(t["gate"][:], t["u"][:], ACT.Tanh, scale=0.5).then_inc(gated, 1)

        @block.tensor
        def _(pe):
            pe.wait_ge(summed, 1)
            pe.matmul(ps[:, 0:1], keep["ones"][:], rowsum[:], start=True, stop=True).then_inc(all_summed, 1)


def output_block(nc, io, scr, keep):
    with ExitStack() as ctx:
        m = Memory(nc, ctx, "ob")
        ident = keep["ident"]
        ctx1, ctx2 = m.sb("ctx_stack", [P, BATCH, D], F32R), m.sb("ctx_low", [NCTX, BATCH, D], F32R)
        wvu = [m.sb(f"wvu{i}", [P, D], F32R) for i in range(2)]
        RING = 4
        x = [m.sb(f"x{s}", [P, D]) for s in range(RING)]
        az = [m.sb(f"att_z{u}", [P, 2 * P]) for u in range(2)]
        azT = [m.sb(f"att_z_turned{u}", [P, 2 * P], F32R) for u in range(2)]
        zl = [m.sb(f"z_low{u}", [P, P], F32R) for u in range(2)]
        turn_ps = [m.ps(f"turned{u}") for u in range(2)]
        po = [m.ps(f"out{n}") for n in range(4)]
        w_in = m.sem("weights_in")
        ctx_in = [m.sem(f"ctx_in{b}") for b in range(BATCH)]
        x_in = [m.sem(f"x_in{s}") for s in range(RING)]
        stored = [m.sem(f"stored{s}") for s in range(RING)]
        S = {n: m.sem(n) for n in ("scaled", "turned", "hi", "lo", "affine", "summed", "added")}
        block = ctx.enter_context(nc.Block())
        xin = io["x"].rearrange("(t p) d -> t p d", p=P)
        xout = io["out"].rearrange("(t p) d -> t p d", p=P)
        LAST = TILES // RING - 1

        @block.sync
        def _(sp):
            def load(t, s):
                sp.dma_start(x[s][:], xin[bass.ds(t, 1)].rearrange("o p d -> p (o d)")).then_inc(x_in[s], 16)

            def load_ctx(b):
                for half in range(2):
                    sp.dma_start(f32(ctx1[half * NCTX:(half + 1) * NCTX, b, :]),
                                 scr["ctx"][0, b * NCTX:(b + 1) * NCTX, :]).then_inc(ctx_in[b], 16)
                sp.dma_start(f32(ctx2[:, b, :]), scr["ctx"][1, b * NCTX:(b + 1) * NCTX, :]).then_inc(ctx_in[b], 16)

            load_ctx(0)
            for i in range(2):
                sp.dma_start(f32(wvu[i][:]), scr["wvu"][i]).then_inc(w_in, 16)
            for s in range(RING):
                load(s, s)
            for b in range(1, BATCH):
                load_ctx(b)
            with sp.Fori(1, LAST + 1) as j:
                for s in range(RING):
                    sp.wait_ge(stored[s], 16 * j)
                    load(RING * j + s, s)

        @block.tensor
        def _(pe):
            def turn(t, u):
                pe.wait_ge(S["scaled"], t + 1)
                pe.transpose(turn_ps[u][:, 0:P], az[u][:, 0:P], ident[:])
                pe.transpose(turn_ps[u][:, P:2 * P], az[u][:, P:2 * P], ident[:]).then_inc(S["turned"], 1)

            def chunk(t, u, n, b, first):
                if not first:
                    pe.wait_ge(S["added"], 4 * t + n - 3)
                cols = slice(n * QN, (n + 1) * QN)
                c1 = ctx1[:, bass.ds(b, 1), cols].rearrange("p o n -> p (o n)")
                c2 = ctx2[:, bass.ds(b, 1), cols].rearrange("p o n -> p (o n)")
                pe.matmul(po[n][:], azT[u][:, 0:P], c1, start=True, stop=False)
                pe.matmul(po[n][:], azT[u][0:NCTX, 0:P], c2, start=False, stop=False)
                split_product(pe, po[n][:], (azT[u][:, P:2 * P], zl[u][:]), (wvu[0][:, cols], wvu[1][:, cols]),
                              False, True).then_inc(S["summed"], 1)

            def body(j, first=False, last=False):
                for s in range(RING):
                    t, u = RING * j + s, s % 2
                    pe.wait_ge(S["lo"], t + 1)
                    for n in range(4):
                        chunk(t, u, n, j // 2, first and s == 0)
                        if n == 1 and not (last and s == RING - 1):
                            turn(t + 1, 1 - u)

            pe.wait_ge(w_in, 32)
            pe.wait_ge(ctx_in[0], 48)
            turn(0, 0)
            body(0, first=True)
            for b in range(1, BATCH):
                pe.wait_ge(ctx_in[b], 48)
            with pe.Fori(1, LAST) as j:
                body(j)
            body(LAST, last=True)

        @block.scalar
        def _(act):
            def hi(t, u):
                act.wait_ge(S["turned"], t + 1)
                act.activation(azT[u][:], turn_ps[u][:, 0:2 * P], ACT.Copy).then_inc(S["hi"], 1)

            def affine(t, s, j):
                act.wait_ge(x_in[s], 16 * j + 16)
                act.activation(x[s][:], x[s][:], ACT.Identity, bias=keep["f_0"][:, bass.ds(t, 1)],
                               scale=keep["f_x"][:, bass.ds(t, 1)]).then_inc(S["affine"], 1)

            def store(t, s):
                act.wait_ge(S["added"], 4 * t + 4)
                act.dma_start(xout[bass.ds(t, 1)].rearrange("o p d -> p (o d)"), x[s][:]).then_inc(stored[s], 16)

            def body(j, last=False):
                for s in range(RING):
                    t = RING * j + s
                    if not (last and s == RING - 1):
                        hi(t + 1, 1 - s % 2)
                        affine(t + 1, (s + 1) % RING, j + (s + 1) // RING)
                    store(t, s)

            hi(0, 0)
            affine(0, 0, 0)
            with act.Fori(0, LAST) as j:
                body(j)
            body(LAST, last=True)
            for s in range(RING):
                act.wait_ge(stored[s], 16 * (LAST + 1))

        @block.vector
        def _(dve):
            def scale(t, u):
                f_att, f_z = keep["f_att"][:, bass.ds(t, 1)], keep["f_z"][:, bass.ds(t, 1)]
                for half in range(2):
                    dve.tensor_scalar(az[u][:, half * NCTX:(half + 1) * NCTX], at(keep["att"], t), f_att, None,
                                      ALU.mult)
                dve.tensor_scalar(az[u][:, P:2 * P], at(keep["z"], t), f_z, None, ALU.mult).then_inc(S["scaled"], 1)

            def lo(t, u):
                dve.wait_ge(S["hi"], t + 1)
                dve.tensor_tensor(azT[u][NCTX:P, 0:P], turn_ps[u][NCTX:P, 0:P], f32(azT[u][NCTX:P, 0:P]),
                                  ALU.subtract)
                dve.tensor_tensor(zl[u][:], turn_ps[u][:, P:2 * P], f32(azT[u][:, P:2 * P]),
                                  ALU.subtract).then_inc(S["lo"], 1)

            def add(t, s, n):
                dve.wait_ge(S["summed"], 4 * t + n + 1)
                if n == 0:
                    dve.wait_ge(S["affine"], t + 1)
                cols = slice(n * QN, (n + 1) * QN)
                dve.tensor_tensor(x[s][:, cols], x[s][:, cols], po[n][:], ALU.add).then_inc(S["added"], 1)

            def body(j, last=False):
                for s in range(RING):
                    t, ahead = RING * j + s, not (last and s == RING - 1)
                    if ahead:
                        scale(t + 1, 1 - s % 2)
                    add(t, s, 0)
                    add(t, s, 1)
                    if ahead:
                        lo(t + 1, 1 - s % 2)
                    add(t, s, 2)
                    add(t, s, 3)

            scale(0, 0)
            lo(0, 0)
            with dve.Fori(0, LAST) as j:
                body(j)
            body(LAST, last=True)


def gated_cross_attention_and_memory(nc, io):
    scr = {
        "x": nc.dram_tensor("scratch_b", [BATCH, 2, P, KC, 2 * NCTX], F32).ap(),
        "cw": nc.dram_tensor("scratch_cw", [2, CR, CWN], F32).ap(),
        "ctx": nc.dram_tensor("scratch_ctx", [2, CR, D], F32).ap(),
        "wvu": nc.dram_tensor("scratch_wvu", [2, P, D], F32).ap(),
    }
    with ExitStack() as outer:
        m = Memory(nc, outer, "k")
        keep = {
            "ident": m.sb("ident", [P, P]), "ones": m.sb("ones", [P, P]),
            "mu_rows": m.sb("mu_rows", [P, PAIRS, NCTX]), "bq_rows": m.sb("bq_rows", [P, PAIRS, NCTX]),
            "bias_cols": m.sb("bias_cols", [P, 2 * KC]),
            "stats": m.sb("stats", [P, TILES, 4]),
            "att": m.sb("att", [P, TILES, NCTX]), "z": m.sb("z", [P, TILES, VB]),
        }
        for n in ("tgx", "tgf", "w1", "gb", "bu2", "minus_half", "eps", "cov_scale"):
            keep[n] = m.sb(n, [P, 1])
        for n in ("f_x", "f_0", "f_att", "f_z"):
            keep[n] = m.sb(n, [P, TILES])
        with ExitStack() as first:
            m = Memory(nc, first, "a")
            keep["rows"] = [m.sb(f"rows{u}", [P, D]) for u in range(2)]
            for n, shape in (("ctxT", [P, KC, CR]), ("KT", [P, KC, CR])):
                keep[n] = [m.sb(f"{n}{i}", shape, F32R) for i in range(2)]
            keep["T"] = [[m.sb(f"T{u}{i}", [P, KC, P], F32R) for i in range(2)] for u in range(2)]
            context_block(nc, m, io, scr, keep)
            keys_block(nc, io, keep)
            score_weights_block(nc, io, scr, keep)
        with ExitStack() as second:
            m = Memory(nc, second, "b")
            keep["bw"] = [m.sb(f"b_weights{i}", [P, KC, BW], F32R) for i in range(2)]
            keep["wu"] = [m.sb(f"wu{i}", [P, KC, HU], F32R) for i in range(2)]
            keep["rs1"], keep["rs2"] = m.sb("slots_hi", [P, 2 * NSLOT], F32R), m.sb("slots_lo", [BOT + 2, 2 * NSLOT], F32R)
            keep["q2s"] = m.sb("query_ones", [BOT + 2, P], F32R)
            keep["av"] = m.sb("av", [P, 4, VB])
            keep["bu1"], keep["wu2"] = m.sb("bu1", [P, HU]), m.sb("wu2", [P, HU])
            with ExitStack() as third:
                keep["ak2"] = Memory(nc, third, "c").sb("aux_keys_twice", [P, 4, P])
                ffn_block(nc, io, scr, keep)
            context_weights_block(nc, io, scr, keep)
            token_block(nc, io, scr, keep)
        gate_block(nc, keep)
        output_block(nc, io, scr, keep)


_INS = {"x": "x", "ctx_4096": "ctx", "g_xattn": "g_xattn", "g_ffn": "g_ffn", "L0_xattn_Wq": "Wq",
        "L0_xattn_bq": "bq", "L0_xattn_Wk": "Wk", "L0_xattn_bk": "bk", "L0_ffn_Wq": "fWq", "L0_ffn_Wr": "Wr",
        "L0_ffn_aux_keys": "aux_keys", "L0_ffn_aux_values": "aux_values", "L0_ffn_Wvd": "Wvd",
        "L0_ffn_Wvu": "Wvu", "L0_ffn_Wu1": "Wu1", "L0_ffn_bu1": "bu1", "L0_ffn_Wu2": "wu2",
        "L0_ffn_bu2": "bu2", "L0_ffn_gate_w1": "gate_w1", "L0_ffn_gate_bias": "gate_bias",
        "L0_ffn_log_rel": "log_rel"}
_SHAPES = {"x": (BATCH * SEQ, D), "ctx": (CR, D), "g_xattn": (1, 1), "g_ffn": (1, 1), "bu2": (1, 1),
           "gate_w1": (1, 1), "gate_bias": (1, 1), "wu2": (HU,)}


def kernel(**inputs):
    import numpy as _np
    import concourse.bacc as _bacc
    from concourse import mybir as _mybir
    from concourse.bass_utils import run_bass_kernel_spmd as _run

    nc = _bacc.Bacc("TRN2", target_bir_lowering=False, num_devices=1)
    arrays, io = {}, {}
    for name, short in _INS.items():
        a = _np.ascontiguousarray(inputs[name])
        if short in _SHAPES:
            a = a.reshape(_SHAPES[short])
        arrays[f"in_{short}_dram"] = a
        io[short] = nc.dram_tensor(f"in_{short}_dram", a.shape, _mybir.dt.from_np(a.dtype), kind="ExternalInput").ap()
    io["out"] = nc.dram_tensor("out_0_dram", (BATCH * SEQ, D), F32, kind="ExternalOutput").ap()
    gated_cross_attention_and_memory(nc, io)
    r = _run(nc, [arrays], core_ids=[0])
    return r.results[0]["out_0_dram"].reshape(BATCH, SEQ, D)
```

```python
from contextlib import ExitStack

import concourse.bass as bass
from concourse import mybir

P = 128
D = 2048
KC = D // P
BATCH, SEQ, NCTX = 4, 1024, 64
TILES = BATCH * SEQ // P
PAIRS = TILES // 2
CR = BATCH * NCTX
HU = 512
BOT, RDIM, NSLOT, VB, TOPK = 64, 48, 512, 128, 8
QN = 512
GROUPS = KC // 4
UA = 128
UB = HU - UA
QC = 2 * NCTX
BW = QC + BOT + UA
CWN = NCTX + BOT + HU
EPS = 1e-5
TAU_LOW, TAU_HIGH, EARLY_EXIT = 0.5, 2.0, 0.05
ATT_SCALE = 1.0 / float(D) ** 0.5
OUT_OF_RANGE = -1.0e30
PICKED = 1.0e30

ALU = mybir.AluOpType
ACT = mybir.ActivationFunctionType
AX = mybir.AxisListType
F32 = mybir.dt.float32
F32R = mybir.dt.float32r


def f32(ap):
    return ap.bitcast(F32)


def split_product(pe, out, left, right, start, stop, skip=False):
    (lh, ll), (rh, rl) = left, right
    pe.matmul(out, lh, rh, start=start, stop=False, skip_group_check=skip)
    pe.matmul(out, lh, rl, start=False, stop=False, skip_group_check=skip)
    return pe.matmul(out, ll, rh, start=False, stop=stop, skip_group_check=skip)


def at(t, i):
    return t[:, bass.ds(i, 1), :].rearrange("p o n -> p (o n)")


class Memory:

    def __init__(self, nc, ctx, tag):
        self.nc, self.ctx, self.tag = nc, ctx, tag

    def sb(self, name, shape, dt=F32):
        return self.ctx.enter_context(self.nc.sbuf_tensor(f"{self.tag}_{name}", shape, dt))

    def ps(self, name, shape=(P, QN), dt=F32):
        return self.ctx.enter_context(self.nc.psum_tensor(f"{self.tag}_{name}", list(shape), dt))

    def sem(self, name):
        return self.ctx.enter_context(self.nc.semaphore(f"{self.tag}_{name}"))


def transpose_group(pe, bank, src, g, ident, rows=P):
    for k in range(4):
        c = 4 * g + k
        ins = pe.transpose(bank[:, k * rows:(k + 1) * rows], src[0:rows, c * P:(c + 1) * P],
                           ident[0:rows, 0:rows])
    return ins


def keys_block(nc, io, scr, keep):
    with ExitStack() as ctx:
        m = Memory(nc, ctx, "ky")
        rows, T, ctxT, KT = keep["rows"], keep["T"], keep["ctxT"], keep["KT"]
        ident, ones, bias = keep["ident"], keep["ones"], keep["bias_cols"]
        crow, chi = keep["ctx_rows"], keep["ctx_hi"]
        raw = m.sb("bias_rows", [2 * KC, P])
        stats = [m.sb(f"stats{r}", [P, 4, 6]) for r in range(2)]
        mv = [m.sb(f"mv{r}", [P, 2]) for r in range(2)]
        diag = [m.sb(f"diag{r}", [P, P]) for r in range(2)]
        kf = [m.sb(f"key_f32_{u}", [P, CR]) for u in range(2)]
        dot = m.sb("bq_dot", [P, CR])
        bank = [m.ps(f"bank{i}") for i in range(2)]
        kp = [m.ps(f"keys{u}") for u in range(2)]
        ps_row, ps_mu, ps_bias = m.ps("bq_row"), m.ps("mu"), m.ps("bias")
        ctx_in = [m.sem(f"ctx_in{r}") for r in range(2)]
        small_in, ident_zero, ident_done = m.sem("small_in"), m.sem("ident_zero"), m.sem("ident_done")
        diag_done, mu_ready, bias_turned = m.sem("diag_done"), m.sem("mu_ready"), m.sem("bias_turned")
        bias_done = m.sem("bias_done")
        gates_ready, ctx_high, ctx_low = m.sem("gates_ready"), m.sem("ctx_high"), m.sem("ctx_low")
        rows_in = [m.sem(f"rows_in{u}") for u in range(2)]
        next_in = keep["wq_in"]
        turned, hi_done, lo_done = m.sem("turned"), m.sem("hi_done"), m.sem("lo_done")
        product, biased, key_hi, key_lo = m.sem("product"), m.sem("biased"), m.sem("key_hi"), m.sem("key_lo")
        dot_done, row_done = m.sem("dot_done"), m.sem("row_done")
        block = ctx.enter_context(nc.Block())
        wk = io["Wk"].rearrange("(t p) d -> t p d", p=P)
        C = 2 * GROUPS

        def load(sp, n, u):
            sp.dma_start(rows[u][:], wk[bass.ds(n, 1)].rearrange("o p d -> p (o d)")).then_inc(rows_in[u], 16)

        @block.sync
        def _(sp):
            for r in range(2):
                sp.dma_start(crow[r][:], io["ctx"][r * P:(r + 1) * P, :]).then_inc(ctx_in[r], 16)
            for u in range(2):
                load(sp, u, u)
            sp.dma_start(raw[0:KC, :], io["bk"].rearrange("(c p) -> c p", p=P)).then_inc(small_in, 16)
            sp.dma_start(raw[KC:2 * KC, :], io["bq"].rearrange("(c p) -> c p", p=P)).then_inc(small_in, 16)
            for dst, src in (("tgx", "g_xattn"), ("tgf", "g_ffn"), ("w1", "gate_w1"), ("gb", "gate_bias"),
                             ("bu2", "bu2")):
                sp.dma_start(keep[dst][:], io[src].broadcast_to([P, 1])).then_inc(small_in, 16)
            with sp.Fori(1, KC // 2) as j:
                for u in range(2):
                    sp.wait_ge(turned, C + GROUPS * (2 * j + u - 1))
                    load(sp, 2 * j + u, u)
            for u in range(2):
                sp.wait_ge(turned, C + GROUPS * (KC + u - 1))
                load_wq(sp, io, rows, next_in, u, u)

        @block.gpsimd
        def _(pool):
            pool.memset(ident[:], 0.0).then_inc(ident_zero, 1)
            pool.memset(ones[:], 1.0).then_inc(ident_done, 1)
            pool.wait_ge(ident_zero, 1)
            pool.affine_select(out=ident[:], in_=ident[:], compare_op=ALU.not_equal, fill=1.0, base=0,
                               pattern=[[-1, P]], channel_multiplier=1).then_inc(ident_done, 1)
            for r in range(2):
                pool.wait_ge(ctx_high, r + 1)
                pool.tensor_tensor(crow[r][:], crow[r][:], f32(chi[r][:]), ALU.subtract).then_inc(ctx_low, 1)
                pool.wait_ge(ctx_low, r + 1)
                for part, src in ((0, f32(chi[r][:])), (1, crow[r][:])):
                    pool.dma_start(scr["ctx"][part, r * P:(r + 1) * P, :], src).then_inc(keep["ctx_stored"], 16)

        @block.tensor
        def _(pe):
            pe.wait_ge(ident_done, 2)
            for n in range(C):
                if n % GROUPS == 0:
                    pe.wait_ge(ctx_in[n // GROUPS], 16)
                if n >= 2:
                    pe.wait_ge(lo_done, n - 1)
                transpose_group(pe, bank[n % 2], crow[n // GROUPS], n % GROUPS, ident).then_inc(turned, 1)
            for g in range(GROUPS):
                if g == 0:
                    pe.wait_ge(rows_in[0], 16)
                pe.wait_ge(lo_done, C + g - 1)
                transpose_group(pe, bank[g % 2], rows[0], g, ident).then_inc(turned, 1)
            pe.wait_ge(small_in, 16 * 7)
            pe.transpose(ps_bias[:, 0:2 * KC], raw[:], ident[0:2 * KC, 0:2 * KC]).then_inc(bias_turned, 1)

            def body(j, first=False, last=False):
                for u in range(2):
                    n = 2 * j + u
                    if not first:
                        pe.wait_ge(biased, n - 1)
                    for g in range(GROUPS):
                        pe.wait_ge(lo_done, C + GROUPS * n + g + 1)
                        for c in range(4 * g, 4 * g + 4):
                            ins = split_product(pe, kp[u][:, 0:CR], (T[u][0][:, c, :], T[u][1][:, c, :]),
                                                (ctxT[0][:, c, :], ctxT[1][:, c, :]), c == 0, c == KC - 1)
                        if g == GROUPS - 1:
                            ins.then_inc(product, 1)
                        if last and u == 1:
                            continue
                        if g == 0:
                            pe.wait_ge(rows_in[1 - u], 16 * (j + 1 + u))
                        pe.wait_ge(lo_done, C + GROUPS * (n + 1) + g - 1)
                        transpose_group(pe, bank[g % 2], rows[1 - u], g, ident).then_inc(turned, 1)

            body(0, first=True)
            pe.wait_ge(diag_done, 2)
            for r in range(2):
                ins = pe.matmul(ps_mu[:, r * P:(r + 1) * P], ones[:], diag[r][:], start=True, stop=True)
            ins.then_inc(mu_ready, 1)
            with pe.Fori(1, KC // 2 - 1) as j:
                body(j)
            body(KC // 2 - 1, last=True)
            pe.wait_ge(dot_done, KC)
            pe.matmul(ps_row[:, 0:CR], ones[:], dot[:], start=True, stop=True).then_inc(row_done, 1)

        def ctx_part(n, part):
            r, g = n // GROUPS, n % GROUPS
            return ctxT[part][:, 4 * g:4 * g + 4, r * P:(r + 1) * P]

        @block.scalar
        def _(act):
            def parts_hi(n, u):
                for g in range(GROUPS):
                    act.wait_ge(turned, C + GROUPS * n + g + 1)
                    act.activation(T[u][0][:, 4 * g:4 * g + 4, :],
                                   bank[g % 2][:].rearrange("p (k n) -> p k n", k=4),
                                   ACT.Copy).then_inc(hi_done, 1)

            def key_parts(n, u):
                act.wait_ge(biased, n + 1)
                act.activation(KT[0][:, bass.ds(n, 1), :].rearrange("p o n -> p (o n)"), kf[u][:],
                               ACT.Copy).then_inc(key_hi, 1)

            def body(j, last=False):
                for u in range(2):
                    if not (last and u == 1):
                        parts_hi(2 * j + u + 1, 1 - u)
                    key_parts(2 * j + u, u)

            for n in range(C):
                act.wait_ge(turned, n + 1)
                act.activation(ctx_part(n, 0), bank[n % 2][:].rearrange("p (k n) -> p k n", k=4),
                               ACT.Copy).then_inc(hi_done, 1)
            parts_hi(0, 0)
            act.wait_ge(small_in, 16 * 7)
            act.activation(keep["tgx"][:], keep["tgx"][:], ACT.Tanh).then_inc(gates_ready, 1)
            act.activation(keep["tgf"][:], keep["tgf"][:], ACT.Tanh).then_inc(gates_ready, 1)
            body(0)
            act.wait_ge(diag_done, 2)
            for r in range(2):
                act.activation(chi[r][:], crow[r][:], ACT.Copy).then_inc(ctx_high, 1)
            with act.Fori(1, KC // 2 - 1) as j:
                body(j)
            body(KC // 2 - 1, last=True)

        @block.vector
        def _(dve):
            def parts_lo(n, u):
                for g in range(GROUPS):
                    dve.wait_ge(hi_done, C + GROUPS * n + g + 1)
                    dve.tensor_tensor(T[u][1][:, 4 * g:4 * g + 4, :],
                                      bank[g % 2][:].rearrange("p (k n) -> p k n", k=4),
                                      f32(T[u][0][:, 4 * g:4 * g + 4, :]), ALU.subtract).then_inc(lo_done, 1)

            def key_parts(n, u):
                dve.wait_ge(product, n + 1)
                dve.tensor_scalar(kf[u][:], kp[u][:, 0:CR], bias[:, bass.ds(n, 1)], None,
                                  ALU.add).then_inc(biased, 1)
                dve.drain()
                dve.scalar_tensor_tensor(dot[:], kf[u][:], bias[:, bass.ds(KC + n, 1)], dot[:],
                                         ALU.mult, ALU.add).then_inc(dot_done, 1)
                dve.wait_ge(key_hi, n + 1)
                hi = f32(KT[0][:, bass.ds(n, 1), :]).rearrange("p o n -> p (o n)")
                dve.tensor_tensor(KT[1][:, bass.ds(n, 1), :].rearrange("p o n -> p (o n)"), kf[u][:], hi,
                                  ALU.subtract).then_inc(key_lo, 1)

            def body(j, last=False):
                for u in range(2):
                    if not (last and u == 1):
                        parts_lo(2 * j + u + 1, 1 - u)
                    key_parts(2 * j + u, u)

            dve.memset(dot[:], 0.0)
            for n in range(C):
                dve.wait_ge(hi_done, n + 1)
                dve.tensor_tensor(ctx_part(n, 1), bank[n % 2][:].rearrange("p (k n) -> p k n", k=4),
                                  f32(ctx_part(n, 0)), ALU.subtract).then_inc(lo_done, 1)
            parts_lo(0, 0)
            dve.wait_ge(bias_turned, 1)
            dve.tensor_copy(bias[:], ps_bias[:, 0:2 * KC])
            for r in range(2):
                for k in range(4):
                    dve.bn_stats(stats[r][:, k, :], crow[r][:, k * QN:(k + 1) * QN])
                dve.drain()
                dve.bn_aggr(mv[r][:], stats[r][:])
                dve.drain()
                dve.tensor_scalar(diag[r][:], ident[:], mv[r][:, 0:1], None, ALU.mult).then_inc(diag_done, 1)
            body(0)
            dve.wait_ge(mu_ready, 1)
            dve.tensor_copy(keep["mu_all"][:], ps_mu[:, 0:CR])
            dve.wait_ge(gates_ready, 2)
            dve.tensor_scalar(keep["mu_scaled"][:].rearrange("p b n -> p (b n)"), ps_mu[:, 0:CR],
                              keep["tgx"][:, 0:1], None, ALU.mult)
            with dve.Fori(1, KC // 2 - 1) as j:
                body(j)
            body(KC // 2 - 1, last=True)
            dve.wait_ge(row_done, 1)
            dve.tensor_scalar(keep["bq_rows"][:].rearrange("p b n -> p (b n)"), ps_row[:, 0:CR],
                              ATT_SCALE, None, ALU.mult)


def load_wq(sp, io, rows, sems, n, u):
    wq = io["Wq"].rearrange("(c p) (t x) -> t p c x", p=P, x=P)
    sp.dma_start(rows[u][:].rearrange("p (c x) -> p c x", x=P),
                 wq[bass.ds(n, 1)].rearrange("o p c x -> p (o c) x")).then_inc(sems[u], 16)


def score_weights_block(nc, io, scr, keep):
    with ExitStack() as ctx:
        m = Memory(nc, ctx, "sw")
        rows, T, KT, ctxT = keep["rows"], keep["T"], keep["KT"], keep["ctxT"]
        cent = m.sb("ctx_centred", [P, KC, CR])
        shifted, summed, cent_hi, cent_lo = m.sem("shifted"), m.sem("summed"), m.sem("cent_hi"), m.sem("cent_lo")
        mp = [m.ps(f"mt{u}") for u in range(2)]
        out = [(m.sb(f"mt_hi{u}", [P, CR], F32R), m.sb(f"mt_lo{u}", [P, CR], F32R)) for u in range(2)]
        rows_in = keep["wq_in"]
        hi_done, lo_done, product = m.sem("hi_done"), m.sem("lo_done"), m.sem("product")
        out_hi, out_lo = m.sem("out_hi"), m.sem("out_lo")
        stored = keep["mt_out"]
        block = ctx.enter_context(nc.Block())

        @block.sync
        def _(sp):
            with sp.Fori(1, KC // 2) as j:
                for u in range(2):
                    sp.wait_ge(lo_done, 2 * j + u - 1)
                    load_wq(sp, io, rows, rows_in, 2 * j + u, u)
            for n in range(2):
                sp.wait_ge(lo_done, KC + n - 1)
                load_ffn(sp, io, rows, keep["ffn_in"], n)
            for u in range(2):
                sp.wait_ge(stored[u], 32 * KC // 2)
            sp.wait_ge(keep["ctx_stored"], 64)

        @block.gpsimd
        def _(pool):
            mean = keep["mu_all"][:].unsqueeze(1).broadcast_to([P, KC, CR])
            pool.tensor_tensor(cent[:], f32(ctxT[0][:]), mean, ALU.subtract).then_inc(shifted, 1)
            pool.wait_ge(shifted, 1)
            pool.tensor_tensor(cent[:], cent[:], f32(ctxT[1][:]), ALU.add).then_inc(summed, 1)
            pool.wait_ge(cent_lo, 1)
            for part in range(2):
                for b in range(BATCH):
                    pool.dma_start(scr["x"][b, part, :, :, NCTX:2 * NCTX],
                                   f32(ctxT[part][:, :, b * NCTX:(b + 1) * NCTX])).then_inc(keep["cent_out"], 16)

        @block.scalar
        def _(act):
            def weights_hi(n, u, first=False):
                act.wait_ge(rows_in[u], 8 * (n - u) + 16)
                if not first:
                    act.wait_ge(product, n - 1)
                act.activation(T[u][0][:].rearrange("p c x -> p (c x)"), rows[u][:], ACT.Copy).then_inc(hi_done, 1)

            def result(n, u, j, first):
                act.wait_ge(product, n + 1)
                if not first:
                    act.wait_ge(stored[u], 32 * j)
                act.activation(out[u][0][:], mp[u][:, 0:CR], ACT.Copy).then_inc(out_hi, 1)
                act.wait_ge(out_lo, n + 1)
                for part in range(2):
                    act.dma_start(scr["x"][:, part, :, bass.ds(n, 1), 0:NCTX].rearrange("b p o n -> p (o b) n"),
                                  f32(out[u][part][:]).rearrange("p (b n) -> p b n", n=NCTX)
                                  ).then_inc(stored[u], 16)

            def body(j, first=False, last=False):
                for u in range(2):
                    if not (last and u == 1):
                        weights_hi(2 * j + u + 1, 1 - u, first and u == 0)
                    result(2 * j + u, u, j, first)

            weights_hi(0, 0, True)
            body(0, first=True)
            act.wait_ge(summed, 1)
            act.activation(ctxT[0][:], cent[:], ACT.Copy).then_inc(cent_hi, 1)
            with act.Fori(1, KC // 2 - 1) as j:
                body(j)
            body(KC // 2 - 1, last=True)

        @block.vector
        def _(dve):
            def weights_lo(n, u):
                dve.wait_ge(hi_done, n + 1)
                dve.tensor_tensor(T[u][1][:].rearrange("p c x -> p (c x)"), rows[u][:],
                                  f32(T[u][0][:]).rearrange("p c x -> p (c x)"), ALU.subtract).then_inc(lo_done, 1)

            def body(j, last=False):
                for u in range(2):
                    n = 2 * j + u
                    if not (last and u == 1):
                        weights_lo(n + 1, 1 - u)
                    dve.wait_ge(out_hi, n + 1)
                    dve.tensor_tensor(out[u][1][:], mp[u][:, 0:CR], f32(out[u][0][:]),
                                      ALU.subtract).then_inc(out_lo, 1)

            weights_lo(0, 0)
            body(0)
            dve.wait_ge(cent_hi, 1)
            dve.tensor_tensor(ctxT[1][:], cent[:], f32(ctxT[0][:]), ALU.subtract).then_inc(cent_lo, 1)
            with dve.Fori(1, KC // 2 - 1) as j:
                body(j)
            body(KC // 2 - 1, last=True)

        @block.tensor
        def _(pe):
            def body(j, first):
                for u in range(2):
                    n = 2 * j + u
                    pe.wait_ge(lo_done, n + 1)
                    if not first:
                        pe.wait_ge(out_lo, n - 1)
                    for c in range(KC):
                        ins = split_product(pe, mp[u][:, 0:CR], (T[u][0][:, c, :], T[u][1][:, c, :]),
                                            (KT[0][:, c, :], KT[1][:, c, :]), c == 0, c == KC - 1)
                    ins.then_inc(product, 1)

            body(0, True)
            with pe.Fori(1, KC // 2) as j:
                body(j, False)


def ffn_jobs(io):
    av = io["aux_values"].rearrange("(t p) d -> t p d", p=P)
    wu1 = io["Wu1"].rearrange("(t p) d -> t p d", p=P)
    return ([(io["Wvd"], P), (None, P)] + [(av[t], P) for t in range(4)] + [(io["fWq"], BOT)]
            + [(wu1[t], P) for t in range(4)])


def load_ffn(sp, io, rows, sems, n):
    src, r = ffn_jobs(io)[n]
    if src is None:
        sp.dma_start(rows[n % 2][:].rearrange("p (c v) -> p c v", v=VB),
                     io["Wvu"].rearrange("(c p) v -> p c v", p=P)).then_inc(sems[n % 2], 16)
    else:
        sp.dma_start(rows[n % 2][0:r, :], src).then_inc(sems[n % 2], 16)


def ffn_block(nc, io, scr, keep):
    with ExitStack() as ctx:
        m = Memory(nc, ctx, "fw")
        ident, rows, W = keep["ident"], keep["rows"], keep["weights"]
        bw, wu = keep["bw"], keep["wu"]
        spare = [[W[i][:, KC * BW + k * D:KC * BW + (k + 1) * D].rearrange("p (c n) -> p c n", n=P)
                  for k in range(3)] for i in range(2)]
        wvd = [spare[i][0] for i in range(2)]
        part = [[spare[i][1 + u] for i in range(2)] for u in range(2)]
        wvu = [W[i][:, 0:D].rearrange("p (c n) -> p c n", n=P) for i in range(2)]
        wr, ak, ak2 = m.sb("wr", [RDIM, BOT]), m.sb("aux_keys", [P, 4, BOT]), m.sb("aux_keys_twice", [P, 4, P])
        wrT, wr2 = m.sb("wr_turned", [BOT, RDIM]), m.sb("wr_twice", [RDIM, 2 * BOT])
        akT, rkT = m.sb("aux_keys_turned", [P, NSLOT]), m.sb("router_keys", [RDIM, NSLOT])
        spare_z = keep["z"][:].rearrange("p t v -> p (t v)")
        gate2, akT8 = spare_z[:, 0:NSLOT], spare_z[:, NSLOT:2 * NSLOT]
        logr = spare_z[:, 2 * NSLOT:4 * NSLOT]
        bank = [m.ps(f"bank{i}") for i in range(GROUPS)]
        ps_av, ps_small, ps_rk, ps_g = m.ps("av"), m.ps("small"), m.ps("rk"), m.ps("g")
        rows_in = keep["ffn_in"]
        small_in, wvu_stored = m.sem("small_in"), m.sem("wvu_stored")
        turned, hi_done, lo_done = m.sem("turned"), m.sem("hi_done"), m.sem("lo_done")
        product, av_done = m.sem("product"), m.sem("av_done")
        keys_turned, keys_out, wr_turned, wr_out = (m.sem("keys_turned"), m.sem("keys_out"),
                                                    m.sem("wr_turned"), m.sem("wr_out"))
        wr2_done, ak2_done = m.sem("wr2_done"), m.sem("ak2_done")
        rk_ready, rk_out, g_ready = m.sem("rk_ready"), m.sem("rk_out"), m.sem("g_ready")
        slot_f32, slot_hi = m.sem("slot_f32"), m.sem("slot_hi")
        rs1, rs2, q2s = keep["rs1"], keep["rs2"], keep["q2s"]
        block = ctx.enter_context(nc.Block())

        WVU, FIRST_AV, FIRST_BW, FIRST_WU = 1, 2, 6, 8
        targets = [wvd, wvu] + [part[t % 2] for t in range(4)]
        targets += [[bw[i][:, :, QC:QC + BOT] for i in range(2)], [bw[i][:, :, QC + BOT:BW] for i in range(2)]]
        targets += [[wu[i][:, :, t * P:(t + 1) * P] for i in range(2)] for t in range(3)]
        jobs = [(r, dst) for (_, r), dst in zip(ffn_jobs(io), targets)]

        @block.sync
        def _(sp):
            sp.dma_start(wr[:], io["Wr"]).then_inc(small_in, 16)
            sp.dma_start(ak[:], io["aux_keys"].rearrange("(t p) b -> p t b", p=P)).then_inc(small_in, 16)
            for half in range(2):
                sp.dma_start(logr[BOT:BOT + 2, half * NSLOT:(half + 1) * NSLOT],
                             io["log_rel"].rearrange("(a n) -> a n", a=1).broadcast_to([2, NSLOT])
                             ).then_inc(small_in, 16)
            for n in ("bu1", "wu2"):
                sp.dma_start(keep[n][:], io[n].rearrange("(a n) -> a n", a=1).broadcast_to([P, HU])
                             ).then_inc(small_in, 16)
            for n in range(2, len(jobs)):
                sp.wait_ge(turned, GROUPS * (n - 1))
                load_ffn(sp, io, rows, rows_in, n)
                if n == WVU + 2:
                    sp.wait_ge(lo_done, GROUPS * (WVU + 1))
                    for i in range(2):
                        sp.dma_start(scr["wvu"][i], f32(W[i][:, 0:D])).then_inc(wvu_stored, 16)
            for u in range(2):
                sp.wait_ge(turned, GROUPS * (len(jobs) + u - 1))
                load_x(sp, io, rows, keep["x_in"], 1 - u, 1 - u)
            for u in range(2):
                sp.wait_ge(keep["mt_out"][u], 32 * KC // 2)
            sp.wait_ge(keep["cent_out"], 16 * 2 * BATCH)
            sp.wait_ge(wvu_stored, 32)
            load_batch_b(sp, scr, keep, 0)

        @block.tensor
        def _(pe):
            for n, (r, _) in enumerate(jobs):
                pe.wait_ge(rows_in[n % 2], 16 * (n // 2 + 1))
                for g in range(GROUPS):
                    if n:
                        pe.wait_ge(lo_done, GROUPS * (n - 1) + g + 1)
                    transpose_group(pe, bank[g], rows[n % 2], g, ident, r).then_inc(turned, 1)
                if n == 1:
                    pe.wait_ge(small_in, 16 * 6)
                    for t in range(4):
                        ins = pe.transpose(ps_small[0:BOT, t * P:(t + 1) * P], ak[:, t, :], ident[:])
                    ins.then_inc(keys_turned, 1)
                    pe.transpose(ps_g[0:BOT, 0:RDIM], wr[:], ident[0:RDIM, 0:RDIM]).then_inc(wr_turned, 1)
                if n == 2:
                    pe.wait_ge(keys_out, 1)
                    pe.wait_ge(wr_out, 1)
                    pe.matmul(ps_rk[0:RDIM, :], wrT[:], akT[0:BOT, :], start=True, stop=True).then_inc(rk_ready, 1)
                if n == 3:
                    pe.wait_ge(rk_out, 1)
                    pe.wait_ge(wr2_done, 1)
                    pe.matmul(ps_g[:], wr2[:], rkT[:], start=True, stop=True).then_inc(g_ready, 1)
                    pe.wait_ge(ak2_done, 1)
                    for t in range(4):
                        ins = pe.transpose(ps_small[:, t * P:(t + 1) * P], ak2[:, t, :], ident[:])
                    ins.then_inc(keys_turned, 1)
                if FIRST_AV < n <= FIRST_BW:
                    s = n - 1 - FIRST_AV
                    pe.wait_ge(lo_done, GROUPS * n)
                    if s:
                        pe.wait_ge(av_done, s)
                    for c in range(KC):
                        ins = split_product(pe, ps_av[:, 0:VB], (part[s % 2][0][:, c, :], part[s % 2][1][:, c, :]),
                                            (wvd[0][:, c, :], wvd[1][:, c, :]), c == 0, c == KC - 1)
                    ins.then_inc(product, 1)

        @block.scalar
        def _(act):
            for n, (r, dst) in enumerate(jobs):
                if FIRST_AV + 2 <= n < FIRST_BW:
                    act.wait_ge(product, n - FIRST_AV - 1)
                if n == FIRST_BW:
                    act.wait_ge(wvu_stored, 32)
                if n == FIRST_WU:
                    act.wait_ge(product, 4)
                for g in range(GROUPS):
                    act.wait_ge(turned, GROUPS * n + g + 1)
                    act.activation(dst[0][:, 4 * g:4 * g + 4, :],
                                   bank[g][:, 0:4 * r].rearrange("p (k n) -> p k n", k=4),
                                   ACT.Copy).then_inc(hi_done, 1)
                if n == 1:
                    act.wait_ge(small_in, 16 * 6)
                    act.activation(wr2[:, 0:BOT], wr[:], ACT.Copy)
                    act.activation(wr2[:, BOT:2 * BOT], wr[:], ACT.Copy).then_inc(wr2_done, 1)
                    act.activation(ak2[:, :, 0:BOT], ak[:], ACT.Copy, scale=0.125)
                    act.activation(ak2[:, :, BOT:2 * BOT], ak[:], ACT.Copy, scale=0.125).then_inc(ak2_done, 1)
                if n == 4:
                    act.wait_ge(slot_f32, 2)
                    act.activation(rs1[:, 0:NSLOT], gate2, ACT.Copy)
                    act.activation(rs1[:, NSLOT:2 * NSLOT], akT8, ACT.Copy)
                    act.activation(rs2[BOT:BOT + 2, :], logr[BOT:BOT + 2, :], ACT.Copy).then_inc(slot_hi, 1)

        @block.vector
        def _(dve):
            dve.memset(q2s[BOT:BOT + 2, :].bitcast(F32), 1.0)
            for n, (r, dst) in enumerate(jobs):
                for g in range(GROUPS):
                    dve.wait_ge(hi_done, GROUPS * n + g + 1)
                    dve.tensor_tensor(dst[1][:, 4 * g:4 * g + 4, :],
                                      bank[g][:, 0:4 * r].rearrange("p (k n) -> p k n", k=4),
                                      f32(dst[0][:, 4 * g:4 * g + 4, :]), ALU.subtract).then_inc(lo_done, 1)
                if n == 1:
                    dve.wait_ge(small_in, 16 * 6)
                    dve.tensor_scalar(keep["wu2"][:], keep["wu2"][:], 0.5, None, ALU.mult)
                    dve.wait_ge(keys_turned, 1)
                    dve.tensor_copy(akT[0:BOT, :], ps_small[0:BOT, :]).then_inc(keys_out, 1)
                    dve.wait_ge(wr_turned, 1)
                    dve.tensor_copy(wrT[:], ps_g[0:BOT, 0:RDIM]).then_inc(wr_out, 1)
                if n == 2:
                    dve.wait_ge(rk_ready, 1)
                    dve.tensor_copy(rkT[:], ps_rk[0:RDIM, :]).then_inc(rk_out, 1)
                if n == 3:
                    dve.wait_ge(g_ready, 1)
                    dve.tensor_scalar(gate2, ps_g[:], 1.0 / float(RDIM) ** 0.5, None, ALU.mult).then_inc(slot_f32, 1)
                    dve.wait_ge(keys_turned, 2)
                    dve.tensor_copy(akT8, ps_small[:]).then_inc(slot_f32, 1)
                if n == 4:
                    dve.wait_ge(slot_hi, 1)
                    dve.tensor_tensor(rs2[0:BOT, 0:NSLOT], gate2[0:BOT, :], f32(rs1[0:BOT, 0:NSLOT]), ALU.subtract)
                    dve.tensor_tensor(rs2[0:BOT, NSLOT:2 * NSLOT], akT8[0:BOT, :],
                                      f32(rs1[0:BOT, NSLOT:2 * NSLOT]), ALU.subtract)
                    dve.tensor_tensor(rs2[BOT:BOT + 1, :], logr[BOT:BOT + 1, :], f32(rs2[BOT:BOT + 1, :]),
                                      ALU.subtract)
                if FIRST_AV < n <= FIRST_BW:
                    s = n - 1 - FIRST_AV
                    dve.wait_ge(product, s + 1)
                    dve.tensor_copy(keep["av"][:, s, :], ps_av[:, 0:VB]).then_inc(av_done, 1)


def load_x(sp, io, rows, sems, t, u):
    sp.dma_start(rows[u][:], io["x"].rearrange("(t p) d -> t p d", p=P)[bass.ds(t, 1)].rearrange("o p d -> p (o d)")
                 ).then_inc(sems[u], 16)


def load_ctx(sp, scr, keep, b):
    hi, lo = keep["ctx_out"]
    for half in range(2):
        sp.dma_start(f32(hi[half * NCTX:(half + 1) * NCTX, b, :]),
                     scr["ctx"][0, b * NCTX:(b + 1) * NCTX, :]).then_inc(keep["ctx_in"][b], 16)
    sp.dma_start(f32(lo[0:NCTX, b, :]), scr["ctx"][1, b * NCTX:(b + 1) * NCTX, :]).then_inc(keep["ctx_in"][b], 16)


def load_batch_b(sp, scr, keep, b):
    for part in range(2):
        sp.dma_start(f32(keep["bw"][part][:, :, 0:2 * NCTX]),
                     scr["x"][bass.ds(b, 1), part].rearrange("o p c n -> p (o c) n")).then_inc(keep["b_in"], 16)


def context_weights_block(nc, scr, keep):
    with ExitStack() as ctx:
        m = Memory(nc, ctx, "cw")
        bw, wu, tgx = keep["bw"], keep["wu"], keep["tgx"]
        cT = keep["ctxT"]
        cw = [m.sb(f"cw{r}", [P, CWN]) for r in range(2)]
        hr = [m.sb(f"cw_hi{r}", [P, CWN], F32R) for r in range(2)]
        lo = [m.sb(f"cw_lo{r}", [P, CWN]) for r in range(2)]
        bank_u = [m.ps(f"hidden{r}") for r in range(2)]
        bank_q = [m.ps(f"query{r}") for r in range(2)]
        product, scaled, high, low, stored = (m.sem("product"), m.sem("scaled"), m.sem("high"), m.sem("low"),
                                              m.sem("stored"))
        block = ctx.enter_context(nc.Block())

        @block.sync
        def _(sp):
            for r in range(2):
                sp.wait_ge(low, r + 1)
                for part, src in ((0, f32(hr[r][:])), (1, lo[r][:])):
                    sp.dma_start(scr["cw"][part, r * P:(r + 1) * P, :], src).then_inc(stored, 16)
            sp.wait_ge(stored, 64)

        @block.tensor
        def _(pe):
            for r in range(2):
                for c in range(KC):
                    left = tuple(cT[i][:, c, r * P:(r + 1) * P] for i in range(2))
                    split_product(pe, bank_q[r][:, 0:P], left,
                                  tuple(cT[i][:, c, r * P:(r + 1) * P] for i in range(2)), c == 0, c == KC - 1, True)
                    split_product(pe, bank_q[r][:, P:P + BOT + UA], left,
                                  (bw[0][:, c, QC:BW], bw[1][:, c, QC:BW]), False, c == KC - 1, True)
                    ins = split_product(pe, bank_u[r][:, 0:UB], left, (wu[0][:, c, :], wu[1][:, c, :]), c == 0,
                                        c == KC - 1)
                ins.then_inc(product, 1)

        @block.vector
        def _(dve):
            for r in range(2):
                dve.wait_ge(product, r + 1)
                dve.tensor_scalar(cw[r][:, CWN - UB:CWN], bank_u[r][:, 0:UB], tgx[:, 0:1], None, ALU.mult)
                dve.tensor_scalar(cw[r][:, NCTX:CWN - UB], bank_q[r][:, P:P + BOT + UA], tgx[:, 0:1], None, ALU.mult)
                for k in range(2):
                    own = slice(k * NCTX, (k + 1) * NCTX)
                    ins = dve.tensor_scalar(cw[r][own, 0:NCTX], bank_q[r][own, own], tgx[own, 0:1], 0.5,
                                            ALU.mult, ALU.mult)
                ins.then_inc(scaled, 1)
                dve.wait_ge(high, r + 1)
                dve.tensor_tensor(lo[r][:], cw[r][:], f32(hr[r][:]), ALU.subtract).then_inc(low, 1)

        @block.scalar
        def _(act):
            for r in range(2):
                act.wait_ge(scaled, r + 1)
                act.activation(hr[r][:], cw[r][:], ACT.Copy).then_inc(high, 1)


def token_block(nc, io, scr, keep):
    with ExitStack() as ctx:
        m = Memory(nc, ctx, "tk")
        ident = keep["ident"]
        bw, wu, rs1, rs2, av = keep["bw"], keep["wu"], keep["rs1"], keep["rs2"], keep["av"]
        x = keep["rows"]
        xT = [tuple(z[:, i * D:(i + 1) * D].rearrange("p (c n) -> p c n", n=P) for i in range(2)) for z in keep["Z"]]
        cw1, cw2 = m.sb("cw_stack", [P, CWN], F32R), m.sb("cw_low", [NCTX, CWN], F32R)
        stats = m.sb("stats", [P, 4, 6])
        mv = [m.sb(f"mean_var{u}", [P, 2]) for u in range(2)]
        nmean = [m.sb(f"nmean{u}", [P, 1]) for u in range(2)]
        rstd1 = [m.sb(f"rstd1_{u}", [P, 1]) for u in range(2)]
        nscale = m.sb("neg_score_scale", [P, 1])
        neg_s, neg_max = m.sb("neg_scores", [P, NCTX]), m.sb("neg_max", [P, 1])
        esum, einv = m.sb("exp_sum", [P, 1]), m.sb("exp_inv", [P, 1])
        e1 = m.sb("exp_scores", [P, NCTX])
        att2 = [m.sb(f"att_twice{u}", [P, 2 * NCTX]) for u in range(2)]
        attS = m.sb("att_stack", [P, P], F32R)
        junk, junk2, shift = m.sb("junk", [P, NCTX]), m.sb("junk2", [P, NCTX]), m.sb("mean_shift", [P, 1])
        mvk = [m.sb(f"mean_var_kept{u}", [P, 2]) for u in range(2)]
        st2 = [m.sb(f"stats2_{u}", [P, 4]) for u in range(2)]
        ve = m.sb("var_eps", [P, 1])
        ve1 = m.sb("var_eps1", [P, 1])
        q2, qS = m.sb("query_twice", [P, 2 * BOT]), m.sb("query_stack", [P, P], F32R)
        q2s = keep["q2s"]
        hid, act1, hw = m.sb("hidden", [P, HU]), m.sb("gelu", [P, HU]), m.sb("hidden_wu2", [P, HU])
        top8, picked = m.sb("top8", [P, TOPK]), m.sb("picked", [P, NSLOT])
        ws, wmax, wneg = m.sb("slot_weights", [P, NSLOT]), m.sb("slot_max", [P, 1]), m.sb("slot_neg", [P, 1])
        wsum, winv = m.sb("slot_sum", [P, 1]), m.sb("slot_inv", [P, 1])
        wT = m.sb("weights_turned", [P, NSLOT])
        bank = [m.ps(f"bank{i}") for i in range(2)]
        psA, psB = m.ps("hidden_sum"), [m.ps(f"b_sum{u}") for u in range(2)]
        psR, psS, psM = m.ps("router"), m.ps("slots"), m.ps("small")
        att_turned_ps, q_turned_ps, z_ps = psM[:, 0:P], psM[:, P:2 * P], psM[:, 2 * P:2 * P + VB]

        S = {n: m.sem(n) for n in (
            "cw_in", "turned", "x_hi", "x_lo", "b_sum", "c_sum", "centred",
            "mean_var", "rstd1", "neg_scores", "exp", "att", "att_turned", "att_hi", "att_lo",
            "var1", "rstd2", "query", "q_turned", "q_hi", "q_lo", "hidden", "routed", "slots",
            "slot_exp", "w_turned", "w_out", "z_sum", "z_out", "square", "inner", "tanh", "hw", "learned",
            "kept_att", "kept_stats", "poly")}
        x_in, b_in = keep["x_in"], keep["b_in"]
        block = ctx.enter_context(nc.Block())
        G = GROUPS

        def load_batch_cw(sp, b):
            for half in range(2):
                sp.dma_start(f32(cw1[half * NCTX:(half + 1) * NCTX, :]),
                             scr["cw"][0, bass.ds(b * NCTX, NCTX), :]).then_inc(S["cw_in"], 16)
            sp.dma_start(f32(cw2[:]), scr["cw"][1, bass.ds(b * NCTX, NCTX), :]).then_inc(S["cw_in"], 16)

        @block.sync
        def _(sp):
            load_batch_cw(sp, 0)
            for t in range(2, 8):
                sp.wait_ge(S["turned"], G * (t - 1))
                load_x(sp, io, x, x_in, t, t % 2)
            with sp.Fori(1, BATCH) as b:
                for k in range(8):
                    sp.wait_ge(S["turned"], G * (8 * b + k - 1))
                    load_x(sp, io, x, x_in, 8 * b + k, k % 2)
                    if k == 1:
                        sp.wait_ge(S["b_sum"], 8 * b)
                        load_batch_b(sp, scr, keep, b)
                        sp.wait_ge(S["c_sum"], 8 * b)
                        load_batch_cw(sp, b)
            for u in range(2):
                sp.wait_ge(S["turned"], G * (TILES + u - 1))
                load_x(sp, io, x, keep["out_x_in"], u, u)
            sp.wait_ge(S["c_sum"], TILES)
            load_ctx(sp, scr, keep, 0)
            for i in range(2):
                sp.dma_start(f32(keep["wvu_out"][i]), scr["wvu"][i]).then_inc(keep["wvu_in"], 16)
            for b in range(1, BATCH):
                load_ctx(sp, scr, keep, b)

        @block.tensor
        def _(pe):
            def turn_x(t, u, g, first=False):
                if not (first and g < 2):
                    pe.wait_ge(S["x_lo"], G * t + g - 1)
                transpose_group(pe, bank[g % 2], x[u], g, ident).then_inc(S["turned"], 1)

            def b_part(t, u, g):
                pe.wait_ge(S["x_lo"], G * t + g + 1)
                for c in range(4 * g, 4 * g + 4):
                    ins = split_product(pe, psB[u][:, 0:BW], (xT[u][0][:, c, :], xT[u][1][:, c, :]),
                                        (bw[0][:, c, :], bw[1][:, c, :]), c == 0, c == KC - 1, True)
                return ins

            def a_part(t, u, g, first):
                if g == 0 and not first:
                    pe.wait_ge(S["hidden"], t)
                for c in range(4 * g, 4 * g + 4):
                    split_product(pe, psA[:, 0:UB], (xT[u][0][:, c, :], xT[u][1][:, c, :]),
                                  (wu[0][:, c, :], wu[1][:, c, :]), c == 0, c == KC - 1, True)

            def late_query(t, first=False):
                pe.wait_ge(S["query"], t + 1)
                if not first:
                    pe.wait_ge(S["z_out"], t)
                pe.transpose(q_turned_ps, q2[:], ident[:]).then_inc(S["q_turned"], 1)

            def late_route(t, first):
                pe.wait_ge(S["q_lo"], t + 1)
                pe.wait_ge(S["q_hi"], t + 1)
                if not first:
                    pe.wait_ge(S["w_out"], t)
                    pe.wait_ge(S["slots"], t)
                for bank_, n in ((psR, 0), (psS, NSLOT)):
                    pe.matmul(bank_[:], qS[:], rs1[:, n:n + NSLOT], start=True, stop=False)
                    ins = pe.matmul(bank_[:], q2s[0:BOT + 2, :], rs2[:, n:n + NSLOT], start=False, stop=True)
                ins.then_inc(S["routed"], 1)

            def late_turn_w(t):
                pe.wait_ge(S["slot_exp"], t + 1)
                for k in range(4):
                    ins = pe.transpose(psR[:, k * P:(k + 1) * P], ws[:, k * P:(k + 1) * P], ident[:])
                ins.then_inc(S["w_turned"], 1)

            def late_z(t, more=True):
                pe.wait_ge(S["w_out"], t + 1)
                pe.wait_ge(S["att_lo"], t + 2 if more else t + 1)
                for k in range(4):
                    ins = pe.matmul(z_ps, wT[:, k * P:(k + 1) * P], av[:, k, :], start=(k == 0), stop=(k == 3))
                ins.then_inc(S["z_sum"], 1)

            def tile(t, u, late=True, late_first=False, first=False, last=False, second=False, j=None):
                pe.wait_ge(b_in, 32 * b_of(j))
                if not (first or second):
                    pe.wait_ge(S["hidden"], t - 1)
                b_part(t, u, 0)
                b_part(t, u, 1)
                if late:
                    late_query(t - 1, late_first)
                b_part(t, u, 2)
                b_part(t, u, 3).then_inc(S["b_sum"], 1)
                if late:
                    late_route(t - 1, late_first)
                a_part(t, u, 0, first)
                if not last:
                    pe.wait_ge(S["centred"], t + 2)
                    turn_x(t + 1, 1 - u, 0)
                a_part(t, u, 1, first)
                if not last:
                    turn_x(t + 1, 1 - u, 1)
                pe.wait_ge(S["att"], t + 1)
                pe.transpose(att_turned_ps, att2[u][:], ident[:]).then_inc(S["att_turned"], 1)
                a_part(t, u, 2, first)
                if not last:
                    turn_x(t + 1, 1 - u, 2)
                if late:
                    late_turn_w(t - 1)
                a_part(t, u, 3, first)
                if not last:
                    turn_x(t + 1, 1 - u, 3)
                if late:
                    late_z(t - 1)
                pe.wait_ge(S["cw_in"], 48 * b_of(j))
                pe.wait_ge(S["att_hi"], t + 1)
                pe.wait_ge(S["att_lo"], t + 1)
                for out, n0, n1 in ((psB[u][:, NCTX:BW], 0, CWN - UB), (psA[:, 0:UB], CWN - UB, CWN)):
                    pe.matmul(out, attS[:], cw1[:, n0:n1], start=False, stop=False, skip_group_check=True)
                    ins = pe.matmul(out, attS[0:NCTX, :], cw2[:, n0:n1], start=False, stop=True,
                                    skip_group_check=True)
                ins.then_inc(S["c_sum"], 1)

            def b_of(j):
                return j // 4 + 1

            pe.wait_ge(S["centred"], 1)
            for g in range(G):
                turn_x(0, 0, g, first=True)
            tile(0, 0, late=False, first=True, j=0)
            tile(1, 1, late_first=True, second=True, j=0)
            with pe.Fori(1, PAIRS - 1) as j:
                for u in range(2):
                    tile(2 * j + u, u, j=j)
            tile(TILES - 2, 0, j=PAIRS - 1)
            tile(TILES - 1, 1, j=PAIRS - 1, last=True)
            late_query(TILES - 1)
            late_route(TILES - 1, False)
            late_turn_w(TILES - 1)
            late_z(TILES - 1, more=False)

        @block.scalar
        def _(act):
            def centre(t, u, j):
                act.wait_ge(S["mean_var"], t + 1)
                act.activation(x[u][:], x[u][:], ACT.Identity, bias=nmean[u][:, 0:1]).then_inc(S["centred"], 1)

            def x_hi(t, u, g):
                act.wait_ge(S["turned"], G * t + g + 1)
                act.activation(xT[u][0][:, 4 * g:4 * g + 4, :], bank[g % 2][:].rearrange("p (k n) -> p k n", k=4),
                               ACT.Copy).then_inc(S["x_hi"], 1)

            def soft(t, u):
                act.wait_ge(S["neg_scores"], t + 1)
                act.activation(e1[:], neg_s[:], ACT.Exp, bias=neg_max[:, 0:1], scale=-1.0,
                               accum_out=esum[:]).then_inc(S["exp"], 1)

            def late_square(t):
                act.wait_ge(S["hidden"], t + 1)
                act.activation(act1[:], hid[:], ACT.Square).then_inc(S["square"], 1)

            def late_q_hi(t, first):
                act.wait_ge(S["q_turned"], t + 1)
                if not first:
                    act.wait_ge(S["routed"], t)
                act.activation(qS[:], q_turned_ps, ACT.Copy)
                act.activation(q2s[0:BOT, :], q_turned_ps[0:BOT, :], ACT.Copy).then_inc(S["q_hi"], 1)

            def att_hi(t):
                act.wait_ge(S["att_turned"], t + 1)
                act.activation(attS[:], att_turned_ps, ACT.Copy).then_inc(S["att_hi"], 1)

            def late_exp(t):
                act.wait_ge(S["slots"], t + 1)
                act.activation(ws[:], ws[:], ACT.Exp, bias=wneg[:, 0:1], accum_out=wsum[:]).then_inc(S["slot_exp"], 1)

            def late_w_out(t, first):
                act.wait_ge(S["w_turned"], t + 1)
                if not first:
                    act.wait_ge(S["z_sum"], t)
                act.activation(wT[:], psR[:], ACT.Copy).then_inc(S["w_out"], 1)

            def late_tanh(t):
                act.wait_ge(S["inner"], t + 1)
                act.activation(act1[:], act1[:], ACT.Tanh, scale=0.7978845608028654).then_inc(S["tanh"], 1)

            def tile(t, u, late=True, late_first=False, last=False, ahead=True, j=None):
                if late:
                    late_square(t - 1)
                    late_q_hi(t - 1, late_first)
                soft(t, u)
                if late:
                    late_tanh(t - 1)
                if not last:
                    x_hi(t + 1, 1 - u, 0)
                if late:
                    late_exp(t - 1)
                if not last:
                    x_hi(t + 1, 1 - u, 1)
                att_hi(t)
                if not last:
                    x_hi(t + 1, 1 - u, 2)
                if late:
                    late_w_out(t - 1, late_first)
                if not last:
                    x_hi(t + 1, 1 - u, 3)
                if ahead:
                    centre(t + 2, u, j)

            for t in range(2):
                centre(t, t, 0)
            for g in range(G):
                x_hi(0, 0, g)
            tile(0, 0, late=False, j=0)
            tile(1, 1, late_first=True, j=0)
            with act.Fori(1, PAIRS - 1) as j:
                for u in range(2):
                    tile(2 * j + u, u, j=j)
            tile(TILES - 2, 0, ahead=False)
            tile(TILES - 1, 1, last=True, ahead=False)
            t = TILES - 1
            late_square(t)
            late_q_hi(t, False)
            late_tanh(t)
            late_exp(t)
            late_w_out(t, False)

        @block.gpsimd
        def _(pool):
            def power(out, in_, tmp):
                pool.tensor_tensor(tmp, in_, keep["eps"][:], ALU.add)
                pool.drain()
                return pool.tensor_tensor(out, tmp, keep["minus_half"][:], ALU.pow)

            def first_rstd(t, u):
                pool.drain()
                pool.wait_ge(S["mean_var"], t + 1)
                power(rstd1[u][:], mv[u][:, 1:2], ve1[:]).then_inc(S["rstd1"], 1)

            def late(t, u):
                pool.drain()
                pool.wait_ge(S["var1"], t + 1)
                power(st2[u][:, 2:3], st2[u][:, 1:2], ve[:]).then_inc(S["rstd2"], 1)
                pool.wait_ge(S["hidden"], t + 1)
                if not (isinstance(t, int) and t == 0):
                    pool.wait_ge(S["learned"], t)
                pool.tensor_tensor(hw[:], hid[:], keep["wu2"][:], ALU.mult).then_inc(S["hw"], 1)
                pool.wait_ge(S["poly"], t + 1)
                pool.tensor_tensor(act1[:], act1[:], hid[:], ALU.mult).then_inc(S["inner"], 1)
                pool.wait_ge(S["learned"], t + 1)
                pool.tensor_copy(keep["stats"][:, bass.ds(t, 1), :].rearrange("p o n -> p (o n)"),
                                 st2[u][:]).then_inc(S["kept_stats"], 1)

            def keep_att(t, u):
                pool.wait_ge(S["att"], t + 1)
                pool.tensor_copy(keep["att"][:, bass.ds(t, 1), :].rearrange("p o n -> p (o n)"),
                                 att2[u][:, 0:NCTX]).then_inc(S["kept_att"], 1)

            pool.memset(keep["minus_half"][:], -0.5)
            pool.memset(keep["eps"][:], EPS).then_inc(S["kept_stats"], 1)
            pool.drain()
            for t in range(2):
                first_rstd(t, t)
            keep_att(0, 0)
            first_rstd(2, 0)
            late(0, 0)
            keep_att(1, 1)
            first_rstd(3, 1)
            with pool.Fori(1, PAIRS - 1) as j:
                for u in range(2):
                    t = 2 * j + u
                    late(t - 1, 1 - u)
                    keep_att(t, u)
                    first_rstd(t + 2, u)
            for t in (TILES - 2, TILES - 1):
                late(t - 1, 1 - t % 2)
                keep_att(t, t % 2)
            late(TILES - 1, 1)

        @block.vector
        def _(dve):
            def moments_of(t, u, j, quarters):
                dve.wait_ge(x_in[u], 16 * j + 16)
                for k in quarters:
                    dve.bn_stats(stats[:, k, :], x[u][:, k * QN:(k + 1) * QN])

            def moments(t, u):
                dve.drain()
                dve.bn_aggr(mv[u][:], stats[:])
                dve.drain()
                dve.tensor_scalar(nmean[u][:], mv[u][:, 0:1], -1.0, None, ALU.mult).then_inc(S["mean_var"], 1)

            def x_lo(t, u, g):
                dve.wait_ge(S["x_hi"], G * t + g + 1)
                dve.tensor_tensor(xT[u][1][:, 4 * g:4 * g + 4, :], bank[g % 2][:].rearrange("p (k n) -> p k n", k=4),
                                  f32(xT[u][0][:, 4 * g:4 * g + 4, :]), ALU.subtract).then_inc(S["x_lo"], 1)

            def soft_scores(t, u, batch):
                dve.wait_ge(S["rstd1"], t + 1)
                dve.tensor_scalar(nscale[:], rstd1[u][:], -ATT_SCALE, None, ALU.mult)
                dve.tensor_copy(mvk[u][:], mv[u][:])
                dve.drain()
                dve.wait_ge(S["b_sum"], t + 1)
                dve.scalar_tensor_tensor(neg_s[:], psB[u][:, 0:NCTX], nscale[:, 0:1], at(keep["bq_rows"], batch),
                                         ALU.mult, ALU.subtract)
                dve.drain()
                dve.tensor_reduce(neg_max[:], neg_s[:], AX.X, ALU.min).then_inc(S["neg_scores"], 1)

            def soft_att(t, u, first):
                dve.wait_ge(S["exp"], t + 1)
                dve.reciprocal(einv[:], esum[:])
                dve.drain()
                if not first:
                    dve.wait_ge(S["kept_att"], t - 1)
                dve.tensor_scalar(att2[u][:, 0:NCTX], e1[:], einv[:, 0:1], None, ALU.mult)
                dve.tensor_scalar(att2[u][:, NCTX:2 * NCTX], e1[:], einv[:, 0:1], None,
                                  ALU.mult).then_inc(S["att"], 1)

            def att_lo(t):
                dve.wait_ge(S["att_hi"], t + 1)
                dve.tensor_tensor(attS[NCTX:P, :], att_turned_ps[NCTX:P, :], f32(attS[NCTX:P, :]),
                                  ALU.subtract).then_inc(S["att_lo"], 1)

            def late_stats(t, u, batch, first):
                dve.wait_ge(S["c_sum"], t + 1)
                if not first:
                    dve.wait_ge(S["kept_stats"], t)
                dve.tensor_tensor_reduce(junk[:], psB[u][:, NCTX:2 * NCTX], att2[u][:, 0:NCTX],
                                         keep["cov_scale"][:, 0:1], mvk[u][:, 1:2],
                                         ALU.mult, ALU.add, st2[u][:, 1:2]).then_inc(S["var1"], 1)
                dve.scalar_tensor_tensor(junk2[:], att2[u][:, 0:NCTX], 1.0, at(keep["mu_scaled"], batch),
                                         ALU.mult, ALU.mult, accum_out=shift[:])
                dve.drain()
                dve.tensor_tensor(st2[u][:, 0:1], shift[:], mvk[u][:, 0:1], ALU.add)

            def late_scale(t, u):
                dve.wait_ge(S["rstd2"], t + 1)
                dve.tensor_scalar(q2[:, 0:BOT], psB[u][:, QC:QC + BOT], st2[u][:, 2:3], None, ALU.mult)
                dve.tensor_scalar(q2[:, BOT:2 * BOT], psB[u][:, QC:QC + BOT], st2[u][:, 2:3], None,
                                  ALU.mult).then_inc(S["query"], 1)
                dve.scalar_tensor_tensor(hid[:, 0:UA], psB[u][:, QC + BOT:BW], st2[u][:, 2:3], keep["bu1"][:, 0:UA],
                                         ALU.mult, ALU.add)
                dve.scalar_tensor_tensor(hid[:, UA:HU], psA[:, 0:UB], st2[u][:, 2:3], keep["bu1"][:, UA:HU], ALU.mult,
                                         ALU.add).then_inc(S["hidden"], 1)

            def late_q_lo(t):
                dve.wait_ge(S["q_hi"], t + 1)
                dve.tensor_tensor(qS[BOT:P, :], q_turned_ps[BOT:P, :], f32(qS[BOT:P, :]),
                                  ALU.subtract).then_inc(S["q_lo"], 1)

            def late_poly(t):
                dve.wait_ge(S["square"], t + 1)
                dve.tensor_scalar(act1[:], act1[:], 0.044715, 1.0, ALU.mult, ALU.add).then_inc(S["poly"], 1)

            def late_slots(t):
                dve.wait_ge(S["routed"], t + 1)
                dve.memset(wmax[:], OUT_OF_RANGE)
                dve.max(top8[:], psR[:])
                dve.drain()
                dve.match_replace(picked[:], top8[:], psR[:], PICKED)
                dve.drain()
                dve.tensor_scalar(picked[:], picked[:], PICKED, OUT_OF_RANGE, ALU.is_lt, ALU.mult)
                dve.drain()
                dve.tensor_tensor_reduce(ws[:], psS[:], picked[:], 1.0, -3.0e38, ALU.add, ALU.max, wmax[:])
                dve.drain()
                dve.tensor_scalar(wneg[:], wmax[:], -1.0, None, ALU.mult).then_inc(S["slots"], 1)

            def late_learned(t, u):
                dve.wait_ge(S["tanh"], t + 1)
                dve.wait_ge(S["hw"], t + 1)
                dve.scalar_tensor_tensor(act1[:], act1[:], 1.0, hw[:], ALU.add, ALU.mult,
                                         accum_out=st2[u][:, 3:4]).then_inc(S["learned"], 1)

            def late_z(t):
                dve.wait_ge(S["slot_exp"], t + 1)
                dve.reciprocal(winv[:], wsum[:])
                dve.drain()
                dve.wait_ge(S["z_sum"], t + 1)
                dve.tensor_scalar(keep["z"][:, bass.ds(t, 1), :].rearrange("p o n -> p (o n)"), z_ps,
                                  winv[:, 0:1], None, ALU.mult).then_inc(S["z_out"], 1)

            def tile(t, u, j, late=True, last=False, ahead=True, first=False, second=False):
                if late:
                    late_stats(t - 1, 1 - u, (j if u else j - 1) // 4, second)
                    late_scale(t - 1, 1 - u)
                    late_q_lo(t - 1)
                    late_poly(t - 1)
                soft_scores(t, u, j // 4)
                soft_att(t, u, first or second)
                if late:
                    late_slots(t - 1)
                if not last:
                    x_lo(t + 1, 1 - u, 0)
                    x_lo(t + 1, 1 - u, 1)
                att_lo(t)
                if late:
                    late_learned(t - 1, 1 - u)
                if ahead:
                    moments_of(t + 2, u, j + 1, (0, 1))
                if not last:
                    x_lo(t + 1, 1 - u, 2)
                if ahead:
                    moments_of(t + 2, u, j + 1, (2, 3))
                    moments(t + 2, u)
                if not last:
                    x_lo(t + 1, 1 - u, 3)
                if late:
                    late_z(t - 1)

            dve.tensor_scalar(keep["cov_scale"][:], keep["tgx"][:], 2.0 / D, None, ALU.mult)
            for t in range(2):
                moments_of(t, t, 0, range(4))
                moments(t, t)
            for g in range(G):
                x_lo(0, 0, g)
            tile(0, 0, 0, late=False, first=True)
            tile(1, 1, 0, second=True)
            with dve.Fori(1, PAIRS - 1) as j:
                for u in range(2):
                    tile(2 * j + u, u, j)
            tile(TILES - 2, 0, PAIRS - 1, ahead=False)
            tile(TILES - 1, 1, PAIRS - 1, ahead=False, last=True)
            t, u = TILES - 1, 1
            late_stats(t, u, BATCH - 1, False)
            late_scale(t, u)
            late_q_lo(t)
            late_poly(t)
            late_slots(t)
            late_learned(t, u)
            late_z(t)


def gate_block(nc, keep):
    with ExitStack() as ctx:
        m = Memory(nc, ctx, "gt")
        st, tgx, tgf = keep["stats"], keep["tgx"], keep["tgf"]
        mean, var, rstd, learned = (st[:, :, k] for k in range(4))
        t = {n: m.sb(n, [P, TILES]) for n in ("ve", "ratio", "one_plus", "flat", "dist", "log", "th", "u", "gate")}
        total, rowsum, half_bu2, half_gb = (m.sb("mean_log", [P, 1]), m.sb("row_sum", [P, 1]),
                                            m.sb("half_bu2", [P, 1]), m.sb("half_bias", [P, 1]))
        ps = m.ps("total")
        ready, logged, summed, unit, squashed, gated = (m.sem("ready"), m.sem("logged"), m.sem("summed"),
                                                        m.sem("unit"), m.sem("squashed"), m.sem("gated"))
        all_summed = m.sem("all_summed")
        block = ctx.enter_context(nc.Block())

        @block.vector
        def _(dve):
            def op(f, *args, **kw):
                ins = f(*args, **kw)
                dve.drain()
                return ins

            op(dve.tensor_scalar, half_bu2[:], keep["bu2"][:], 0.5, None, ALU.mult)
            op(dve.tensor_scalar, half_gb[:], keep["gb"][:], 0.5, None, ALU.mult)
            op(dve.tensor_scalar, t["ve"][:], var, EPS, None, ALU.add)
            op(dve.reciprocal, t["ve"][:], t["ve"][:])
            op(dve.tensor_tensor, t["ratio"][:], t["ve"][:], var, ALU.mult)
            dve.tensor_scalar(t["one_plus"][:], t["ratio"][:], 1.0, None, ALU.add).then_inc(ready, 1)
            dve.drain()
            op(dve.tensor_scalar, t["dist"][:], t["one_plus"][:], 1.0, None, ALU.subtract)
            op(dve.tensor_scalar, t["flat"][:], t["dist"][:], 0.0, None, ALU.is_equal)
            op(dve.tensor_tensor, t["dist"][:], t["dist"][:], t["flat"][:], ALU.add)
            op(dve.reciprocal, t["dist"][:], t["dist"][:])
            op(dve.tensor_tensor, t["ratio"][:], t["ratio"][:], t["dist"][:], ALU.mult)
            dve.wait_ge(logged, 1)
            op(dve.tensor_tensor, t["log"][:], t["log"][:], t["flat"][:], ALU.add)
            op(dve.tensor_tensor, t["log"][:], t["log"][:], t["ratio"][:], ALU.mult)
            dve.tensor_reduce(rowsum[:], t["log"][:], AX.X, ALU.add).then_inc(summed, 1)
            dve.wait_ge(all_summed, 1)
            op(dve.tensor_scalar, total[:], ps[:, 0:1], 1.0 / (TILES * P), 1.0e-6, ALU.mult, ALU.add)
            op(dve.reciprocal, total[:], total[:])
            op(dve.tensor_scalar, t["log"][:], t["log"][:], total[:, 0:1], 0.5, ALU.mult, ALU.mult)
            dve.wait_ge(unit, 1)
            op(dve.tensor_scalar, t["u"][:], t["th"][:], 1.25, 1.25, ALU.mult, ALU.add)
            op(dve.tensor_tensor, t["u"][:], t["u"][:], t["log"][:], ALU.add)
            op(dve.tensor_scalar, t["u"][:], t["u"][:], 0.0, 5.0, ALU.max, ALU.min)
            op(dve.tensor_scalar, t["u"][:], t["u"][:], -TAU_LOW, 1.0 / (TAU_HIGH - TAU_LOW), ALU.add, ALU.mult)
            op(dve.tensor_scalar, t["u"][:], t["u"][:], 0.0, 1.0, ALU.max, ALU.min)
            dve.tensor_scalar(t["u"][:], t["u"][:], keep["w1"][:, 0:1], keep["gb"][:, 0:1], ALU.mult,
                              ALU.add).then_inc(squashed, 1)
            dve.wait_ge(gated, 1)
            op(dve.tensor_scalar, t["gate"][:], t["gate"][:], 0.5, 0.5, ALU.mult, ALU.add)
            op(dve.tensor_scalar, t["u"][:], t["gate"][:], EARLY_EXIT, None, ALU.is_ge)
            op(dve.tensor_tensor, t["gate"][:], t["gate"][:], t["u"][:], ALU.mult)
            op(dve.tensor_scalar, keep["f_z"][:], t["gate"][:], tgf[:, 0:1], None, ALU.mult)
            op(dve.tensor_scalar, t["u"][:], rstd, tgf[:, 0:1], None, ALU.mult)
            op(dve.tensor_scalar, keep["f_x"][:], t["u"][:], 1.0, None, ALU.add)
            op(dve.tensor_tensor, t["u"][:], t["u"][:], mean, ALU.mult)
            op(dve.tensor_scalar, keep["f_0"][:], t["u"][:], -1.0, None, ALU.mult)
            op(dve.tensor_scalar, keep["f_att"][:], keep["f_x"][:], tgx[:, 0:1], None, ALU.mult)

        @block.scalar
        def _(act):
            act.wait_ge(ready, 1)
            act.activation(t["log"][:], t["one_plus"][:], ACT.Ln).then_inc(logged, 1)
            act.activation(t["th"][:], learned, ACT.Tanh, bias=half_bu2[:, 0:1], scale=0.5).then_inc(unit, 1)
            act.wait_ge(squashed, 1)
            act.activation(t["gate"][:], t["u"][:], ACT.Tanh, scale=0.5).then_inc(gated, 1)

        @block.tensor
        def _(pe):
            pe.wait_ge(summed, 1)
            pe.matmul(ps[:, 0:1], keep["ones"][:], rowsum[:], start=True, stop=True).then_inc(all_summed, 1)


def output_block(nc, io, keep):
    with ExitStack() as ctx:
        m = Memory(nc, ctx, "ob")
        ident = keep["ident"]
        (ctx1, ctx2), wvu = keep["ctx_out"], keep["wvu_out"]
        RING = 4
        x = keep["rows"] + [m.sb(f"x{s}", [P, D]) for s in range(2, RING)]
        az = [m.sb(f"att_z{u}", [P, 2 * P]) for u in range(2)]
        azT = [m.sb(f"att_z_turned{u}", [P, 2 * P], F32R) for u in range(2)]
        zl = [m.sb(f"z_low{u}", [P, P], F32R) for u in range(2)]
        turn_ps = [m.ps(f"turned{u}") for u in range(2)]
        po = [m.ps(f"out{n}") for n in range(4)]
        x_in = keep["out_x_in"]
        stored = [m.sem(f"stored{s}") for s in range(RING)]
        S = {n: m.sem(n) for n in ("scaled", "turned", "hi", "lo", "affine", "summed", "added")}
        block = ctx.enter_context(nc.Block())
        xout = io["out"].rearrange("(t p) d -> t p d", p=P)
        LAST = TILES // RING - 1

        @block.sync
        def _(sp):
            for s in range(2, RING):
                load_x(sp, io, x, x_in, s, s)
            with sp.Fori(1, LAST + 1) as j:
                for s in range(RING):
                    sp.wait_ge(stored[s], 16 * j)
                    load_x(sp, io, x, x_in, RING * j + s, s)

        @block.tensor
        def _(pe):
            def turn(t, u):
                pe.wait_ge(S["scaled"], t + 1)
                pe.transpose(turn_ps[u][:, 0:P], az[u][:, 0:P], ident[:])
                pe.transpose(turn_ps[u][:, P:2 * P], az[u][:, P:2 * P], ident[:]).then_inc(S["turned"], 1)

            def chunk(t, u, n, b, first):
                if not first:
                    pe.wait_ge(S["added"], 4 * t + n - 3)
                cols = slice(n * QN, (n + 1) * QN)
                c1 = ctx1[:, bass.ds(b, 1), cols].rearrange("p o n -> p (o n)")
                c2 = ctx2[0:NCTX, bass.ds(b, 1), cols].rearrange("p o n -> p (o n)")
                pe.matmul(po[n][:], azT[u][:, 0:P], c1, start=True, stop=False)
                pe.matmul(po[n][:], azT[u][0:NCTX, 0:P], c2, start=False, stop=False)
                split_product(pe, po[n][:], (azT[u][:, P:2 * P], zl[u][:]), (wvu[0][:, cols], wvu[1][:, cols]),
                              False, True).then_inc(S["summed"], 1)

            def body(j, first=False, last=False):
                for s in range(RING):
                    t, u = RING * j + s, s % 2
                    pe.wait_ge(S["lo"], t + 1)
                    for n in range(4):
                        chunk(t, u, n, j // 2, first and s == 0)
                        if n == 1 and not (last and s == RING - 1):
                            turn(t + 1, 1 - u)

            pe.wait_ge(keep["wvu_in"], 32)
            pe.wait_ge(keep["ctx_in"][0], 48)
            turn(0, 0)
            body(0, first=True)
            for b in range(1, BATCH):
                pe.wait_ge(keep["ctx_in"][b], 48)
            with pe.Fori(1, LAST) as j:
                body(j)
            body(LAST, last=True)

        @block.scalar
        def _(act):
            def hi(t, u):
                act.wait_ge(S["turned"], t + 1)
                act.activation(azT[u][:], turn_ps[u][:, 0:2 * P], ACT.Copy).then_inc(S["hi"], 1)

            def affine(t, s, j):
                act.wait_ge(x_in[s], 16 * j + 16)
                act.activation(x[s][:], x[s][:], ACT.Identity, bias=keep["f_0"][:, bass.ds(t, 1)],
                               scale=keep["f_x"][:, bass.ds(t, 1)]).then_inc(S["affine"], 1)

            def store(t, s):
                act.wait_ge(S["added"], 4 * t + 4)
                act.dma_start(xout[bass.ds(t, 1)].rearrange("o p d -> p (o d)"), x[s][:]).then_inc(stored[s], 16)

            def body(j, last=False):
                for s in range(RING):
                    t = RING * j + s
                    if not (last and s == RING - 1):
                        hi(t + 1, 1 - s % 2)
                        affine(t + 1, (s + 1) % RING, j + (s + 1) // RING)
                    store(t, s)

            hi(0, 0)
            affine(0, 0, 0)
            with act.Fori(0, LAST) as j:
                body(j)
            body(LAST, last=True)
            for s in range(RING):
                act.wait_ge(stored[s], 16 * (LAST + 1))

        @block.vector
        def _(dve):
            def scale(t, u):
                f_att, f_z = keep["f_att"][:, bass.ds(t, 1)], keep["f_z"][:, bass.ds(t, 1)]
                for half in range(2):
                    dve.tensor_scalar(az[u][:, half * NCTX:(half + 1) * NCTX], at(keep["att"], t), f_att, None,
                                      ALU.mult)
                dve.tensor_scalar(az[u][:, P:2 * P], at(keep["z"], t), f_z, None, ALU.mult).then_inc(S["scaled"], 1)

            def lo(t, u):
                dve.wait_ge(S["hi"], t + 1)
                dve.tensor_tensor(azT[u][NCTX:P, 0:P], turn_ps[u][NCTX:P, 0:P], f32(azT[u][NCTX:P, 0:P]),
                                  ALU.subtract)
                dve.tensor_tensor(zl[u][:], turn_ps[u][:, P:2 * P], f32(azT[u][:, P:2 * P]),
                                  ALU.subtract).then_inc(S["lo"], 1)

            def add(t, s, n):
                dve.wait_ge(S["summed"], 4 * t + n + 1)
                if n == 0:
                    dve.wait_ge(S["affine"], t + 1)
                cols = slice(n * QN, (n + 1) * QN)
                dve.tensor_tensor(x[s][:, cols], x[s][:, cols], po[n][:], ALU.add).then_inc(S["added"], 1)

            def body(j, last=False):
                for s in range(RING):
                    t, ahead = RING * j + s, not (last and s == RING - 1)
                    if ahead:
                        scale(t + 1, 1 - s % 2)
                    add(t, s, 0)
                    add(t, s, 1)
                    if ahead:
                        lo(t + 1, 1 - s % 2)
                    add(t, s, 2)
                    add(t, s, 3)

            scale(0, 0)
            lo(0, 0)
            with dve.Fori(0, LAST) as j:
                body(j)
            body(LAST, last=True)


def gated_cross_attention_and_memory(nc, io):
    scr = {
        "x": nc.dram_tensor("scratch_b", [BATCH, 2, P, KC, 2 * NCTX], F32).ap(),
        "cw": nc.dram_tensor("scratch_cw", [2, CR, CWN], F32).ap(),
        "ctx": nc.dram_tensor("scratch_ctx", [2, CR, D], F32).ap(),
        "wvu": nc.dram_tensor("scratch_wvu", [2, P, D], F32).ap(),
    }
    with ExitStack() as outer:
        m = Memory(nc, outer, "k")
        keep = {
            "ident": m.sb("ident", [P, P]), "ones": m.sb("ones", [P, P]),
            "mu_all": m.sb("mu_all", [P, CR]), "mu_scaled": m.sb("mu_scaled", [P, BATCH, NCTX]),
            "bq_rows": m.sb("bq_rows", [P, BATCH, NCTX]), "bias_cols": m.sb("bias_cols", [P, 2 * KC]),
            "stats": m.sb("stats", [P, TILES, 4]),
            "att": m.sb("att", [P, TILES, NCTX]), "z": m.sb("z", [P, TILES, VB]),
            "rows": [m.sb(f"rows{u}", [P, D]) for u in range(2)],
            "Z": [m.sb(f"turned{i}", [P, KC * CR], F32R) for i in range(2)],
        }
        keep["ctxT"] = [z[:].rearrange("p (c n) -> p c n", n=CR) for z in keep["Z"]]
        for n in ("tgx", "tgf", "w1", "gb", "bu2", "minus_half", "eps", "cov_scale"):
            keep[n] = m.sb(n, [P, 1])
        for n in ("f_x", "f_0", "f_att", "f_z"):
            keep[n] = m.sb(n, [P, TILES])
        for n in ("ctx_stored", "cent_out", "b_in", "wvu_in"):
            keep[n] = m.sem(n)
        for n, count in (("wq_in", 2), ("ffn_in", 2), ("x_in", 2), ("mt_out", 2), ("ctx_in", BATCH), ("out_x_in", 4)):
            keep[n] = [m.sem(f"{n}{i}") for i in range(count)]
        with ExitStack() as first:
            m = Memory(nc, first, "a")
            keep["ctx_rows"] = [m.sb(f"ctx_rows{r}", [P, D]) for r in range(2)]
            keep["ctx_hi"] = [m.sb(f"ctx_hi{r}", [P, D], F32R) for r in range(2)]
            keep["KT"] = [m.sb(f"KT{i}", [P, KC, CR], F32R) for i in range(2)]
            keep["T"] = [[m.sb(f"T{u}{i}", [P, KC, P], F32R) for i in range(2)] for u in range(2)]
            keys_block(nc, io, scr, keep)
            score_weights_block(nc, io, scr, keep)
        with ExitStack() as second:
            m = Memory(nc, second, "b")
            W = keep["weights"] = [m.sb(f"weights{i}", [P, KC * (BW + UB)], F32R) for i in range(2)]
            keep["bw"] = [w[:, 0:KC * BW].rearrange("p (c n) -> p c n", n=BW) for w in W]
            keep["wu"] = [w[:, KC * BW:KC * (BW + UB)].rearrange("p (c n) -> p c n", n=UB) for w in W]
            keep["ctx_out"] = [w[:, 0:BATCH * D].rearrange("p (b d) -> p b d", d=D) for w in W]
            keep["wvu_out"] = [w[:, BATCH * D:(BATCH + 1) * D] for w in W]
            with ExitStack() as third:
                m = Memory(nc, third, "c")
                keep["rs1"] = m.sb("slots_hi", [P, 2 * NSLOT], F32R)
                keep["rs2"] = m.sb("slots_lo", [BOT + 2, 2 * NSLOT], F32R)
                keep["q2s"] = m.sb("query_ones", [BOT + 2, P], F32R)
                keep["av"] = m.sb("av", [P, 4, VB])
                keep["bu1"], keep["wu2"] = m.sb("bu1", [P, HU]), m.sb("wu2", [P, HU])
                ffn_block(nc, io, scr, keep)
                context_weights_block(nc, scr, keep)
                token_block(nc, io, scr, keep)
            gate_block(nc, keep)
            output_block(nc, io, keep)


_INS = {"x": "x", "ctx_4096": "ctx", "g_xattn": "g_xattn", "g_ffn": "g_ffn", "L0_xattn_Wq": "Wq",
        "L0_xattn_bq": "bq", "L0_xattn_Wk": "Wk", "L0_xattn_bk": "bk", "L0_ffn_Wq": "fWq", "L0_ffn_Wr": "Wr",
        "L0_ffn_aux_keys": "aux_keys", "L0_ffn_aux_values": "aux_values", "L0_ffn_Wvd": "Wvd",
        "L0_ffn_Wvu": "Wvu", "L0_ffn_Wu1": "Wu1", "L0_ffn_bu1": "bu1", "L0_ffn_Wu2": "wu2",
        "L0_ffn_bu2": "bu2", "L0_ffn_gate_w1": "gate_w1", "L0_ffn_gate_bias": "gate_bias",
        "L0_ffn_log_rel": "log_rel"}
_SHAPES = {"x": (BATCH * SEQ, D), "ctx": (CR, D), "g_xattn": (1, 1), "g_ffn": (1, 1), "bu2": (1, 1),
           "gate_w1": (1, 1), "gate_bias": (1, 1), "wu2": (HU,)}


def kernel(**inputs):
    import numpy as _np
    import concourse.bacc as _bacc
    from concourse import mybir as _mybir
    from concourse.bass_utils import run_bass_kernel_spmd as _run

    nc = _bacc.Bacc("TRN2", target_bir_lowering=False, num_devices=1)
    arrays, io = {}, {}
    for name, short in _INS.items():
        a = _np.ascontiguousarray(inputs[name])
        if short in _SHAPES:
            a = a.reshape(_SHAPES[short])
        arrays[f"in_{short}_dram"] = a
        io[short] = nc.dram_tensor(f"in_{short}_dram", a.shape, _mybir.dt.from_np(a.dtype), kind="ExternalInput").ap()
    io["out"] = nc.dram_tensor("out_0_dram", (BATCH * SEQ, D), F32, kind="ExternalOutput").ap()
    gated_cross_attention_and_memory(nc, io)
    r = _run(nc, [arrays], core_ids=[0])
    return r.results[0]["out_0_dram"].reshape(BATCH, SEQ, D)
```

```python
from contextlib import ExitStack

import concourse.bass as bass
from concourse import mybir

P = 128
D = 2048
KC = D // P
BATCH, SEQ, NCTX = 4, 1024, 64
TILES = BATCH * SEQ // P
PAIRS = TILES // 2
CR = BATCH * NCTX
HU = 512
BOT, RDIM, NSLOT, VB, TOPK = 64, 48, 512, 128, 8
QN = 512
GROUPS = KC // 4
UA = 128
UB = HU - UA
QC = 2 * NCTX
BW = QC + BOT + UA
CWN = NCTX + BOT + HU
FFN_RING = 4
OUT_RING = 6
EPS = 1e-5
TAU_LOW, TAU_HIGH, EARLY_EXIT = 0.5, 2.0, 0.05
ATT_SCALE = 1.0 / float(D) ** 0.5
OUT_OF_RANGE = -1.0e30
PICKED = 1.0e30

ALU = mybir.AluOpType
ACT = mybir.ActivationFunctionType
AX = mybir.AxisListType
F32 = mybir.dt.float32
F32R = mybir.dt.float32r


def f32(ap):
    return ap.bitcast(F32)


def split_product(pe, out, left, right, start, stop, skip=False):
    (lh, ll), (rh, rl) = left, right
    pe.matmul(out, lh, rh, start=start, stop=False, skip_group_check=skip)
    pe.matmul(out, lh, rl, start=False, stop=False, skip_group_check=skip)
    return pe.matmul(out, ll, rh, start=False, stop=stop, skip_group_check=skip)


def at(t, i):
    return t[:, bass.ds(i, 1), :].rearrange("p o n -> p (o n)")


class Memory:

    def __init__(self, nc, ctx, tag):
        self.nc, self.ctx, self.tag = nc, ctx, tag

    def sb(self, name, shape, dt=F32):
        return self.ctx.enter_context(self.nc.sbuf_tensor(f"{self.tag}_{name}", shape, dt))

    def ps(self, name, shape=(P, QN), dt=F32):
        return self.ctx.enter_context(self.nc.psum_tensor(f"{self.tag}_{name}", list(shape), dt))

    def sem(self, name):
        return self.ctx.enter_context(self.nc.semaphore(f"{self.tag}_{name}"))


def transpose_group(pe, bank, src, g, ident, rows=P):
    for k in range(4):
        c = 4 * g + k
        ins = pe.transpose(bank[:, k * rows:(k + 1) * rows], src[0:rows, c * P:(c + 1) * P],
                           ident[0:rows, 0:rows])
    return ins


def keys_block(nc, io, scr, keep):
    with ExitStack() as ctx:
        m = Memory(nc, ctx, "ky")
        rows, T, ctxT, KT = keep["rows"], keep["T"], keep["ctxT"], keep["KT"]
        ident, ones, bias = keep["ident"], keep["ones"], keep["bias_cols"]
        crow = [m.sb(f"ctx_rows{r}", [P, D]) for r in range(2)]
        raw = m.sb("bias_rows", [2 * KC, P])
        stats = [m.sb(f"stats{r}", [P, 4, 6]) for r in range(2)]
        mv = [m.sb(f"mv{r}", [P, 2]) for r in range(2)]
        diag = [m.sb(f"diag{r}", [P, P]) for r in range(2)]
        kf = [m.sb(f"key_f32_{u}", [P, CR]) for u in range(2)]
        dot = m.sb("bq_dot", [P, CR])
        bank = [m.ps(f"bank{i}") for i in range(GROUPS)]
        kp = [m.ps(f"keys{u}") for u in range(2)]
        ps_small = m.ps("small")
        ps_row, ps_mu, ps_bias = ps_small[:, 0:CR], ps_small[:, CR:2 * CR], ps_small[:, 0:2 * KC]
        quarter_in, rest_in = [m.sem(f"quarter_in{g}") for g in range(GROUPS)], m.sem("rest_in")
        small_in, ident_zero, ident_done = m.sem("small_in"), m.sem("ident_zero"), m.sem("ident_done")
        diag_done, mu_ready, bias_turned = m.sem("diag_done"), m.sem("mu_ready"), m.sem("bias_turned")
        gates_ready, next_hi, next_lo = m.sem("gates_ready"), m.sem("next_hi"), m.sem("next_lo")
        rows_in = [m.sem(f"rows_in{u}") for u in range(2)]
        next_in = keep["wq_in"]
        turned, hi_done, lo_done = m.sem("turned"), m.sem("hi_done"), m.sem("lo_done")
        product, biased, key_hi, key_lo = m.sem("product"), m.sem("biased"), m.sem("key_hi"), m.sem("key_lo")
        dot_done, row_done = m.sem("dot_done"), m.sem("row_done")
        block = ctx.enter_context(nc.Block())
        wk = io["Wk"].rearrange("(t p) d -> t p d", p=P)
        C = 2 * GROUPS

        def load(sp, n, u):
            sp.dma_start(rows[u][:], wk[bass.ds(n, 1)].rearrange("o p d -> p (o d)")).then_inc(rows_in[u], 16)

        @block.sync
        def _(sp):
            for g in range(GROUPS):
                sp.dma_start(crow[0][:, g * QN:(g + 1) * QN],
                             io["ctx"][0:P, g * QN:(g + 1) * QN]).then_inc(quarter_in[g], 16)
            sp.dma_start(crow[1][:], io["ctx"][P:2 * P, :]).then_inc(rest_in, 16)
            load(sp, 0, 0)
            sp.dma_start(raw[0:KC, :], io["bk"].rearrange("(c p) -> c p", p=P)).then_inc(small_in, 16)
            sp.dma_start(raw[KC:2 * KC, :], io["bq"].rearrange("(c p) -> c p", p=P)).then_inc(small_in, 16)
            for dst, src in (("tgx", "g_xattn"), ("tgf", "g_ffn"), ("w1", "gate_w1"), ("gb", "gate_bias"),
                             ("bu2", "bu2")):
                sp.dma_start(keep[dst][:], io[src].broadcast_to([P, 1])).then_inc(small_in, 16)
            load(sp, 1, 1)
            sp.dma_start(scr["ctx"], io["ctx"]).then_inc(keep["ctx_stored"], 16)
            with sp.Fori(1, KC // 2) as j:
                for u in range(2):
                    sp.wait_ge(turned, C + GROUPS * (2 * j + u - 1))
                    load(sp, 2 * j + u, u)
            for u in range(2):
                sp.wait_ge(turned, C + GROUPS * (KC + u - 1))
                load_wq(sp, io, rows, next_in, u, u)

        @block.gpsimd
        def _(pool):
            pool.memset(ident[:], 0.0).then_inc(ident_zero, 1)
            pool.memset(ones[:], 1.0).then_inc(ident_done, 1)
            pool.wait_ge(ident_zero, 1)
            pool.affine_select(out=ident[:], in_=ident[:], compare_op=ALU.not_equal, fill=1.0, base=0,
                               pattern=[[-1, P]], channel_multiplier=1).then_inc(ident_done, 1)

        @block.tensor
        def _(pe):
            pe.wait_ge(ident_done, 2)
            for n in range(C):
                pe.wait_ge(quarter_in[n] if n < GROUPS else rest_in, 16)
                if n >= GROUPS:
                    pe.wait_ge(lo_done, n - GROUPS + 1)
                transpose_group(pe, bank[n % GROUPS], crow[n // GROUPS], n % GROUPS, ident).then_inc(turned, 1)
            for g in range(GROUPS):
                if g == 0:
                    pe.wait_ge(rows_in[0], 16)
                pe.wait_ge(lo_done, C + g - GROUPS + 1)
                transpose_group(pe, bank[g], rows[0], g, ident).then_inc(turned, 1)
            pe.wait_ge(small_in, 16 * 7)
            pe.transpose(ps_bias[:, 0:2 * KC], raw[:], ident[0:2 * KC, 0:2 * KC]).then_inc(bias_turned, 1)

            def body(j, first=False, last=False):
                for u in range(2):
                    n = 2 * j + u
                    if not first:
                        pe.wait_ge(biased, n - 1)
                    for g in range(GROUPS):
                        pe.wait_ge(lo_done, C + GROUPS * n + g + 1)
                        for c in range(4 * g, 4 * g + 4):
                            ins = split_product(pe, kp[u][:, 0:CR], (T[u][0][:, c, :], T[u][1][:, c, :]),
                                                (ctxT[0][:, c, :], ctxT[1][:, c, :]), c == 0, c == KC - 1)
                        if g == GROUPS - 1:
                            ins.then_inc(product, 1)
                        if last and u == 1:
                            continue
                        if g == 0:
                            pe.wait_ge(rows_in[1 - u], 16 * (j + 1 + u))
                        transpose_group(pe, bank[g], rows[1 - u], g, ident).then_inc(turned, 1)

            body(0, first=True)
            pe.wait_ge(diag_done, 2)
            for r in range(2):
                ins = pe.matmul(ps_mu[:, r * P:(r + 1) * P], ones[:], diag[r][:], start=True, stop=True)
            ins.then_inc(mu_ready, 1)
            with pe.Fori(1, KC // 2 - 1) as j:
                body(j)
            body(KC // 2 - 1, last=True)
            pe.wait_ge(dot_done, KC)
            pe.matmul(ps_row[:, 0:CR], ones[:], dot[:], start=True, stop=True).then_inc(row_done, 1)

        def ctx_part(n, part):
            r, g = n // GROUPS, n % GROUPS
            return ctxT[part][:, 4 * g:4 * g + 4, r * P:(r + 1) * P]

        @block.scalar
        def _(act):
            def parts_hi(n, u):
                for g in range(GROUPS):
                    act.wait_ge(turned, C + GROUPS * n + g + 1)
                    act.activation(T[u][0][:, 4 * g:4 * g + 4, :],
                                   bank[g][:].rearrange("p (k n) -> p k n", k=4),
                                   ACT.Copy).then_inc(hi_done, 1)

            def key_parts(n, u):
                act.wait_ge(biased, n + 1)
                act.activation(KT[0][:, bass.ds(n, 1), :].rearrange("p o n -> p (o n)"), kf[u][:],
                               ACT.Copy).then_inc(key_hi, 1)

            def body(j, last=False):
                for u in range(2):
                    if not (last and u == 1):
                        parts_hi(2 * j + u + 1, 1 - u)
                    key_parts(2 * j + u, u)
                    if last and u == 0:
                        act.wait_ge(next_in[0], 16)
                        act.activation(T[0][0][:].rearrange("p c x -> p (c x)"), rows[0][:],
                                       ACT.Copy).then_inc(next_hi, 1)

            for n in range(C):
                act.wait_ge(turned, n + 1)
                act.activation(ctx_part(n, 0), bank[n % GROUPS][:].rearrange("p (k n) -> p k n", k=4),
                               ACT.Copy).then_inc(hi_done, 1)
            parts_hi(0, 0)
            act.wait_ge(small_in, 16 * 7)
            act.activation(keep["tgx"][:], keep["tgx"][:], ACT.Tanh).then_inc(gates_ready, 1)
            act.activation(keep["tgf"][:], keep["tgf"][:], ACT.Tanh).then_inc(gates_ready, 1)
            with act.Fori(0, KC // 2 - 1) as j:
                body(j)
            body(KC // 2 - 1, last=True)

        @block.vector
        def _(dve):
            def parts_lo(n, u):
                for g in range(GROUPS):
                    dve.wait_ge(hi_done, C + GROUPS * n + g + 1)
                    dve.tensor_tensor(T[u][1][:, 4 * g:4 * g + 4, :],
                                      bank[g][:].rearrange("p (k n) -> p k n", k=4),
                                      f32(T[u][0][:, 4 * g:4 * g + 4, :]), ALU.subtract).then_inc(lo_done, 1)

            def key_parts(n, u):
                dve.wait_ge(product, n + 1)
                dve.tensor_scalar(kf[u][:], kp[u][:, 0:CR], bias[:, bass.ds(n, 1)], None,
                                  ALU.add).then_inc(biased, 1)
                dve.drain()
                dve.scalar_tensor_tensor(dot[:], kf[u][:], bias[:, bass.ds(KC + n, 1)], dot[:],
                                         ALU.mult, ALU.add).then_inc(dot_done, 1)
                dve.wait_ge(key_hi, n + 1)
                hi = f32(KT[0][:, bass.ds(n, 1), :]).rearrange("p o n -> p (o n)")
                dve.tensor_tensor(KT[1][:, bass.ds(n, 1), :].rearrange("p o n -> p (o n)"), kf[u][:], hi,
                                  ALU.subtract).then_inc(key_lo, 1)

            def body(j, last=False):
                for u in range(2):
                    if not (last and u == 1):
                        parts_lo(2 * j + u + 1, 1 - u)
                    key_parts(2 * j + u, u)
                    if last and u == 0:
                        dve.wait_ge(next_hi, 1)
                        dve.tensor_tensor(T[0][1][:].rearrange("p c x -> p (c x)"), rows[0][:],
                                          f32(T[0][0][:]).rearrange("p c x -> p (c x)"),
                                          ALU.subtract).then_inc(next_lo, 1)

            dve.memset(dot[:], 0.0)
            for n in range(C):
                dve.wait_ge(hi_done, n + 1)
                dve.tensor_tensor(ctx_part(n, 1), bank[n % GROUPS][:].rearrange("p (k n) -> p k n", k=4),
                                  f32(ctx_part(n, 0)), ALU.subtract).then_inc(lo_done, 1)
            parts_lo(0, 0)
            dve.wait_ge(bias_turned, 1)
            dve.tensor_copy(bias[:], ps_bias[:, 0:2 * KC])
            for r in range(2):
                for k in range(4):
                    dve.bn_stats(stats[r][:, k, :], crow[r][:, k * QN:(k + 1) * QN])
                dve.drain()
                dve.bn_aggr(mv[r][:], stats[r][:])
                dve.drain()
                dve.tensor_scalar(diag[r][:], ident[:], mv[r][:, 0:1], None, ALU.mult).then_inc(diag_done, 1)
            body(0)
            dve.wait_ge(mu_ready, 1)
            dve.tensor_copy(keep["mu_all"][:], ps_mu[:, 0:CR])
            dve.wait_ge(gates_ready, 2)
            dve.tensor_scalar(keep["mu_scaled"][:].rearrange("p b n -> p (b n)"), ps_mu[:, 0:CR],
                              keep["tgx"][:, 0:1], None, ALU.mult)
            with dve.Fori(1, KC // 2 - 1) as j:
                body(j)
            body(KC // 2 - 1, last=True)
            dve.wait_ge(row_done, 1)
            dve.tensor_scalar(keep["bq_rows"][:].rearrange("p b n -> p (b n)"), ps_row[:, 0:CR],
                              ATT_SCALE, None, ALU.mult)


def load_wq(sp, io, rows, sems, n, u):
    wq = io["Wq"].rearrange("(c p) (t x) -> t p c x", p=P, x=P)
    sp.dma_start(rows[u][:].rearrange("p (c x) -> p c x", x=P),
                 wq[bass.ds(n, 1)].rearrange("o p c x -> p (o c) x")).then_inc(sems[u], 16)


def score_weights_block(nc, io, scr, keep):
    with ExitStack() as ctx:
        m = Memory(nc, ctx, "sw")
        rows, T, KT, ctxT = keep["rows"], keep["T"], keep["KT"], keep["ctxT"]
        cent = m.sb("ctx_centred", [P, KC, CR])
        shifted, summed, cent_hi, cent_lo = m.sem("shifted"), m.sem("summed"), m.sem("cent_hi"), m.sem("cent_lo")
        mp = [m.ps(f"mt{u}") for u in range(2)]
        out = keep["mt"]
        rows_in = keep["wq_in"]
        wq_rows = [r[:].rearrange("p (c x) -> p c x", x=P) for r in rows]
        hi_done, lo_done, product = m.sem("hi_done"), m.sem("lo_done"), m.sem("product")
        out_hi, out_lo = m.sem("out_hi"), m.sem("out_lo")
        stored = keep["mt_out"]
        block = ctx.enter_context(nc.Block())

        def half(t, h):
            return t[:, h * KC // 2:(h + 1) * KC // 2, :]

        @block.sync
        def _(sp):
            def store(n, u):
                sp.wait_ge(out_lo, n + 1)
                for part in range(2):
                    sp.dma_start(scr["mt"][part, :, bass.ds(n, 1), :].rearrange("p o n -> p (o n)"),
                                 f32(out[u][part])).then_inc(stored[u], 16)

            def body(j, first=False):
                for u in range(2):
                    n = 2 * j + u
                    if not (first and u == 0):
                        sp.wait_ge(lo_done, 2 * (n - 2))
                    load_wq(sp, io, rows, rows_in, n, u)
                    if not (first and u == 0):
                        store(n - 3, 1 - u)

            body(1, first=True)
            with sp.Fori(2, KC // 2) as j:
                body(j)
            for n in range(2):
                load_ffn(sp, io, rows, keep["ffn_in"], n)
            store(KC - 3, 1)
            for u in range(2):
                sp.wait_ge(lo_done, 2 * (KC - 2 + u))
                load_ffn(sp, io, rows, keep["ffn_in"], 2 + u)
                store(KC - 2 + u, u)

        @block.gpsimd
        def _(pool):
            mean = keep["mu_all"][:].unsqueeze(1).broadcast_to([P, KC, CR])
            pool.tensor_tensor(cent[:], f32(ctxT[0][:]), mean, ALU.subtract).then_inc(shifted, 1)
            pool.wait_ge(shifted, 1)
            pool.tensor_tensor(cent[:], cent[:], f32(ctxT[1][:]), ALU.add).then_inc(summed, 1)
            for h in range(2):
                pool.wait_ge(cent_lo, h + 1)
                for part in range(2):
                    pool.dma_start(half(scr["cent"][part], h), f32(half(ctxT[part], h))).then_inc(keep["cent_out"], 16)

        @block.scalar
        def _(act):
            def weights_hi(n, u):
                act.wait_ge(rows_in[u], 8 * (n - u) + 16)
                for h in range(2):
                    act.activation(half(T[u][0], h), half(wq_rows[u], h), ACT.Copy).then_inc(hi_done, 1)

            def step(n, u, j, first=False, ahead=True):
                act.wait_ge(product, n + 1)
                if ahead:
                    weights_hi(n + 2, u)
                if not first:
                    act.wait_ge(stored[u], 32 * j)
                act.activation(out[u][0], mp[u][:, 0:CR], ACT.Copy).then_inc(out_hi, 1)

            weights_hi(1, 1)
            for u in range(2):
                step(u, u, 0, first=True)
            for u in range(2):
                step(2 + u, u, 1)
            act.wait_ge(summed, 1)
            for u in range(2):
                step(4 + u, u, 2)
                act.activation(half(ctxT[0], u), half(cent, u), ACT.Copy).then_inc(cent_hi, 1)
            with act.Fori(3, KC // 2 - 1) as j:
                for u in range(2):
                    step(2 * j + u, u, j)
            for u in range(2):
                step(KC - 2 + u, u, KC // 2 - 1, ahead=False)

        @block.vector
        def _(dve):
            def weights_lo(n, u):
                for h in range(2):
                    dve.wait_ge(hi_done, 2 * (n - 1) + h + 1)
                    dve.tensor_tensor(half(T[u][1], h), half(wq_rows[u], h), f32(half(T[u][0], h)),
                                      ALU.subtract).then_inc(lo_done, 1)

            def step(n, u, ahead=True):
                if ahead:
                    weights_lo(n + 2, u)
                dve.wait_ge(out_hi, n + 1)
                dve.tensor_tensor(out[u][1], mp[u][:, 0:CR], f32(out[u][0]), ALU.subtract).then_inc(out_lo, 1)

            weights_lo(1, 1)
            for n in range(4):
                step(n, n % 2)
            for u in range(2):
                step(4 + u, u)
                dve.wait_ge(cent_hi, u + 1)
                dve.tensor_tensor(half(ctxT[1], u), half(cent, u), f32(half(ctxT[0], u)),
                                  ALU.subtract).then_inc(cent_lo, 1)
            with dve.Fori(3, KC // 2 - 1) as j:
                for u in range(2):
                    step(2 * j + u, u)
            for u in range(2):
                step(KC - 2 + u, u, ahead=False)

        @block.tensor
        def _(pe):
            def body(j, first=False):
                for u in range(2):
                    n = 2 * j + u
                    if not first:
                        pe.wait_ge(out_lo, n - 1)
                    for c in range(KC):
                        if c % (KC // 2) == 0 and not (first and u == 0):
                            pe.wait_ge(lo_done, 2 * (n - 1) + c // (KC // 2) + 1)
                        ins = split_product(pe, mp[u][:, 0:CR], (T[u][0][:, c, :], T[u][1][:, c, :]),
                                            (KT[0][:, c, :], KT[1][:, c, :]), c == 0, c == KC - 1)
                    ins.then_inc(product, 1)

            body(0, first=True)
            with pe.Fori(1, KC // 2) as j:
                body(j)


def ffn_jobs(io):
    av = io["aux_values"].rearrange("(t p) d -> t p d", p=P)
    wu1 = io["Wu1"].rearrange("(t p) d -> t p d", p=P)
    return ([(io["Wvd"], P), (None, P), (av[0], P), (av[1], P), (io["fWq"], BOT), (wu1[0], P), (av[2], P), (av[3], P)]
            + [(wu1[t], P) for t in range(1, 4)])


def ffn_buffer(n):
    return (n + 2) % FFN_RING


def load_ffn(sp, io, rows, sems, n):
    (src, r), u = ffn_jobs(io)[n], ffn_buffer(n)
    if src is None:
        sp.dma_start(rows[u][:].rearrange("p (c v) -> p c v", v=VB),
                     io["Wvu"].rearrange("(c p) v -> p c v", p=P)).then_inc(sems[u], 16)
    else:
        sp.dma_start(rows[u][0:r, :], src).then_inc(sems[u], 16)


def ffn_block(nc, io, scr, keep):
    with ExitStack() as ctx:
        m = Memory(nc, ctx, "fw")
        ident, W = keep["ident"], keep["weights"]
        rows = keep["rows"]
        bw, wu = keep["bw"], keep["wu"]
        wvd = [W[i][:, KC * BW:KC * BW + D].rearrange("p (c n) -> p c n", n=P) for i in range(2)]
        part = [W[i][:, KC * BW + D:KC * BW + 3 * D].rearrange("p (c n) -> p c n", n=2 * P) for i in range(2)]
        wr, ak, ak2 = m.sb("wr", [RDIM, BOT]), m.sb("aux_keys", [P, 4, BOT]), m.sb("aux_keys_twice", [P, 4, P])
        wrT, wr2 = m.sb("wr_turned", [BOT, RDIM]), m.sb("wr_twice", [RDIM, 2 * BOT])
        spare_z = keep["z"][:].rearrange("p t v -> p (t v)")
        gate2, akT8 = spare_z[:, 0:NSLOT], spare_z[:, NSLOT:2 * NSLOT]
        logr = keep["att"][:].rearrange("p t n -> p (t n)")[:, 0:2 * NSLOT]
        avT = keep["att"][:].rearrange("p t n -> p (t n)")[:, 2 * NSLOT:2 * NSLOT + 2 * P]
        akT, rkT = (spare_z[:, 2 * NSLOT + D + k * NSLOT:2 * NSLOT + D + (k + 1) * NSLOT] for k in range(2))
        wvuT = spare_z[:, 2 * NSLOT:2 * NSLOT + D].rearrange("p (c n) -> p c n", n=P)
        bank = [m.ps(f"bank{i}") for i in range(GROUPS)]
        ps_av, ps_small, ps_rk, ps_g = m.ps("av"), m.ps("small"), m.ps("rk"), m.ps("g")
        rows_in = keep["ffn_in"]
        small_in, late_in, wvu_stored = m.sem("small_in"), m.sem("late_in"), m.sem("wvu_stored")
        turned, hi_done, lo_done = m.sem("turned"), m.sem("hi_done"), m.sem("lo_done")
        product, av_out, av_turned, av_kept = m.sem("product"), m.sem("av_out"), m.sem("av_turned"), m.sem("av_kept")
        keys_turned, keys_out, wr_turned, wr_out = (m.sem("keys_turned"), m.sem("keys_out"),
                                                    m.sem("wr_turned"), m.sem("wr_out"))
        wr2_done, ak2_done = m.sem("wr2_done"), m.sem("ak2_done")
        rk_ready, rk_out, g_ready = m.sem("rk_ready"), m.sem("rk_out"), m.sem("g_ready")
        slot_f32, slot_hi = m.sem("slot_f32"), m.sem("slot_hi")
        rs1, rs2, q2s = keep["rs1"], keep["rs2"], keep["q2s"]
        block = ctx.enter_context(nc.Block())

        WVU = 1
        PRODUCTS = (4, 8)
        turned_av = [[part[i][:, :, u * P:(u + 1) * P] for i in range(2)] for u in range(2)]
        targets = [wvd, None] + turned_av + [[bw[i][:, :, QC:QC + BOT] for i in range(2)],
                                             [bw[i][:, :, QC + BOT:BW] for i in range(2)]]
        targets += turned_av + [[wu[i][:, :, t * P:(t + 1) * P] for i in range(2)] for t in range(3)]
        jobs = [(r, dst) for (_, r), dst in zip(ffn_jobs(io), targets)]

        @block.sync
        def _(sp):
            sp.dma_start(wr[:], io["Wr"]).then_inc(small_in, 16)
            sp.dma_start(ak[:], io["aux_keys"].rearrange("(t p) b -> p t b", p=P)).then_inc(small_in, 16)
            for half in range(2):
                sp.dma_start(logr[BOT:BOT + 2, half * NSLOT:(half + 1) * NSLOT],
                             io["log_rel"].rearrange("(a n) -> a n", a=1).broadcast_to([2, NSLOT])
                             ).then_inc(small_in, 16)
            for n in range(FFN_RING, len(jobs)):
                sp.wait_ge(turned, GROUPS * (n - FFN_RING + 1))
                load_ffn(sp, io, rows, rows_in, n)
            for n in ("bu1", "wu2"):
                sp.dma_start(keep[n][:], io[n].rearrange("(a n) -> a n", a=1).broadcast_to([P, HU])
                             ).then_inc(late_in, 16)
            sp.wait_ge(lo_done, GROUPS * (WVU + 1))
            sp.dma_start(scr["wvu"], wvuT.rearrange("p c n -> p (c n)")).then_inc(wvu_stored, 16)
            for u in (1, 0):
                last = max(n for n in range(len(jobs)) if ffn_buffer(n) == u)
                sp.wait_ge(turned, GROUPS * (last + 1))
                load_x(sp, io, rows, keep["x_in"], u, u)
            sp.wait_ge(wvu_stored, 16)

        @block.tensor
        def _(pe):
            def turn_values(k):
                pe.wait_ge(av_out, k + 1)
                if k:
                    pe.wait_ge(av_kept, k)
                for t in range(2):
                    ins = pe.transpose(ps_rk[:, t * P:(t + 1) * P], avT[:, t * P:(t + 1) * P], ident[:])
                ins.then_inc(av_turned, 1)

            for n, (r, _) in enumerate(jobs):
                pe.wait_ge(rows_in[ffn_buffer(n)], 16 * (n // FFN_RING + 1))
                for g in range(GROUPS):
                    if n:
                        pe.wait_ge(lo_done, GROUPS * (n - 1) + g + 1)
                    transpose_group(pe, bank[g], rows[ffn_buffer(n)], g, ident, r).then_inc(turned, 1)
                if n in PRODUCTS:
                    pe.wait_ge(lo_done, GROUPS * n)
                    for c in range(KC):
                        ins = split_product(pe, ps_av[:, 0:2 * P], (wvd[0][:, c, :], wvd[1][:, c, :]),
                                            (part[0][:, c, :], part[1][:, c, :]), c == 0, c == KC - 1)
                    ins.then_inc(product, 1)
                if n - 1 in PRODUCTS:
                    turn_values(PRODUCTS.index(n - 1))
                if n == 2:
                    pe.wait_ge(small_in, 16 * 4)
                    for t in range(4):
                        ins = pe.transpose(ps_small[0:BOT, t * P:(t + 1) * P], ak[:, t, :], ident[:])
                    ins.then_inc(keys_turned, 1)
                    pe.transpose(ps_g[0:BOT, 0:RDIM], wr[:], ident[0:RDIM, 0:RDIM]).then_inc(wr_turned, 1)
                if n == 3:
                    pe.wait_ge(keys_out, 1)
                    pe.wait_ge(wr_out, 1)
                    pe.matmul(ps_rk[0:RDIM, :], wrT[:], akT[0:BOT, :], start=True, stop=True).then_inc(rk_ready, 1)
                if n == 4:
                    pe.wait_ge(rk_out, 1)
                    pe.wait_ge(wr2_done, 1)
                    pe.matmul(ps_g[:], wr2[:], rkT[0:RDIM, :], start=True, stop=True).then_inc(g_ready, 1)
                    pe.wait_ge(ak2_done, 1)
                    for t in range(4):
                        ins = pe.transpose(ps_small[:, t * P:(t + 1) * P], ak2[:, t, :], ident[:])
                    ins.then_inc(keys_turned, 1)

        def high_parts(n):
            return GROUPS * (n - (n > WVU))

        @block.scalar
        def _(act):
            for n, (r, dst) in enumerate(jobs):
                if n == WVU:
                    continue
                if n == 6:
                    act.wait_ge(product, 1)
                if n == 8:
                    act.wait_ge(product, 2)
                for g in range(GROUPS):
                    act.wait_ge(turned, GROUPS * n + g + 1)
                    act.activation(dst[0][:, 4 * g:4 * g + 4, :],
                                   bank[g][:, 0:4 * r].rearrange("p (k n) -> p k n", k=4),
                                   ACT.Copy).then_inc(hi_done, 1)
                if n == 2:
                    act.wait_ge(small_in, 16 * 4)
                    act.activation(wr2[:, 0:BOT], wr[:], ACT.Copy)
                    act.activation(wr2[:, BOT:2 * BOT], wr[:], ACT.Copy).then_inc(wr2_done, 1)
                    act.activation(ak2[:, :, 0:BOT], ak[:], ACT.Copy, scale=0.125)
                    act.activation(ak2[:, :, BOT:2 * BOT], ak[:], ACT.Copy, scale=0.125).then_inc(ak2_done, 1)
                if n == 7:
                    act.wait_ge(slot_f32, 2)
                    act.activation(rs1[:, 0:NSLOT], gate2, ACT.Copy)
                    act.activation(rs1[:, NSLOT:2 * NSLOT], akT8, ACT.Copy)
                    act.activation(rs2[BOT:BOT + 2, :], logr[BOT:BOT + 2, :], ACT.Copy).then_inc(slot_hi, 1)

        @block.vector
        def _(dve):
            dve.memset(q2s[BOT:BOT + 2, :].bitcast(F32), 1.0)
            for n, (r, dst) in enumerate(jobs):
                for g in range(GROUPS):
                    turned_group = bank[g][:, 0:4 * r].rearrange("p (k n) -> p k n", k=4)
                    if n == WVU:
                        dve.wait_ge(turned, GROUPS * n + g + 1)
                        dve.tensor_copy(wvuT[:, 4 * g:4 * g + 4, :], turned_group).then_inc(lo_done, 1)
                    else:
                        dve.wait_ge(hi_done, high_parts(n) + g + 1)
                        dve.tensor_tensor(dst[1][:, 4 * g:4 * g + 4, :], turned_group,
                                          f32(dst[0][:, 4 * g:4 * g + 4, :]), ALU.subtract).then_inc(lo_done, 1)
                if n in PRODUCTS:
                    dve.wait_ge(product, PRODUCTS.index(n) + 1)
                    dve.tensor_copy(avT, ps_av[:, 0:2 * P]).then_inc(av_out, 1)
                if n - 1 in PRODUCTS:
                    k = PRODUCTS.index(n - 1)
                    dve.wait_ge(av_turned, k + 1)
                    dve.tensor_copy(keep["av"][:, 2 * k:2 * k + 2, :].rearrange("p t v -> p (t v)"),
                                    ps_rk[:, 0:2 * P]).then_inc(av_kept, 1)
                if n == 2:
                    dve.wait_ge(keys_turned, 1)
                    dve.tensor_copy(akT[0:BOT, :], ps_small[0:BOT, :]).then_inc(keys_out, 1)
                    dve.wait_ge(wr_turned, 1)
                    dve.tensor_copy(wrT[:], ps_g[0:BOT, 0:RDIM]).then_inc(wr_out, 1)
                if n == 3:
                    dve.wait_ge(rk_ready, 1)
                    dve.tensor_copy(rkT[0:RDIM, :], ps_rk[0:RDIM, :]).then_inc(rk_out, 1)
                if n == 4:
                    dve.wait_ge(g_ready, 1)
                    dve.tensor_scalar(gate2, ps_g[:], 1.0 / float(RDIM) ** 0.5, None, ALU.mult).then_inc(slot_f32, 1)
                    dve.wait_ge(keys_turned, 2)
                    dve.tensor_copy(akT8, ps_small[:]).then_inc(slot_f32, 1)
                if n == 7:
                    dve.wait_ge(slot_hi, 1)
                    dve.tensor_tensor(rs2[0:BOT, 0:NSLOT], gate2[0:BOT, :], f32(rs1[0:BOT, 0:NSLOT]), ALU.subtract)
                    dve.tensor_tensor(rs2[0:BOT, NSLOT:2 * NSLOT], akT8[0:BOT, :],
                                      f32(rs1[0:BOT, NSLOT:2 * NSLOT]), ALU.subtract)
                    dve.tensor_tensor(rs2[BOT:BOT + 1, :], logr[BOT:BOT + 1, :], f32(rs2[BOT:BOT + 1, :]),
                                      ALU.subtract)
            dve.wait_ge(late_in, 32)
            dve.tensor_scalar(keep["wu2"][:], keep["wu2"][:], 0.5, None, ALU.mult)


def load_x(sp, io, rows, sems, t, u):
    sp.dma_start(rows[u][:], io["x"].rearrange("(t p) d -> t p d", p=P)[bass.ds(t, 1)].rearrange("o p d -> p (o d)")
                 ).then_inc(sems[u], 16)


def join_batch_b(sp, scr, done, part, k):
    sp.dma_start(scr["b"][part, :, :, :, k, :],
                 scr[("mt", "cent")[k]][part].rearrange("p c (b n) -> p c b n", n=NCTX)).then_inc(done, 16)


def load_joined_b(sp, scr, keep, b):
    for part in range(2):
        sp.dma_start(f32(keep["bw"][part][:, :, 0:2 * NCTX]),
                     scr["b"][part, :, :, bass.ds(b, 1), :, :].rearrange("p c o k n -> p c (o k n)")
                     ).then_inc(keep["b_in"], 16)


def load_ctx(sp, scr, keep, b):
    sp.dma_start(f32(keep["ctx_out"][1][0:NCTX, b, :]),
                 scr["ctx"][b * NCTX:(b + 1) * NCTX, :]).then_inc(keep["ctx_in"][b], 16)


def context_high(act, keep, done, b, halves=(0, 1)):
    hi, raw = keep["ctx_out"]
    act.wait_ge(keep["ctx_in"][b], 16)
    for half in halves:
        act.activation(hi[half * NCTX:(half + 1) * NCTX, b, :], f32(raw[0:NCTX, b, :]), ACT.Copy).then_inc(done, 1)


def context_low(pool, keep, high_done, done, b):
    hi, raw = keep["ctx_out"]
    pool.wait_ge(high_done, 2 * (b + 1))
    pool.tensor_tensor(raw[0:NCTX, b, :], f32(raw[0:NCTX, b, :]), f32(hi[0:NCTX, b, :]), ALU.subtract).then_inc(done, 1)


def load_batch_b(sp, scr, keep, b):
    for part in range(2):
        for k, name in enumerate(("mt", "cent")):
            sp.dma_start(f32(keep["bw"][part][:, :, k * NCTX:(k + 1) * NCTX]),
                         scr[name][part, :, :, bass.ds(b * NCTX, NCTX)]).then_inc(keep["b_in"], 16)


def token_block(nc, io, scr, keep):
    with ExitStack() as ctx:
        m = Memory(nc, ctx, "tk")
        ident = keep["ident"]
        bw, wu, rs1, rs2, av = keep["bw"], keep["wu"], keep["rs1"], keep["rs2"], keep["av"]
        x = keep["rows"]
        xT = [tuple(z[:, i * D:(i + 1) * D].rearrange("p (c n) -> p c n", n=P) for i in range(2)) for z in keep["Z"]]
        cw1, cw2 = m.sb("cw_stack", [P, CWN], F32R), m.sb("cw_low", [NCTX, CWN], F32R)
        stats = m.sb("stats", [P, 4, 6])
        mv = [m.sb(f"mean_var{u}", [P, 2]) for u in range(2)]
        nmean = [m.sb(f"nmean{u}", [P, 1]) for u in range(2)]
        rstd1 = [m.sb(f"rstd1_{u}", [P, 1]) for u in range(2)]
        nscale = m.sb("neg_score_scale", [P, 1])
        neg_max = m.sb("neg_max", [P, 1])
        esum, einv = m.sb("exp_sum", [P, 1]), m.sb("exp_inv", [P, 1])
        hid, act1, hw, picked = (keep["rows"][2][:, k * HU:(k + 1) * HU] for k in range(4))
        ws, wT = (keep["rows"][3][:, k * NSLOT:(k + 1) * NSLOT] for k in range(2))
        rest = keep["rows"][3][:, 2 * NSLOT:D]
        q2, att2 = rest[:, 0:P], [rest[:, (k + 1) * P:(k + 2) * P] for k in range(2)]
        neg_s, e1, junk, junk2 = (rest[:, 3 * P + k * NCTX:3 * P + (k + 1) * NCTX] for k in range(4))
        attS = m.sb("att_stack", [P, P], F32R)
        shift = m.sb("mean_shift", [P, 1])
        mvk = [m.sb(f"mean_var_kept{u}", [P, 2]) for u in range(2)]
        st2 = [m.sb(f"stats2_{u}", [P, 4]) for u in range(2)]
        ve = m.sb("var_eps", [P, 1])
        ve1 = m.sb("var_eps1", [P, 1])
        qS = m.sb("query_stack", [P, P], F32R)
        q2s = keep["q2s"]
        top8, wmax, wneg = m.sb("top8", [P, TOPK]), m.sb("slot_max", [P, 1]), m.sb("slot_neg", [P, 1])
        wsum, winv = m.sb("slot_sum", [P, 1]), m.sb("slot_inv", [P, 1])
        bank = [m.ps(f"bank{i}") for i in range(2)]
        psA, psB = m.ps("hidden_sum"), [m.ps(f"b_sum{u}") for u in range(2)]
        psR, psS, psM = m.ps("router"), m.ps("slots"), m.ps("small")
        cT, tgx = keep["ctxT"], keep["tgx"]
        gram_ps, wide_ps = [psR, psM], [psS, psB[1]]
        spare_z = keep["z"][:].rearrange("p t v -> p (t v)")[:, TILES * VB - 4 * CWN:TILES * VB]
        cw, cw_lo = ([spare_z[:, (2 * k + r) * CWN:(2 * k + r + 1) * CWN] for r in range(2)] for k in range(2))
        cw_hi = keep["cw_hi"]
        att_turned_ps, q_turned_ps, z_ps = psM[:, 0:P], psM[:, P:2 * P], psM[:, 2 * P:2 * P + VB]

        S = {n: m.sem(n) for n in (
            "cw_product", "cw_scaled", "cw_high", "cw_low", "cw_stored", "cw_in", "joined", "turned", "x_hi",
            "x_lo", "b_sum", "c_sum", "centred",
            "mean_var", "rstd1", "neg_scores", "exp", "att", "att_turned", "att_hi", "att_lo",
            "var1", "rstd2", "query", "q_turned", "q_hi", "q_lo", "hidden", "routed", "slots",
            "slot_exp", "w_turned", "w_out", "z_sum", "z_out", "square", "inner", "tanh", "hw", "learned",
            "kept_att", "kept_stats", "poly", "half_bias", "ready", "logged", "log_summed", "all_summed", "unit",
            "squashed", "gated")}
        tgf, names = keep["tgf"], ("ve", "ratio", "one_plus", "flat", "dist", "log", "th", "u", "gate")
        mean, var, rstd, learned = (keep["stats"][:, :, k] for k in range(4))
        v = {n: hw[:, k * TILES:(k + 1) * TILES] for k, n in enumerate(names)}
        total, rowsum, half_bu2 = (hw[:, len(names) * TILES + k:len(names) * TILES + k + 1] for k in range(3))
        ps_total = psA
        x_in, b_in = keep["x_in"], keep["b_in"]
        block = ctx.enter_context(nc.Block())
        G = GROUPS

        def load_batch_cw(sp, b):
            for half in range(2):
                sp.dma_start(f32(cw1[half * NCTX:(half + 1) * NCTX, :]),
                             scr["cw"][0, bass.ds(b * NCTX, NCTX), :]).then_inc(S["cw_in"], 16)
            sp.dma_start(f32(cw2[:]), scr["cw"][1, bass.ds(b * NCTX, NCTX), :]).then_inc(S["cw_in"], 16)

        @block.sync
        def _(sp):
            for u in range(2):
                sp.wait_ge(keep["mt_out"][u], 32 * KC // 2)
            sp.wait_ge(keep["cent_out"], 16 * 4)
            load_batch_b(sp, scr, keep, 0)
            for r in range(2):
                sp.wait_ge(S["cw_low"], r + 1)
                for part, src in ((0, f32(cw_hi[r])), (1, cw_lo[r])):
                    sp.dma_start(scr["cw"][part, r * P:(r + 1) * P, :], src).then_inc(S["cw_stored"], 16)
                if r == 0:
                    sp.wait_ge(S["cw_stored"], 32)
                    load_batch_cw(sp, 0)
            for t in range(2, 8):
                sp.wait_ge(S["turned"], G * (t - 1))
                load_x(sp, io, x, x_in, t, t % 2)
                if t < 6:
                    join_batch_b(sp, scr, S["joined"], *divmod(t - 2, 2))
            sp.wait_ge(S["cw_stored"], 64)
            sp.wait_ge(S["joined"], 64)
            with sp.Fori(1, BATCH) as b:
                for k in range(8):
                    sp.wait_ge(S["turned"], G * (8 * b + k - 1))
                    load_x(sp, io, x, x_in, 8 * b + k, k % 2)
                    if k == 1:
                        sp.wait_ge(S["b_sum"], 8 * b)
                        load_joined_b(sp, scr, keep, b)
                        sp.wait_ge(S["c_sum"], 8 * b)
                        load_batch_cw(sp, b)
            for u in range(2):
                sp.wait_ge(S["turned"], G * (TILES + u - 1))
                load_x(sp, io, x, keep["out_x_in"], u, u)
            sp.wait_ge(S["c_sum"], TILES)
            sp.wait_ge(keep["ctx_stored"], 16)
            load_ctx(sp, scr, keep, 0)
            sp.dma_start(f32(keep["wvu_out"][1]), scr["wvu"]).then_inc(keep["wvu_in"], 16)
            for b in range(1, BATCH):
                load_ctx(sp, scr, keep, b)

        @block.tensor
        def _(pe):
            def turn_x(t, u, g, first=False):
                if not (first and g < 2):
                    pe.wait_ge(S["x_lo"], G * t + g - 1)
                transpose_group(pe, bank[g % 2], x[u], g, ident).then_inc(S["turned"], 1)

            def b_part(t, u, g):
                pe.wait_ge(S["x_lo"], G * t + g + 1)
                for c in range(4 * g, 4 * g + 4):
                    ins = split_product(pe, psB[u][:, 0:BW], (xT[u][0][:, c, :], xT[u][1][:, c, :]),
                                        (bw[0][:, c, :], bw[1][:, c, :]), c == 0, c == KC - 1, True)
                return ins

            def a_part(t, u, g, first):
                if g == 0 and not first:
                    pe.wait_ge(S["hidden"], t)
                for c in range(4 * g, 4 * g + 4):
                    split_product(pe, psA[:, 0:UB], (xT[u][0][:, c, :], xT[u][1][:, c, :]),
                                  (wu[0][:, c, :], wu[1][:, c, :]), c == 0, c == KC - 1, True)

            def late_query(t, first=False):
                pe.wait_ge(S["query"], t + 1)
                if not first:
                    pe.wait_ge(S["z_out"], t)
                pe.transpose(q_turned_ps, q2, ident[:]).then_inc(S["q_turned"], 1)

            def late_route(t, first):
                pe.wait_ge(S["q_lo"], t + 1)
                pe.wait_ge(S["q_hi"], t + 1)
                if not first:
                    pe.wait_ge(S["w_out"], t)
                    pe.wait_ge(S["slots"], t)
                for bank_, n in ((psR, 0), (psS, NSLOT)):
                    pe.matmul(bank_[:], qS[:], rs1[:, n:n + NSLOT], start=True, stop=False)
                    ins = pe.matmul(bank_[:], q2s[0:BOT + 2, :], rs2[:, n:n + NSLOT], start=False, stop=True)
                ins.then_inc(S["routed"], 1)

            def late_turn_w(t):
                pe.wait_ge(S["slot_exp"], t + 1)
                for k in range(4):
                    ins = pe.transpose(psR[:, k * P:(k + 1) * P], ws[:, k * P:(k + 1) * P], ident[:])
                ins.then_inc(S["w_turned"], 1)

            def late_z(t, more=True):
                pe.wait_ge(S["w_out"], t + 1)
                pe.wait_ge(S["att_lo"], t + 2 if more else t + 1)
                for k in range(4):
                    ins = pe.matmul(z_ps, wT[:, k * P:(k + 1) * P], av[:, k, :], start=(k == 0), stop=(k == 3))
                ins.then_inc(S["z_sum"], 1)

            def tile(t, u, late=True, late_first=False, first=False, last=False, second=False, j=None):
                pe.wait_ge(b_in, 32 * b_of(j) + 32)
                if not (first or second):
                    pe.wait_ge(S["hidden"], t - 1)
                b_part(t, u, 0)
                b_part(t, u, 1)
                if late:
                    late_query(t - 1, late_first)
                b_part(t, u, 2)
                b_part(t, u, 3).then_inc(S["b_sum"], 1)
                if late:
                    late_route(t - 1, late_first)
                a_part(t, u, 0, first)
                if not last:
                    pe.wait_ge(S["centred"], t + 2)
                    turn_x(t + 1, 1 - u, 0)
                a_part(t, u, 1, first)
                if not last:
                    turn_x(t + 1, 1 - u, 1)
                pe.wait_ge(S["att"], t + 1)
                if first:
                    pe.wait_ge(S["cw_scaled"], 2)
                pe.transpose(att_turned_ps, att2[u], ident[:]).then_inc(S["att_turned"], 1)
                a_part(t, u, 2, first)
                if not last:
                    turn_x(t + 1, 1 - u, 2)
                if late:
                    late_turn_w(t - 1)
                a_part(t, u, 3, first)
                if not last:
                    turn_x(t + 1, 1 - u, 3)
                if late:
                    late_z(t - 1)
                pe.wait_ge(S["cw_in"], 48 * b_of(j))
                pe.wait_ge(S["att_hi"], t + 1)
                pe.wait_ge(S["att_lo"], t + 1)
                for out, n0, n1 in ((psB[u][:, NCTX:BW], 0, CWN - UB), (psA[:, 0:UB], CWN - UB, CWN)):
                    pe.matmul(out, attS[:], cw1[:, n0:n1], start=False, stop=False, skip_group_check=True)
                    ins = pe.matmul(out, attS[0:NCTX, :], cw2[:, n0:n1], start=False, stop=True,
                                    skip_group_check=True)
                ins.then_inc(S["c_sum"], 1)

            def b_of(j):
                return j // 4 + 1

            def context_products(r):
                for c in range(KC):
                    left = tuple(cT[i][:, c, r * P:(r + 1) * P] for i in range(2))
                    split_product(pe, gram_ps[r][:, 0:P], left, left, c == 0, c == KC - 1, True)
                    split_product(pe, gram_ps[r][:, P:P + BOT + UA], left,
                                  (bw[0][:, c, QC:BW], bw[1][:, c, QC:BW]), False, c == KC - 1, True)
                    ins = split_product(pe, wide_ps[r][:, 0:UB], left, (wu[0][:, c, :], wu[1][:, c, :]), c == 0,
                                        c == KC - 1)
                ins.then_inc(S["cw_product"], 1)

            context_products(0)
            pe.wait_ge(S["centred"], 1)
            turn_x(0, 0, 0, first=True)
            turn_x(0, 0, 1, first=True)
            context_products(1)
            turn_x(0, 0, 2, first=True)
            turn_x(0, 0, 3, first=True)
            tile(0, 0, late=False, first=True, j=0)
            tile(1, 1, late_first=True, second=True, j=0)
            with pe.Fori(1, PAIRS - 1) as j:
                for u in range(2):
                    tile(2 * j + u, u, j=j)
            tile(TILES - 2, 0, j=PAIRS - 1)
            tile(TILES - 1, 1, j=PAIRS - 1, last=True)
            late_query(TILES - 1)
            late_route(TILES - 1, False)
            late_turn_w(TILES - 1)
            late_z(TILES - 1, more=False)
            pe.wait_ge(S["log_summed"], 1)
            pe.matmul(ps_total[:, 0:1], keep["ones"][:], rowsum, start=True, stop=True).then_inc(S["all_summed"], 1)

        @block.scalar
        def _(act):
            def centre(t, u):
                act.wait_ge(S["mean_var"], t + 1)
                act.activation(x[u][:], x[u][:], ACT.Identity, bias=nmean[u][:, 0:1]).then_inc(S["centred"], 1)

            def x_hi(t, u, g):
                act.wait_ge(S["turned"], G * t + g + 1)
                act.activation(xT[u][0][:, 4 * g:4 * g + 4, :], bank[g % 2][:].rearrange("p (k n) -> p k n", k=4),
                               ACT.Copy).then_inc(S["x_hi"], 1)

            def soft(t):
                act.wait_ge(S["neg_scores"], t + 1)
                act.activation(e1, neg_s, ACT.Exp, bias=neg_max[:, 0:1], scale=-1.0,
                               accum_out=esum[:]).then_inc(S["exp"], 1)

            def late_square(t):
                act.wait_ge(S["hidden"], t + 1)
                act.activation(act1, hid, ACT.Square).then_inc(S["square"], 1)

            def late_q_hi(t, first):
                act.wait_ge(S["q_turned"], t + 1)
                if not first:
                    act.wait_ge(S["routed"], t)
                act.activation(qS[:], q_turned_ps, ACT.Copy)
                act.activation(q2s[0:BOT, :], q_turned_ps[0:BOT, :], ACT.Copy).then_inc(S["q_hi"], 1)

            def att_hi(t):
                act.wait_ge(S["att_turned"], t + 1)
                act.activation(attS[:], att_turned_ps, ACT.Copy).then_inc(S["att_hi"], 1)

            def late_exp(t):
                act.wait_ge(S["slots"], t + 1)
                act.activation(ws, ws, ACT.Exp, bias=wneg[:, 0:1], accum_out=wsum[:]).then_inc(S["slot_exp"], 1)

            def late_w_out(t, first):
                act.wait_ge(S["w_turned"], t + 1)
                if not first:
                    act.wait_ge(S["z_sum"], t)
                act.activation(wT, psR[:], ACT.Copy).then_inc(S["w_out"], 1)

            def late_tanh(t):
                act.wait_ge(S["inner"], t + 1)
                act.activation(act1, act1, ACT.Tanh, scale=0.7978845608028654).then_inc(S["tanh"], 1)

            def tile(t, u, late=True, late_first=False, last=False, ahead=True):
                if late:
                    late_square(t - 1)
                    late_q_hi(t - 1, late_first)
                soft(t)
                if late:
                    late_tanh(t - 1)
                if not last:
                    x_hi(t + 1, 1 - u, 0)
                if late:
                    late_exp(t - 1)
                if not last:
                    x_hi(t + 1, 1 - u, 1)
                att_hi(t)
                if not last:
                    x_hi(t + 1, 1 - u, 2)
                if late:
                    late_w_out(t - 1, late_first)
                if not last:
                    x_hi(t + 1, 1 - u, 3)
                if ahead:
                    centre(t + 2, u)

            def context_hi(r):
                act.wait_ge(S["cw_scaled"], r + 1)
                act.activation(cw_hi[r], cw[r], ACT.Copy).then_inc(S["cw_high"], 1)

            for t in range(2):
                centre(t, t)
            context_hi(0)
            act.wait_ge(S["cw_product"], 2)
            for g in range(G):
                x_hi(0, 0, g)
            context_hi(1)
            tile(0, 0, late=False)
            tile(1, 1, late_first=True)
            with act.Fori(1, PAIRS - 1) as j:
                for u in range(2):
                    tile(2 * j + u, u)
            tile(TILES - 2, 0, ahead=False)
            tile(TILES - 1, 1, last=True, ahead=False)
            t = TILES - 1
            late_square(t)
            late_q_hi(t, False)
            late_tanh(t)
            context_high(act, keep, keep["ctx_hi"], 0, (0,))
            late_exp(t)
            context_high(act, keep, keep["ctx_hi"], 0, (1,))
            late_w_out(t, False)
            act.wait_ge(S["ready"], 1)
            act.activation(v["log"], v["one_plus"], ACT.Ln).then_inc(S["logged"], 1)
            act.wait_ge(S["half_bias"], 1)
            act.activation(v["th"], learned, ACT.Tanh, bias=half_bu2, scale=0.5).then_inc(S["unit"], 1)
            act.wait_ge(keep["wvu_in"], 16)
            act.activation(keep["wvu_out"][0], f32(keep["wvu_out"][1]), ACT.Copy).then_inc(keep["wvu_hi"], 1)
            act.wait_ge(S["squashed"], 1)
            act.activation(v["gate"], v["u"], ACT.Tanh, scale=0.5).then_inc(S["gated"], 1)

        @block.gpsimd
        def _(pool):
            def power(out, in_, tmp):
                pool.tensor_tensor(tmp, in_, keep["eps"][:], ALU.add)
                pool.drain()
                return pool.tensor_tensor(out, tmp, keep["minus_half"][:], ALU.pow)

            def first_rstd(t, u):
                pool.drain()
                pool.wait_ge(S["mean_var"], t + 1)
                power(rstd1[u][:], mv[u][:, 1:2], ve1[:]).then_inc(S["rstd1"], 1)

            def late(t, u):
                pool.drain()
                pool.wait_ge(S["var1"], t + 1)
                power(st2[u][:, 2:3], st2[u][:, 1:2], ve[:]).then_inc(S["rstd2"], 1)
                pool.wait_ge(S["hidden"], t + 1)
                if not (isinstance(t, int) and t == 0):
                    pool.wait_ge(S["learned"], t)
                pool.tensor_tensor(hw, hid, keep["wu2"][:], ALU.mult).then_inc(S["hw"], 1)
                pool.wait_ge(S["poly"], t + 1)
                pool.tensor_tensor(act1, act1, hid, ALU.mult).then_inc(S["inner"], 1)
                pool.wait_ge(S["learned"], t + 1)
                pool.tensor_copy(keep["stats"][:, bass.ds(t, 1), :].rearrange("p o n -> p (o n)"),
                                 st2[u][:]).then_inc(S["kept_stats"], 1)

            def keep_att(t, u):
                pool.wait_ge(S["att"], t + 1)
                pool.tensor_copy(keep["att"][:, bass.ds(t, 1), :].rearrange("p o n -> p (o n)"),
                                 att2[u][:, 0:NCTX]).then_inc(S["kept_att"], 1)

            pool.memset(keep["minus_half"][:], -0.5)
            pool.memset(keep["eps"][:], EPS).then_inc(S["kept_stats"], 1)
            pool.drain()
            for t in range(2):
                first_rstd(t, t)
            keep_att(0, 0)
            first_rstd(2, 0)
            late(0, 0)
            keep_att(1, 1)
            first_rstd(3, 1)
            with pool.Fori(1, PAIRS - 1) as j:
                for u in range(2):
                    t = 2 * j + u
                    late(t - 1, 1 - u)
                    keep_att(t, u)
                    first_rstd(t + 2, u)
            for t in (TILES - 2, TILES - 1):
                late(t - 1, 1 - t % 2)
                keep_att(t, t % 2)
            late(TILES - 1, 1)
            context_low(pool, keep, keep["ctx_hi"], keep["ctx_lo"], 0)
            pool.wait_ge(keep["wvu_hi"], 1)
            pool.tensor_tensor(keep["wvu_out"][1], f32(keep["wvu_out"][1]), f32(keep["wvu_out"][0]),
                               ALU.subtract).then_inc(keep["wvu_lo"], 1)

        @block.vector
        def _(dve):
            def moments_of(u, j, quarters):
                dve.wait_ge(x_in[u], 16 * j + 16)
                for k in quarters:
                    dve.bn_stats(stats[:, k, :], x[u][:, k * QN:(k + 1) * QN])

            def moments(u):
                dve.drain()
                dve.bn_aggr(mv[u][:], stats[:])
                dve.drain()
                dve.tensor_scalar(nmean[u][:], mv[u][:, 0:1], -1.0, None, ALU.mult).then_inc(S["mean_var"], 1)

            def x_lo(t, u, g):
                dve.wait_ge(S["x_hi"], G * t + g + 1)
                dve.tensor_tensor(xT[u][1][:, 4 * g:4 * g + 4, :], bank[g % 2][:].rearrange("p (k n) -> p k n", k=4),
                                  f32(xT[u][0][:, 4 * g:4 * g + 4, :]), ALU.subtract).then_inc(S["x_lo"], 1)

            def soft_scores(t, u, batch):
                dve.wait_ge(S["rstd1"], t + 1)
                dve.tensor_scalar(nscale[:], rstd1[u][:], -ATT_SCALE, None, ALU.mult)
                dve.tensor_copy(mvk[u][:], mv[u][:])
                dve.drain()
                dve.wait_ge(S["b_sum"], t + 1)
                dve.scalar_tensor_tensor(neg_s, psB[u][:, 0:NCTX], nscale[:, 0:1], at(keep["bq_rows"], batch),
                                         ALU.mult, ALU.subtract)
                dve.drain()
                dve.tensor_reduce(neg_max[:], neg_s, AX.X, ALU.min).then_inc(S["neg_scores"], 1)

            def soft_att(t, u, first):
                dve.wait_ge(S["exp"], t + 1)
                dve.reciprocal(einv[:], esum[:])
                dve.drain()
                if not first:
                    dve.wait_ge(S["kept_att"], t - 1)
                dve.tensor_scalar(att2[u][:, 0:NCTX], e1, einv[:, 0:1], None, ALU.mult)
                dve.tensor_scalar(att2[u][:, NCTX:2 * NCTX], e1, einv[:, 0:1], None,
                                  ALU.mult).then_inc(S["att"], 1)

            def att_lo(t):
                dve.wait_ge(S["att_hi"], t + 1)
                dve.tensor_tensor(attS[NCTX:P, :], att_turned_ps[NCTX:P, :], f32(attS[NCTX:P, :]),
                                  ALU.subtract).then_inc(S["att_lo"], 1)

            def late_stats(t, u, batch, first):
                dve.wait_ge(S["c_sum"], t + 1)
                if not first:
                    dve.wait_ge(S["kept_stats"], t)
                dve.tensor_tensor_reduce(junk, psB[u][:, NCTX:2 * NCTX], att2[u][:, 0:NCTX],
                                         keep["cov_scale"][:, 0:1], mvk[u][:, 1:2],
                                         ALU.mult, ALU.add, st2[u][:, 1:2]).then_inc(S["var1"], 1)
                dve.scalar_tensor_tensor(junk2, att2[u][:, 0:NCTX], 1.0, at(keep["mu_scaled"], batch),
                                         ALU.mult, ALU.mult, accum_out=shift[:])
                dve.drain()
                dve.tensor_tensor(st2[u][:, 0:1], shift[:], mvk[u][:, 0:1], ALU.add)

            def late_scale(t, u):
                dve.wait_ge(S["rstd2"], t + 1)
                dve.tensor_scalar(q2[:, 0:BOT], psB[u][:, QC:QC + BOT], st2[u][:, 2:3], None, ALU.mult)
                dve.tensor_scalar(q2[:, BOT:2 * BOT], psB[u][:, QC:QC + BOT], st2[u][:, 2:3], None,
                                  ALU.mult).then_inc(S["query"], 1)
                dve.scalar_tensor_tensor(hid[:, 0:UA], psB[u][:, QC + BOT:BW], st2[u][:, 2:3], keep["bu1"][:, 0:UA],
                                         ALU.mult, ALU.add)
                dve.scalar_tensor_tensor(hid[:, UA:HU], psA[:, 0:UB], st2[u][:, 2:3], keep["bu1"][:, UA:HU], ALU.mult,
                                         ALU.add).then_inc(S["hidden"], 1)

            def late_q_lo(t):
                dve.wait_ge(S["q_hi"], t + 1)
                dve.tensor_tensor(qS[BOT:P, :], q_turned_ps[BOT:P, :], f32(qS[BOT:P, :]),
                                  ALU.subtract).then_inc(S["q_lo"], 1)

            def late_poly(t):
                dve.wait_ge(S["square"], t + 1)
                dve.tensor_scalar(act1, act1, 0.044715, 1.0, ALU.mult, ALU.add).then_inc(S["poly"], 1)

            def late_slots(t):
                dve.wait_ge(S["routed"], t + 1)
                dve.memset(wmax[:], OUT_OF_RANGE)
                dve.max(top8[:], psR[:])
                dve.drain()
                dve.match_replace(picked, top8[:], psR[:], PICKED)
                dve.drain()
                dve.tensor_scalar(picked, picked, PICKED, OUT_OF_RANGE, ALU.is_lt, ALU.mult)
                dve.drain()
                dve.tensor_tensor_reduce(ws, psS[:], picked, 1.0, -3.0e38, ALU.add, ALU.max, wmax[:])
                dve.drain()
                dve.tensor_scalar(wneg[:], wmax[:], -1.0, None, ALU.mult).then_inc(S["slots"], 1)

            def late_learned(t, u):
                dve.wait_ge(S["tanh"], t + 1)
                dve.wait_ge(S["hw"], t + 1)
                dve.scalar_tensor_tensor(act1, act1, 1.0, hw, ALU.add, ALU.mult,
                                         accum_out=st2[u][:, 3:4]).then_inc(S["learned"], 1)

            def late_z(t):
                dve.wait_ge(S["slot_exp"], t + 1)
                dve.reciprocal(winv[:], wsum[:])
                dve.drain()
                dve.wait_ge(S["z_sum"], t + 1)
                dve.tensor_scalar(keep["z"][:, bass.ds(t, 1), :].rearrange("p o n -> p (o n)"), z_ps,
                                  winv[:, 0:1], None, ALU.mult).then_inc(S["z_out"], 1)

            def gates():
                def op(f, *args, **kw):
                    ins = f(*args, **kw)
                    dve.drain()
                    return ins

                dve.wait_ge(S["kept_stats"], TILES + 1)
                dve.tensor_scalar(half_bu2, keep["bu2"][:], 0.5, None, ALU.mult).then_inc(S["half_bias"], 1)
                op(dve.tensor_scalar, v["ve"], var, EPS, None, ALU.add)
                op(dve.reciprocal, v["ve"], v["ve"])
                op(dve.tensor_tensor, v["ratio"], v["ve"], var, ALU.mult)
                dve.tensor_scalar(v["one_plus"], v["ratio"], 1.0, None, ALU.add).then_inc(S["ready"], 1)
                dve.drain()
                op(dve.tensor_scalar, v["dist"], v["one_plus"], 1.0, None, ALU.subtract)
                op(dve.tensor_scalar, v["flat"], v["dist"], 0.0, None, ALU.is_equal)
                op(dve.tensor_tensor, v["dist"], v["dist"], v["flat"], ALU.add)
                op(dve.reciprocal, v["dist"], v["dist"])
                op(dve.tensor_tensor, v["ratio"], v["ratio"], v["dist"], ALU.mult)
                dve.wait_ge(S["logged"], 1)
                op(dve.tensor_tensor, v["log"], v["log"], v["flat"], ALU.add)
                op(dve.tensor_tensor, v["log"], v["log"], v["ratio"], ALU.mult)
                dve.tensor_reduce(rowsum, v["log"], AX.X, ALU.add).then_inc(S["log_summed"], 1)
                dve.wait_ge(S["all_summed"], 1)
                op(dve.tensor_scalar, total, ps_total[:, 0:1], 1.0 / (TILES * P), 1.0e-6, ALU.mult, ALU.add)
                op(dve.reciprocal, total, total)
                op(dve.tensor_scalar, v["log"], v["log"], total, 0.5, ALU.mult, ALU.mult)
                dve.wait_ge(S["unit"], 1)
                op(dve.tensor_scalar, v["u"], v["th"], 1.25, 1.25, ALU.mult, ALU.add)
                op(dve.tensor_tensor, v["u"], v["u"], v["log"], ALU.add)
                op(dve.tensor_scalar, v["u"], v["u"], 0.0, 5.0, ALU.max, ALU.min)
                op(dve.tensor_scalar, v["u"], v["u"], -TAU_LOW, 1.0 / (TAU_HIGH - TAU_LOW), ALU.add, ALU.mult)
                op(dve.tensor_scalar, v["u"], v["u"], 0.0, 1.0, ALU.max, ALU.min)
                dve.tensor_scalar(v["u"], v["u"], keep["w1"][:, 0:1], keep["gb"][:, 0:1], ALU.mult,
                                  ALU.add).then_inc(S["squashed"], 1)
                dve.wait_ge(S["gated"], 1)
                op(dve.tensor_scalar, v["gate"], v["gate"], 0.5, 0.5, ALU.mult, ALU.add)
                op(dve.tensor_scalar, v["u"], v["gate"], EARLY_EXIT, None, ALU.is_ge)
                op(dve.tensor_tensor, v["gate"], v["gate"], v["u"], ALU.mult)
                op(dve.tensor_scalar, keep["f_z"][:], v["gate"], tgf[:, 0:1], None, ALU.mult)
                op(dve.tensor_scalar, v["u"], rstd, tgf[:, 0:1], None, ALU.mult)
                op(dve.tensor_scalar, keep["f_x"][:], v["u"], 1.0, None, ALU.add)
                op(dve.tensor_tensor, v["u"], v["u"], mean, ALU.mult)
                dve.tensor_scalar(keep["f_0"][:], v["u"], -1.0, None, ALU.mult)
                op(dve.tensor_scalar, keep["f_att"][:], keep["f_x"][:], tgx[:, 0:1], None, ALU.mult)

            def tile(t, u, j, late=True, last=False, ahead=True, first=False, second=False):
                if late:
                    late_stats(t - 1, 1 - u, (j if u else j - 1) // 4, second)
                    late_scale(t - 1, 1 - u)
                    late_q_lo(t - 1)
                    late_poly(t - 1)
                soft_scores(t, u, j // 4)
                soft_att(t, u, first or second)
                if late:
                    late_slots(t - 1)
                if not last:
                    x_lo(t + 1, 1 - u, 0)
                    x_lo(t + 1, 1 - u, 1)
                att_lo(t)
                if late:
                    late_learned(t - 1, 1 - u)
                if ahead:
                    moments_of(u, j + 1, (0, 1))
                if not last:
                    x_lo(t + 1, 1 - u, 2)
                if ahead:
                    moments_of(u, j + 1, (2, 3))
                    moments(u)
                if not last:
                    x_lo(t + 1, 1 - u, 3)
                if late:
                    late_z(t - 1)

            def context_scale(r):
                dve.wait_ge(S["cw_product"], r + 1)
                dve.tensor_scalar(cw[r][:, CWN - UB:CWN], wide_ps[r][:, 0:UB], tgx[:, 0:1], None, ALU.mult)
                dve.tensor_scalar(cw[r][:, NCTX:CWN - UB], gram_ps[r][:, P:P + BOT + UA], tgx[:, 0:1], None,
                                  ALU.mult)
                for k in range(2):
                    own = slice(k * NCTX, (k + 1) * NCTX)
                    ins = dve.tensor_scalar(cw[r][own, 0:NCTX], gram_ps[r][own, own], tgx[own, 0:1], 0.5,
                                            ALU.mult, ALU.mult)
                ins.then_inc(S["cw_scaled"], 1)

            def context_lo(r):
                dve.wait_ge(S["cw_high"], r + 1)
                dve.tensor_tensor(cw_lo[r], cw[r], f32(cw_hi[r]), ALU.subtract).then_inc(S["cw_low"], 1)

            dve.tensor_scalar(keep["cov_scale"][:], keep["tgx"][:], 2.0 / D, None, ALU.mult)
            for t in range(2):
                moments_of(t, 0, range(4))
                moments(t)
            context_scale(0)
            context_lo(0)
            for g in range(G):
                x_lo(0, 0, g)
            context_scale(1)
            context_lo(1)
            tile(0, 0, 0, late=False, first=True)
            tile(1, 1, 0, second=True)
            with dve.Fori(1, PAIRS - 1) as j:
                for u in range(2):
                    tile(2 * j + u, u, j)
            tile(TILES - 2, 0, PAIRS - 1, ahead=False)
            tile(TILES - 1, 1, PAIRS - 1, ahead=False, last=True)
            t, u = TILES - 1, 1
            late_stats(t, u, BATCH - 1, False)
            late_scale(t, u)
            late_q_lo(t)
            late_poly(t)
            late_slots(t)
            late_learned(t, u)
            gates()
            late_z(t)


def output_block(nc, io, keep):
    with ExitStack() as ctx:
        m = Memory(nc, ctx, "ob")
        ident = keep["ident"]
        (ctx1, ctx2), wvu = keep["ctx_out"], keep["wvu_out"]
        RING = OUT_RING
        x = keep["rows"] + [m.sb(f"x{s}", [P, D]) for s in range(FFN_RING, RING)]
        az = [m.sb(f"att_z{u}", [P, 2 * P]) for u in range(2)]
        azT = [keep["Z"][u][:, 0:2 * P] for u in range(2)]
        zl = [keep["Z"][u][:, 2 * P:3 * P] for u in range(2)]
        turn_ps = [m.ps(f"turned{u}") for u in range(2)]
        po = [m.ps(f"out{n}") for n in range(4)]
        x_in = keep["out_x_in"]
        stored = [m.sem(f"stored{s}") for s in range(RING)]
        S = {n: m.sem(n) for n in ("scaled", "turned", "hi", "lo", "affine", "summed", "added")}
        block = ctx.enter_context(nc.Block())
        xout = io["out"].rearrange("(t p) d -> t p d", p=P)
        FULL, REST = TILES // RING, TILES % RING

        @block.sync
        def _(sp):
            for s in range(2, RING):
                load_x(sp, io, x, x_in, s, s)

            def body(j, count):
                for s in range(count):
                    sp.wait_ge(stored[s], 16 * j)
                    load_x(sp, io, x, x_in, RING * j + s, s)

            with sp.Fori(1, FULL) as j:
                body(j, RING)
            body(FULL, REST)

        @block.gpsimd
        def _(pool):
            for b in range(1, BATCH):
                context_low(pool, keep, keep["ctx_hi"], keep["ctx_lo"], b)

        @block.tensor
        def _(pe):
            def turn(t, u):
                pe.wait_ge(S["scaled"], t + 1)
                pe.transpose(turn_ps[u][:, 0:P], az[u][:, 0:P], ident[:])
                pe.transpose(turn_ps[u][:, P:2 * P], az[u][:, P:2 * P], ident[:]).then_inc(S["turned"], 1)

            def chunk(t, u, n, b, first):
                if not first:
                    pe.wait_ge(S["added"], 4 * t + n - 3)
                cols = slice(n * QN, (n + 1) * QN)
                c1 = ctx1[:, bass.ds(b, 1), cols].rearrange("p o n -> p (o n)")
                c2 = ctx2[0:NCTX, bass.ds(b, 1), cols].rearrange("p o n -> p (o n)")
                pe.matmul(po[n][:], azT[u][:, 0:P], c1, start=True, stop=False)
                pe.matmul(po[n][:], azT[u][0:NCTX, 0:P], c2, start=False, stop=False)
                split_product(pe, po[n][:], (azT[u][:, P:2 * P], zl[u]), (wvu[0][:, cols], wvu[1][:, cols]),
                              False, True).then_inc(S["summed"], 1)

            def body(j, count=RING, first=False, last=False):
                for s in range(count):
                    t, u = RING * j + s, s % 2
                    pe.wait_ge(S["lo"], t + 1)
                    for n in range(4):
                        chunk(t, u, n, t // 8, first and s == 0)
                        if n == 1 and not (last and s == count - 1):
                            turn(t + 1, 1 - u)

            pe.wait_ge(keep["wvu_lo"], 1)
            pe.wait_ge(keep["ctx_lo"], 1)
            turn(0, 0)
            body(0, first=True)
            pe.wait_ge(keep["ctx_lo"], BATCH)
            with pe.Fori(1, FULL) as j:
                body(j)
            body(FULL, REST, last=True)

        @block.scalar
        def _(act):
            def hi(t, u):
                act.wait_ge(S["turned"], t + 1)
                act.activation(azT[u], turn_ps[u][:, 0:2 * P], ACT.Copy).then_inc(S["hi"], 1)

            def affine(t, s, j):
                act.wait_ge(x_in[s], 16 * j + 16)
                act.activation(x[s][:], x[s][:], ACT.Identity, bias=keep["f_0"][:, bass.ds(t, 1)],
                               scale=keep["f_x"][:, bass.ds(t, 1)]).then_inc(S["affine"], 1)

            def store(t, s):
                act.wait_ge(S["added"], 4 * t + 4)
                act.dma_start(xout[bass.ds(t, 1)].rearrange("o p d -> p (o d)"), x[s][:]).then_inc(stored[s], 16)

            def body(j, count=RING, first=False, last=False):
                for s in range(count):
                    t = RING * j + s
                    if not (last and s == count - 1):
                        hi(t + 1, 1 - s % 2)
                        affine(t + 1, (s + 1) % RING, j + (s + 1) // RING)
                    store(t, s)
                    if first and s < 2:
                        context_high(act, keep, keep["ctx_hi"], s + 2)

            hi(0, 0)
            affine(0, 0, 0)
            context_high(act, keep, keep["ctx_hi"], 1)
            body(0, first=True)
            with act.Fori(1, FULL) as j:
                body(j)
            body(FULL, REST, last=True)
            for s in range(RING):
                act.wait_ge(stored[s], 16 * (FULL + (s < REST)))

        @block.vector
        def _(dve):
            def scale(t, u):
                f_att, f_z = keep["f_att"][:, bass.ds(t, 1)], keep["f_z"][:, bass.ds(t, 1)]
                for half in range(2):
                    dve.tensor_scalar(az[u][:, half * NCTX:(half + 1) * NCTX], at(keep["att"], t), f_att, None,
                                      ALU.mult)
                dve.tensor_scalar(az[u][:, P:2 * P], at(keep["z"], t), f_z, None, ALU.mult).then_inc(S["scaled"], 1)

            def lo(t, u):
                dve.wait_ge(S["hi"], t + 1)
                dve.tensor_tensor(azT[u][NCTX:P, 0:P], turn_ps[u][NCTX:P, 0:P], f32(azT[u][NCTX:P, 0:P]),
                                  ALU.subtract)
                dve.tensor_tensor(zl[u], turn_ps[u][:, P:2 * P], f32(azT[u][:, P:2 * P]),
                                  ALU.subtract).then_inc(S["lo"], 1)

            def add(t, s, n):
                dve.wait_ge(S["summed"], 4 * t + n + 1)
                if n == 0:
                    dve.wait_ge(S["affine"], t + 1)
                cols = slice(n * QN, (n + 1) * QN)
                dve.tensor_tensor(x[s][:, cols], x[s][:, cols], po[n][:], ALU.add).then_inc(S["added"], 1)

            def body(j, count=RING, last=False):
                for s in range(count):
                    t, ahead = RING * j + s, not (last and s == count - 1)
                    if ahead:
                        scale(t + 1, 1 - s % 2)
                    add(t, s, 0)
                    add(t, s, 1)
                    if ahead:
                        lo(t + 1, 1 - s % 2)
                    add(t, s, 2)
                    add(t, s, 3)

            scale(0, 0)
            lo(0, 0)
            body(0)
            with dve.Fori(1, FULL) as j:
                body(j)
            body(FULL, REST, last=True)


def gated_cross_attention_and_memory(nc, io):
    scr = {
        "mt": nc.dram_tensor("scratch_mt", [2, P, KC, CR], F32).ap(),
        "cent": nc.dram_tensor("scratch_centred", [2, P, KC, CR], F32).ap(),
        "b": nc.dram_tensor("scratch_b", [2, P, KC, BATCH, 2, NCTX], F32).ap(),
        "cw": nc.dram_tensor("scratch_cw", [2, CR, CWN], F32).ap(),
        "ctx": nc.dram_tensor("scratch_ctx", [CR, D], F32).ap(),
        "wvu": nc.dram_tensor("scratch_wvu", [P, D], F32).ap(),
    }
    with ExitStack() as outer:
        m = Memory(nc, outer, "k")
        keep = {
            "ident": m.sb("ident", [P, P]), "ones": m.sb("ones", [P, P]),
            "mu_all": m.sb("mu_all", [P, CR]), "mu_scaled": m.sb("mu_scaled", [P, BATCH, NCTX]),
            "bq_rows": m.sb("bq_rows", [P, BATCH, NCTX]), "bias_cols": m.sb("bias_cols", [P, 2 * KC]),
            "stats": m.sb("stats", [P, TILES, 4]),
            "att": m.sb("att", [P, TILES, NCTX]), "z": m.sb("z", [P, TILES, VB]),
            "rows": [m.sb(f"rows{u}", [P, D]) for u in range(FFN_RING)],
            "Z": [m.sb(f"turned{i}", [P, KC * CR], F32R) for i in range(2)],
        }
        way_out = m.sb("way_out", [P, 2 * CWN], F32R)
        keep["mt"] = [[way_out[:, (2 * u + i) * CR:(2 * u + i + 1) * CR] for i in range(2)] for u in range(2)]
        keep["cw_hi"] = [way_out[:, r * CWN:(r + 1) * CWN] for r in range(2)]
        keep["ctxT"] = [z[:].rearrange("p (c n) -> p c n", n=CR) for z in keep["Z"]]
        for n in ("tgx", "tgf", "w1", "gb", "bu2", "minus_half", "eps", "cov_scale"):
            keep[n] = m.sb(n, [P, 1])
        for n in ("f_x", "f_0", "f_att", "f_z"):
            keep[n] = m.sb(n, [P, TILES])
        for n in ("ctx_hi", "ctx_lo", "ctx_stored", "cent_out", "b_in", "wvu_in", "wvu_hi", "wvu_lo"):
            keep[n] = m.sem(n)
        for n, count in (("wq_in", 2), ("ffn_in", FFN_RING), ("x_in", 2), ("mt_out", 2), ("ctx_in", BATCH),
                         ("out_x_in", OUT_RING)):
            keep[n] = [m.sem(f"{n}{i}") for i in range(count)]
        with ExitStack() as first:
            m = Memory(nc, first, "a")
            keep["KT"] = [m.sb(f"KT{i}", [P, KC, CR], F32R) for i in range(2)]
            keep["T"] = [[m.sb(f"T{u}{i}", [P, KC, P], F32R) for i in range(2)] for u in range(2)]
            keys_block(nc, io, scr, keep)
            score_weights_block(nc, io, scr, keep)
        with ExitStack() as second:
            m = Memory(nc, second, "b")
            W = keep["weights"] = [m.sb(f"weights{i}", [P, KC * (BW + UB)], F32R) for i in range(2)]
            keep["bw"] = [w[:, 0:KC * BW].rearrange("p (c n) -> p c n", n=BW) for w in W]
            keep["wu"] = [w[:, KC * BW:KC * (BW + UB)].rearrange("p (c n) -> p c n", n=UB) for w in W]
            keep["ctx_out"] = [w[:, 0:BATCH * D].rearrange("p (b d) -> p b d", d=D) for w in W]
            keep["wvu_out"] = [w[:, BATCH * D:(BATCH + 1) * D] for w in W]
            with ExitStack() as third:
                m = Memory(nc, third, "c")
                keep["rs1"] = m.sb("slots_hi", [P, 2 * NSLOT], F32R)
                keep["rs2"] = m.sb("slots_lo", [BOT + 2, 2 * NSLOT], F32R)
                keep["q2s"] = m.sb("query_ones", [BOT + 2, P], F32R)
                keep["av"] = m.sb("av", [P, 4, VB])
                keep["bu1"], keep["wu2"] = m.sb("bu1", [P, HU]), m.sb("wu2", [P, HU])
                ffn_block(nc, io, scr, keep)
                token_block(nc, io, scr, keep)
            output_block(nc, io, keep)


_INS = {"x": "x", "ctx_4096": "ctx", "g_xattn": "g_xattn", "g_ffn": "g_ffn", "L0_xattn_Wq": "Wq",
        "L0_xattn_bq": "bq", "L0_xattn_Wk": "Wk", "L0_xattn_bk": "bk", "L0_ffn_Wq": "fWq", "L0_ffn_Wr": "Wr",
        "L0_ffn_aux_keys": "aux_keys", "L0_ffn_aux_values": "aux_values", "L0_ffn_Wvd": "Wvd",
        "L0_ffn_Wvu": "Wvu", "L0_ffn_Wu1": "Wu1", "L0_ffn_bu1": "bu1", "L0_ffn_Wu2": "wu2",
        "L0_ffn_bu2": "bu2", "L0_ffn_gate_w1": "gate_w1", "L0_ffn_gate_bias": "gate_bias",
        "L0_ffn_log_rel": "log_rel"}
_SHAPES = {"x": (BATCH * SEQ, D), "ctx": (CR, D), "g_xattn": (1, 1), "g_ffn": (1, 1), "bu2": (1, 1),
           "gate_w1": (1, 1), "gate_bias": (1, 1), "wu2": (HU,)}


def kernel(**inputs):
    import numpy as _np
    import concourse.bacc as _bacc
    from concourse import mybir as _mybir
    from concourse.bass_utils import run_bass_kernel_spmd as _run

    nc = _bacc.Bacc("TRN2", target_bir_lowering=False, num_devices=1)
    arrays, io = {}, {}
    for name, short in _INS.items():
        a = _np.ascontiguousarray(inputs[name])
        if short in _SHAPES:
            a = a.reshape(_SHAPES[short])
        arrays[f"in_{short}_dram"] = a
        io[short] = nc.dram_tensor(f"in_{short}_dram", a.shape, _mybir.dt.from_np(a.dtype), kind="ExternalInput").ap()
    io["out"] = nc.dram_tensor("out_0_dram", (BATCH * SEQ, D), F32, kind="ExternalOutput").ap()
    gated_cross_attention_and_memory(nc, io)
    r = _run(nc, [arrays], core_ids=[0])
    return r.results[0]["out_0_dram"].reshape(BATCH, SEQ, D)
```
